# Optimizing a Trainium2 kernel written in Bass

```python
import numpy as np
import jax
import jax.numpy as jnp

def _softmax(x, axis=-1):
    return jax.nn.softmax(x, axis=axis)

def _gelu(x):
    return jax.nn.gelu(x, approximate=True)

def _silu(x):
    return jax.nn.silu(x)

def _sigmoid(x):
    return jax.nn.sigmoid(x)

def _layernorm(x, axis=-1, eps=1e-05):
    m = jnp.mean(x, axis=axis, keepdims=True)
    v = jnp.var(x, axis=axis, keepdims=True)
    return (x - m) / jnp.sqrt(v + eps)

def _scatter_add(tgt, idx, src, axis=0):
    return tgt.at[idx].add(src)

def _segment_sum(src, seg, n):
    return jax.ops.segment_sum(src, seg, n)
kernel_name = 'mk_decoder_postln_d2_seqx_r8_703b01'

def setup_inputs(seed: int=0):
    np.random.seed(seed)
    _w = jnp.asarray

    def _rec_inputs():
        import jax
        import jax.numpy as jnp
        _rk = jax.random.key(seed)
        x = -0.0002928 + 1 * jax.random.normal(jax.random.fold_in(_rk, 1), (4, 256, 128), jnp.float32)
        _lenS = 256 - jax.random.randint(jax.random.fold_in(_rk, 7), (4,), 0, max(1, 256 // 4) + 1, jnp.int32)
        _lenS2 = 256 - jax.random.randint(jax.random.fold_in(_rk, 8), (4,), 0, max(1, 256 // 4) + 1, jnp.int32)
        _ctx_1024P = jax.random.normal(jax.random.fold_in(_rk, 11), (4, 16, 128), jnp.float32)
        _ctx_1024c = jax.random.dirichlet(jax.random.fold_in(_rk, 511), 0.3 * jnp.ones((16,), jnp.float32), (4, 256))
        _ctx_1024t = jnp.einsum('bsk,bkd->bsd', _ctx_1024c, _ctx_1024P)
        _ctx_1024t = _ctx_1024t * jax.lax.rsqrt(jnp.mean(jnp.square(_ctx_1024t)) + 1e-12) * 0.953939
        ctx_1024 = -1.39393e-06 + 0.999914 * (_ctx_1024t + 0.3 * jax.random.normal(jax.random.fold_in(_rk, 611), (4, 256, 128), jnp.float32))
        return (x, ctx_1024)
    x, ctx_1024 = _rec_inputs()

    def _L0_attn_setup():
        import jax, jax.numpy as jnp
        import numpy as np
        D_MODEL = 128
        NUM_HEADS = 16
        D_K = D_MODEL // NUM_HEADS
        ROPE_BASE = 10000.0

        def _rotate_half(x):
            x1 = x[..., ::2]
            x2 = x[..., 1::2]
            return jnp.stack((-x2, x1), axis=-1).reshape(x.shape)

        def _rope(q, k):
            seq_len = q.shape[-2]
            freqs = ROPE_BASE ** (jnp.arange(0, D_K, 2, dtype=q.dtype) / D_K)
            angles = jnp.arange(seq_len, dtype=q.dtype)[:, None] / freqs[None, :]
            sin = jnp.repeat(jnp.sin(angles), 2, axis=-1)[None, None]
            cos = jnp.repeat(jnp.cos(angles), 2, axis=-1)[None, None]
            return (q * cos + _rotate_half(q) * sin, k * cos + _rotate_half(k) * sin)
        key = jax.random.key(seed)
        ks = jax.random.split(key, 9)
        B, S, D = (2, 256, D_MODEL)
        s = 1.0 / np.sqrt(D)
        inp = {'x': jax.random.normal(ks[0], (B, S, D), dtype=jnp.float32), 'wq': jax.random.uniform(ks[1], (D, D), jnp.float32, -s, s), 'bq': jax.random.uniform(ks[2], (D,), jnp.float32, -s, s), 'wk': jax.random.uniform(ks[3], (D, D), jnp.float32, -s, s), 'bk': jax.random.uniform(ks[4], (D,), jnp.float32, -s, s), 'wv': jax.random.uniform(ks[5], (D, D), jnp.float32, -s, s), 'bv': jax.random.uniform(ks[6], (D,), jnp.float32, -s, s), 'wo': jax.random.uniform(ks[7], (D, D), jnp.float32, -s, s), 'bo': jax.random.uniform(ks[8], (D,), jnp.float32, -s, s)}
        return inp
    _L0_attn_all = _L0_attn_setup()
    _L0_attn_in = {k: v for k, v in _L0_attn_all.items() if k in ('wq', 'bq', 'wk', 'bk', 'wv', 'bv', 'wo', 'bo')}
    del _L0_attn_all

    def _L0_xattn_setup():
        import jax, jax.numpy as jnp
        import numpy as np
        D_MODEL = 128
        NUM_HEADS = 16
        HEAD_DIM = D_MODEL // NUM_HEADS
        key = jax.random.key(seed)
        ks = jax.random.split(key, 11)
        B, S = (2, 256)
        s = 0.02
        return {'query': jax.random.normal(ks[0], (B, S, D_MODEL), jnp.float32), 'key': jax.random.normal(ks[1], (B, S, D_MODEL), jnp.float32), 'value': jax.random.normal(ks[2], (B, S, D_MODEL), jnp.float32), 'Wq': jax.random.normal(ks[3], (D_MODEL, D_MODEL), jnp.float32) * s, 'bq': jnp.zeros((D_MODEL,), jnp.float32), 'Wk': jax.random.normal(ks[4], (D_MODEL, D_MODEL), jnp.float32) * s, 'bk': jnp.zeros((D_MODEL,), jnp.float32), 'Wv': jax.random.normal(ks[5], (D_MODEL, D_MODEL), jnp.float32) * s, 'bv': jnp.zeros((D_MODEL,), jnp.float32), 'Wo': jax.random.normal(ks[6], (D_MODEL, D_MODEL), jnp.float32) * s, 'bo': jnp.zeros((D_MODEL,), jnp.float32)}
    _L0_xattn_all = _L0_xattn_setup()
    _L0_xattn_in = {k: v for k, v in _L0_xattn_all.items() if k in ('Wq', 'bq', 'Wk', 'bk', 'Wv', 'bv', 'Wo', 'bo')}
    del _L0_xattn_all

    def _L0_ffn_setup():
        import jax, jax.numpy as jnp
        import numpy as np
        B, S, D, E, K = (2, 256, 128, 8, 2)
        H = 4 * D
        key = jax.random.key(seed)
        ks = jax.random.split(key, 6)
        x = jax.random.normal(ks[0], (B, S, D), dtype=jnp.float32)
        lim_g = np.sqrt(6.0 / (D + E)).astype(np.float32)
        W_gate = jax.random.uniform(ks[1], (D, E), minval=-lim_g, maxval=lim_g, dtype=jnp.float32)
        lim1 = np.sqrt(1.0 / D).astype(np.float32)
        lim2 = np.sqrt(1.0 / H).astype(np.float32)
        W1 = jax.random.uniform(ks[2], (E, D, H), minval=-lim1, maxval=lim1, dtype=jnp.float32)
        b1 = jax.random.uniform(ks[3], (E, H), minval=-lim1, maxval=lim1, dtype=jnp.float32)
        W2 = jax.random.uniform(ks[4], (E, H, D), minval=-lim2, maxval=lim2, dtype=jnp.float32)
        b2 = jax.random.uniform(ks[5], (E, D), minval=-lim2, maxval=lim2, dtype=jnp.float32)
        return {'x': x, 'W_gate': W_gate, 'W1': W1, 'b1': b1, 'W2': W2, 'b2': b2}
    _L0_ffn_all = _L0_ffn_setup()
    _L0_ffn_in = {k: v for k, v in _L0_ffn_all.items() if k in ('W_gate', 'W1', 'b1', 'W2', 'b2')}
    del _L0_ffn_all

    def _L1_attn_setup():
        import jax, jax.numpy as jnp
        import numpy as np
        D_MODEL = 128
        SCALE = float(np.sqrt(D_MODEL))
        key = jax.random.key(seed)
        k1, k2, k3 = jax.random.split(key, 3)
        input_data = jax.random.normal(k1, (4, 256, D_MODEL), dtype=jnp.float32)
        qk = jax.random.normal(k2, (D_MODEL, D_MODEL), dtype=jnp.float32) / SCALE
        ov = jax.random.normal(k3, (D_MODEL, D_MODEL), dtype=jnp.float32) / SCALE
        return {'input_data': input_data, 'qk': qk, 'ov': ov}
    _L1_attn_all = _L1_attn_setup()
    _L1_attn_in = {k: v for k, v in _L1_attn_all.items() if k in ('qk', 'ov')}
    del _L1_attn_all

    def _L1_xattn_setup():
        import jax, jax.numpy as jnp
        import numpy as np
        DIM = 128
        NUM_HEADS = 16
        HEAD_DIM = DIM // NUM_HEADS
        SCALE = HEAD_DIM ** (-0.5)
        key = jax.random.key(seed)
        ks = jax.random.split(key, 8)
        B, Nx, Nc = (2, 256, 256)
        s = DIM ** (-0.5)
        return {'x': jax.random.normal(ks[0], (B, Nx, DIM), jnp.float32), 'context': jax.random.normal(ks[1], (B, Nc, DIM), jnp.float32), 'Wq': jax.random.normal(ks[2], (DIM, DIM), jnp.float32) * s, 'Wk': jax.random.normal(ks[3], (DIM, DIM), jnp.float32) * s, 'Wv': jax.random.normal(ks[4], (DIM, DIM), jnp.float32) * s, 'Wo': jax.random.normal(ks[5], (DIM, DIM), jnp.float32) * s, 'bo': jnp.zeros((DIM,), jnp.float32)}
    _L1_xattn_all = _L1_xattn_setup()
    _L1_xattn_in = {k: v for k, v in _L1_xattn_all.items() if k in ('Wq', 'Wk', 'Wv', 'Wo', 'bo')}
    del _L1_xattn_all

    def _L1_ffn_setup():
        import math
        import jax, jax.numpy as jnp
        import numpy as np
        B, S, D, F, E = (8, 256, 128, 512, 8)
        CAPACITY_FACTOR = 1.0
        key = jax.random.key(seed)
        k1, k2, k3, k4 = jax.random.split(key, 4)
        x = jax.random.normal(k1, (B, S, D), dtype=jnp.float32)
        Wr = jax.random.normal(k2, (D, E), dtype=jnp.float32) * (1.0 / math.sqrt(D))
        W1 = jax.random.normal(k3, (E, D, F), dtype=jnp.float32) * (1.0 / math.sqrt(D))
        W2 = jax.random.normal(k4, (E, F, D), dtype=jnp.float32) * (1.0 / math.sqrt(F))
        return {'x': x, 'Wr': Wr, 'W1': W1, 'W2': W2}
    _L1_ffn_all = _L1_ffn_setup()
    _L1_ffn_in = {k: v for k, v in _L1_ffn_all.items() if k in ('Wr', 'W1', 'W2')}
    del _L1_ffn_all
    return {'x': x, 'ctx_1024': ctx_1024, 'L0_attn_wq': _L0_attn_in['wq'], 'L0_attn_bq': _L0_attn_in['bq'], 'L0_attn_wk': _L0_attn_in['wk'], 'L0_attn_bk': _L0_attn_in['bk'], 'L0_attn_wv': _L0_attn_in['wv'], 'L0_attn_bv': _L0_attn_in['bv'], 'L0_attn_wo': _L0_attn_in['wo'], 'L0_attn_bo': _L0_attn_in['bo'], 'L0_xattn_Wq': _L0_xattn_in['Wq'], 'L0_xattn_bq': _L0_xattn_in['bq'], 'L0_xattn_Wk': _L0_xattn_in['Wk'], 'L0_xattn_bk': _L0_xattn_in['bk'], 'L0_xattn_Wv': _L0_xattn_in['Wv'], 'L0_xattn_bv': _L0_xattn_in['bv'], 'L0_xattn_Wo': _L0_xattn_in['Wo'], 'L0_xattn_bo': _L0_xattn_in['bo'], 'L0_ffn_W_gate': _L0_ffn_in['W_gate'], 'L0_ffn_W1': _L0_ffn_in['W1'], 'L0_ffn_b1': _L0_ffn_in['b1'], 'L0_ffn_W2': _L0_ffn_in['W2'], 'L0_ffn_b2': _L0_ffn_in['b2'], 'L1_attn_qk': _L1_attn_in['qk'], 'L1_attn_ov': _L1_attn_in['ov'], 'L1_xattn_Wq': _L1_xattn_in['Wq'], 'L1_xattn_Wk': _L1_xattn_in['Wk'], 'L1_xattn_Wv': _L1_xattn_in['Wv'], 'L1_xattn_Wo': _L1_xattn_in['Wo'], 'L1_xattn_bo': _L1_xattn_in['bo'], 'L1_ffn_Wr': _L1_ffn_in['Wr'], 'L1_ffn_W1': _L1_ffn_in['W1'], 'L1_ffn_W2': _L1_ffn_in['W2']}

def reference(x, ctx_1024, L0_attn_wq, L0_attn_bq, L0_attn_wk, L0_attn_bk, L0_attn_wv, L0_attn_bv, L0_attn_wo, L0_attn_bo, L0_xattn_Wq, L0_xattn_bq, L0_xattn_Wk, L0_xattn_bk, L0_xattn_Wv, L0_xattn_bv, L0_xattn_Wo, L0_xattn_bo, L0_ffn_W_gate, L0_ffn_W1, L0_ffn_b1, L0_ffn_W2, L0_ffn_b2, L1_attn_qk, L1_attn_ov, L1_xattn_Wq, L1_xattn_Wk, L1_xattn_Wv, L1_xattn_Wo, L1_xattn_bo, L1_ffn_Wr, L1_ffn_W1, L1_ffn_W2):
    import jax
    import jax.numpy as jnp

    def _L0_attn_ref(x, wq, bq, wk, bk, wv, bv, wo, bo):
        import jax, jax.numpy as jnp
        import numpy as np
        D_MODEL = 128
        NUM_HEADS = 16
        D_K = D_MODEL // NUM_HEADS
        ROPE_BASE = 10000.0

        def _rotate_half(x):
            x1 = x[..., ::2]
            x2 = x[..., 1::2]
            return jnp.stack((-x2, x1), axis=-1).reshape(x.shape)

        def _rope(q, k):
            seq_len = q.shape[-2]
            freqs = ROPE_BASE ** (jnp.arange(0, D_K, 2, dtype=q.dtype) / D_K)
            angles = jnp.arange(seq_len, dtype=q.dtype)[:, None] / freqs[None, :]
            sin = jnp.repeat(jnp.sin(angles), 2, axis=-1)[None, None]
            cos = jnp.repeat(jnp.cos(angles), 2, axis=-1)[None, None]
            return (q * cos + _rotate_half(q) * sin, k * cos + _rotate_half(k) * sin)
        B, S, D = x.shape
        H, dk = (NUM_HEADS, D_K)
        Q = (x @ wq.T + bq).reshape(B, S, H, dk).transpose(0, 2, 1, 3)
        K = (x @ wk.T + bk).reshape(B, S, H, dk).transpose(0, 2, 1, 3)
        V = (x @ wv.T + bv).reshape(B, S, H, dk).transpose(0, 2, 1, 3)
        Q, K = _rope(Q, K)
        score = jnp.einsum('bhqd,bhkd->bhqk', Q, K) / jnp.sqrt(jnp.asarray(dk, x.dtype))
        attn_w = jax.nn.softmax(score, axis=-1)
        out = jnp.einsum('bhqk,bhkd->bhqd', attn_w, V)
        out = out.transpose(0, 2, 1, 3).reshape(B, S, D)
        return out @ wo.T + bo

    def _L0_xattn_ref(query, key, value, Wq, bq, Wk, bk, Wv, bv, Wo, bo):
        import jax, jax.numpy as jnp
        import numpy as np
        D_MODEL = 128
        NUM_HEADS = 16
        HEAD_DIM = D_MODEL // NUM_HEADS
        B, S, _ = query.shape
        scale = HEAD_DIM ** 0.5
        Q = query @ Wq.T + bq
        K = key @ Wk.T + bk
        V = value @ Wv.T + bv
        Q = Q.reshape(B, S, NUM_HEADS, HEAD_DIM).transpose(0, 2, 1, 3)
        K = K.reshape(B, -1, NUM_HEADS, HEAD_DIM).transpose(0, 2, 1, 3)
        V = V.reshape(B, -1, NUM_HEADS, HEAD_DIM).transpose(0, 2, 1, 3)
        scores = jnp.einsum('bhqd,bhkd->bhqk', Q, K) / scale
        attn = jax.nn.softmax(scores, axis=-1)
        ctx = jnp.einsum('bhqk,bhkd->bhqd', attn, V)
        ctx = ctx.transpose(0, 2, 1, 3).reshape(B, S, D_MODEL)
        return ctx @ Wo.T + bo

    def _L0_ffn_ref(x, W_gate, W1, b1, W2, b2):
        import jax, jax.numpy as jnp
        import numpy as np
        B, S, D, E, K = (2, 256, 128, 8, 2)
        H = 4 * D
        gate = jnp.einsum('bsd,de->bse', x, W_gate)
        kth = jax.lax.top_k(gate, K)[0][..., -1:]
        mask = jax.nn.softmax(jnp.where(gate >= kth, gate, -jnp.inf), axis=-1)
        h = jax.nn.relu(jnp.einsum('bsd,edh->bseh', x, W1) + b1)
        y = jnp.einsum('bseh,ehd->bsed', h, W2) + b2
        return (y * mask[..., None]).mean(axis=-2)

    def _L1_attn_ref(input_data, qk, ov):
        import jax, jax.numpy as jnp
        import numpy as np
        D_MODEL = 128
        SCALE = float(np.sqrt(D_MODEL))
        S = input_data.shape[1]
        scores = jnp.einsum('bsd,de,bte->bst', input_data, qk, input_data) / SCALE
        causal = jnp.tril(jnp.ones((S, S), dtype=bool))
        scores = jnp.where(causal, scores, -jnp.inf)
        attn = jax.nn.softmax(scores, axis=-1)
        return jnp.einsum('bst,btd,de->bse', attn, input_data, ov)

    def _L1_xattn_ref(x, context, Wq, Wk, Wv, Wo, bo):
        import jax, jax.numpy as jnp
        import numpy as np
        DIM = 128
        NUM_HEADS = 16
        HEAD_DIM = DIM // NUM_HEADS
        SCALE = HEAD_DIM ** (-0.5)
        B, Nx, C = x.shape
        Nc = context.shape[1]
        H, D = (NUM_HEADS, HEAD_DIM)
        q = (x @ Wq.T).reshape(B, Nx, H, D).transpose(0, 2, 1, 3)
        k = (context @ Wk.T).reshape(B, Nc, H, D).transpose(0, 2, 1, 3)
        v = (context @ Wv.T).reshape(B, Nc, H, D).transpose(0, 2, 1, 3)
        attn = jnp.einsum('bhqd,bhkd->bhqk', q, k) * SCALE
        attn = jax.nn.softmax(attn, axis=-1)
        out = jnp.einsum('bhqk,bhkd->bhqd', attn, v)
        out = out.transpose(0, 2, 1, 3).reshape(B, Nx, C)
        return out @ Wo.T + bo

    def _L1_ffn_ref(x, Wr, W1, W2):
        import math
        import jax, jax.numpy as jnp
        import numpy as np
        B, S, D, F, E = (8, 256, 128, 512, 8)
        CAPACITY_FACTOR = 1.0
        b, s, d = x.shape
        t = b * s
        cap = max(math.ceil(t * CAPACITY_FACTOR / E), 1)
        xf = x.reshape(t, d)
        probs = jax.nn.softmax(xf.astype(jnp.float32) @ Wr, axis=-1)
        eidx = jnp.argmax(probs, axis=-1)
        p_tok = jnp.take_along_axis(probs, eidx[:, None], axis=1)[:, 0]
        onehot = jax.nn.one_hot(eidx, E, dtype=jnp.int32)
        rank_all = jnp.cumsum(onehot, axis=0) - onehot
        rank = jnp.take_along_axis(rank_all, eidx[:, None], axis=1)[:, 0]
        keep = rank < cap
        slot = jnp.where(keep, rank, cap)
        dispatch = jnp.zeros((E, cap + 1), dtype=jnp.int32).at[eidx, slot].set(jnp.arange(t, dtype=jnp.int32))
        valid = jnp.zeros((E, cap + 1), dtype=bool).at[eidx, slot].set(keep)
        dispatch = dispatch[:, :cap]
        valid = valid[:, :cap]
        xe = xf[dispatch]
        h = jnp.maximum(jnp.einsum('ecd,edf->ecf', xe, W1), 0.0)
        ye = jnp.einsum('ecf,efd->ecd', h, W2)
        pe = p_tok[dispatch]
        ye = ye * (pe * valid.astype(ye.dtype))[:, :, None]
        y = jnp.zeros((t, d), dtype=x.dtype).at[dispatch.reshape(-1)].add(ye.reshape(E * cap, d).astype(x.dtype))
        return y.reshape(b, s, d)
    x = _layernorm(x + _L0_attn_ref(x, L0_attn_wq, L0_attn_bq, L0_attn_wk, L0_attn_bk, L0_attn_wv, L0_attn_bv, L0_attn_wo, L0_attn_bo), axis=-1)
    x = _layernorm(x + _L0_xattn_ref(x, ctx_1024, ctx_1024, L0_xattn_Wq, L0_xattn_bq, L0_xattn_Wk, L0_xattn_bk, L0_xattn_Wv, L0_xattn_bv, L0_xattn_Wo, L0_xattn_bo), axis=-1)
    x = _layernorm(x + _L0_ffn_ref(x, L0_ffn_W_gate, L0_ffn_W1, L0_ffn_b1, L0_ffn_W2, L0_ffn_b2), axis=-1)
    x = _layernorm(x + _L1_attn_ref(x, L1_attn_qk, L1_attn_ov), axis=-1)
    x = _layernorm(x + _L1_xattn_ref(x, ctx_1024, L1_xattn_Wq, L1_xattn_Wk, L1_xattn_Wv, L1_xattn_Wo, L1_xattn_bo), axis=-1)
    x = _layernorm(x + _L1_ffn_ref(x, L1_ffn_Wr, L1_ffn_W1, L1_ffn_W2), axis=-1)
    return x

_drawn_inputs = setup_inputs


def setup_inputs(seed=0):
    import zlib

    import numpy as np

    out = dict(_drawn_inputs(seed))
    spreads = {'L0_xattn_bq': (0.0, 0.8),
     'L0_xattn_bk': (0.0, 0.8),
     'L0_xattn_bv': (0.0, 0.1),
     'L0_xattn_bo': (0.0, 0.1),
     'L1_xattn_bo': (0.0, 0.1)}
    factors = {'L0_attn_bq': 4.434,
     'L0_attn_wk': 2.768,
     'L0_attn_bk': 7.302,
     'L0_xattn_Wq': 7.322,
     'L0_xattn_Wk': 8.0,
     'L0_ffn_b1': 5.284,
     'L0_ffn_b2': 3.184}
    for name, (base, spread) in spreads.items():
        noise = np.random.default_rng([zlib.crc32(name.encode()), seed]).standard_normal(out[name].shape)
        drawn = base * np.exp(spread * noise) if base else spread * noise
        out[name] = jnp.asarray(drawn.astype(out[name].dtype))
    for name, factor in factors.items():
        out[name] = (out[name] * factor).astype(out[name].dtype)
    return out
```

```python
import numpy as np
import concourse.bass as bass
from concourse import mybir
from contextlib import ExitStack

P = 128
BATCH, SEQ = 4, 256
TOKENS = BATCH * SEQ
TILES = TOKENS // P
QT = SEQ // P
HEADS, HD = 16, 8
GROUPS = HEADS // 4
EXPERTS, HID = 8, 512
FC = HID // P
CAP = TOKENS // EXPERTS
LANES = 2
EPS = 1e-5
ESLOTS = 6
MASKED = -3.0e38

C_ID, C_TRI, C_ONES, C_MASK, C_COS, C_SIN = 0, 128, 256, 384, 768, 1024
C_KONE, C_EPS, C_FIRST, C_BASE, C_END = 1280, 1281, 1282, 1346, 1410
QHI, QLO, KHI, KLO = range(4)
W_NAMES = ["q0", "q0s", "k0", "k0s", "v0", "o0", "qx0", "kx0", "vx0", "ox0",
           "qk", "ov", "qx1", "kx1", "vx1", "ox1"]
COL_NAMES = ["bq0", "bq0s", "bk0", "bk0s", "bqx0", "bkx0"]
ROW_NAMES = ["bv0", "bo0", "bvx0", "box0", "box1"]

SELF0, CROSS0, MIX0, CAUSAL1, CROSS1 = range(5)
MHA = {SELF0: 0, CROSS0: 1, CROSS1: 2}


def bank_turns():
    turns, count = {}, {"S": 0, "E": 0, "C": 0, "M": 0}

    def turn(block, what, bank):
        turns[block, what] = (bank, count[bank])
        count[bank] += 1

    for block in range(5):
        if block in MHA:
            for what, bank in (("q", "S"), ("k", "E"), ("v", "C"),
                               ("sq0", "M"), ("sq1", "S"), ("sk0", "E"), ("sk1", "C")):
                turn(block, what, bank)
            for h in range(HEADS):
                turn(block, ("max", h), "S")
                turn(block, ("exp", h), "E")
            for t in range(GROUPS):
                turn(block, ("shift", t), "M")
                turn(block, ("pv", t), "C")
            turn(block, "back0", "M")
            turn(block, "back1", "S")
            turn(block, "ctx", "E")
            turn(block, "out", "C")
        elif block == MIX0:
            turn(block, "gate", "M")
            turn(block, "wT", "S")
            turn(block, "b2", "C")
            for n in range(EXPERTS * FC // 2):
                turn(block, ("up", n), "SE"[n % 2])
            for e in range(EXPERTS):
                turn(block, ("down", e), "CM"[e % 2])
        else:
            for what, bank in (("g", "S"), ("score", "E"), ("pT", "M"), ("ax", "C"), ("out", "S")):
                turn(block, what, bank)
        turn(block, "xT", "M")
    turn(CROSS1, "route", "E")
    return turns


TURNS = bank_turns()


def constants():
    c = np.zeros((P, C_END), np.float32)
    c[:, C_ID:C_ID + P] = np.eye(P)
    c[:, C_TRI:C_TRI + P] = np.triu(np.ones((P, P)), 1)
    c[:, C_ONES:C_ONES + P] = 1.0
    diag = np.where(np.arange(P)[None, :] > np.arange(P)[:, None], MASKED, 0.0)
    c[:, C_MASK:C_MASK + P] = diag
    c[:, C_MASK + 2 * P:C_MASK + 3 * P] = diag
    freqs = np.float32(10000.0) ** (np.arange(0, HD, 2, dtype=np.float32) / np.float32(HD))
    angles = np.arange(SEQ, dtype=np.float32)[:, None] / freqs[None, :]
    cos = np.tile(np.repeat(np.cos(angles), 2, axis=1).T, (HEADS, 1))
    sin = np.tile(np.repeat(np.sin(angles), 2, axis=1).T, (HEADS, 1))
    sin[0::2] *= -1.0
    c[:, C_COS:C_COS + SEQ] = cos
    c[:, C_SIN:C_SIN + SEQ] = sin
    c[0::32, C_KONE] = 1.0
    c[:, C_EPS] = EPS
    c[:, C_FIRST:C_FIRST + 64] = np.tile(EXPERTS - np.arange(EXPERTS), TILES)
    c[:, C_BASE:C_BASE + 64] = np.tile(CAP * np.arange(EXPERTS), TILES)
    spread = np.zeros((P, 4, GROUPS, P), np.float32)
    for t in range(GROUPS):
        for g in range(4):
            for j in range(HD):
                d, r = (4 * t + g) * HD + j, 32 * g + j
                spread[d, QHI, t, [r + 8, r + 16]] = 1.0
                spread[d, QLO, t, r + 24] = 1.0
                spread[d, KHI, t, [r + 8, r + 24]] = 1.0
                spread[d, KLO, t, r + 16] = 1.0
    return c, spread.reshape(P, 4 * GROUPS * P)


def decoder(nc, ins, out):
    f32, f32r, u32 = mybir.dt.float32, mybir.dt.float32r, mybir.dt.uint32
    ALU, ACT, AX = mybir.AluOpType, mybir.ActivationFunctionType, mybir.AxisListType
    stack = ExitStack()
    with stack:
        def sb(name, shape, dt=f32):
            return stack.enter_context(nc.sbuf_tensor(name, shape, dt))

        def sem(name):
            return stack.enter_context(nc.semaphore(name))

        const = sb("const", [P, C_END])
        spread = sb("spread", [P, 4, GROUPS, P], f32r)
        proj_w = sb("proj_w", [P, len(W_NAMES), P])
        cols = sb("cols", [P, len(COL_NAMES)])
        rows = sb("rows", [P, len(ROW_NAMES), P])
        gate_w = sb("gate_w", [P, 2, EXPERTS])
        b1 = sb("b1", [P, EXPERTS * FC])
        b2 = sb("b2", [EXPERTS, P])
        mix0_w1 = sb("mix0_w1", [P, EXPERTS, HID])
        mix0_w2 = sb("mix0_w2", [P, EXPERTS, FC, P])
        mix1_w1 = sb("mix1_w1", [P, EXPERTS, HID])
        mix1_w2 = sb("mix1_w2", [P, EXPERTS, FC, P])
        x_all = sb("x_all", [P, BATCH, SEQ])
        xT_all = sb("xT_all", [P, BATCH, SEQ])
        cT_all = sb("cT_all", [P, BATCH, SEQ])
        logit_all = sb("logit_all", [P, BATCH, QT * EXPERTS])

        ident = const[:, C_ID:C_ID + P]

        def weight(name):
            return proj_w[:, W_NAMES.index(name), :]

        def col(name):
            i = COL_NAMES.index(name)
            return cols[:, i:i + 1]

        def row(name):
            return rows[:, ROW_NAMES.index(name), :]

        def lanes(name, shape, dt=f32):
            return [sb(f"{name}{lane}", shape, dt) for lane in range(LANES)]

        x = lanes("x", [P, QT, P])
        xT = lanes("xT", [P, SEQ])
        cT = lanes("cT", [P, SEQ])
        xb = lanes("xb", [P, QT, P])
        qk = lanes("qk", [P, 2, SEQ])
        qk_hi = lanes("qk_hi", [P, 2, SEQ], f32r)
        qk_lo = lanes("qk_lo", [P, 2, SEQ], f32r)
        q_sp = lanes("q_sp", [P, GROUPS, SEQ], f32r)
        k_sp = lanes("k_sp", [P, GROUPS, SEQ], f32r)
        q_sh = lanes("q_sh", [P, GROUPS, SEQ], f32r)
        v_aug = lanes("v_aug", [P, QT, HEADS, 32])
        negmax = lanes("negmax", [P, GROUPS, QT, P])
        expo = lanes("expo", [P, ESLOTS, QT * SEQ])
        ctx_sb = lanes("ctx_sb", [P, GROUPS, SEQ])
        recip = lanes("recip", [P, QT, HEADS])
        ctx_n = lanes("ctx_n", [P, QT, P])
        aT = lanes("aT", [P, SEQ])
        y = lanes("y", [P, QT, P])
        stats = lanes("stats", [P, QT, 6])
        mv = lanes("mv", [P, QT, 2])
        r0 = lanes("r0", [P, QT])
        newton = lanes("newton", [P, 3, QT])
        gate = lanes("gate", [P, QT, EXPERTS])
        top = lanes("top", [P, QT, 8])
        small = lanes("small", [P, 6, QT])
        g_exp = lanes("g_exp", [P, QT, EXPERTS])
        g_sel = lanes("g_sel", [P, QT, EXPERTS])
        g_w = lanes("g_w", [P, QT, EXPERTS])
        g_wT = lanes("g_wT", [EXPERTS, SEQ])
        masked = lanes("masked", [P, 3 * P])

        bank = [{b: stack.enter_context(nc.psum_tensor(f"bank_{b}{lane}", [P, 512], f32))
                 for b in "SECM"} for lane in range(LANES)]

        ld_x, ld_const, ld_spread, ld_gate = sem("ld_x"), sem("ld_const"), sem("ld_spread"), sem("ld_gate")
        ld_p0, ld_p1 = sem("ld_p0"), sem("ld_p1")
        ld_mix0, ld_mix1 = sem("ld_mix0"), sem("ld_mix1")
        setup_done, v_zeroed = sem("setup_done"), sem("v_zeroed")

        first = sem("x_copied0")
        x_copied = [first, sem("x_copied1")]
        xT_copied = [sem(f"xT_copied{i}") for i in range(LANES)]
        filled = [{b: sem(f"filled_{b}{i}") for b in "SECM"} for i in range(LANES)]
        drained = [{b: sem(f"drained_{b}{i}") for b in "SECM"} for i in range(LANES)]
        split_ready = [sem(f"split_ready{i}") for i in range(LANES)]
        var_ready = [sem(f"var_ready{i}") for i in range(LANES)]
        rstd0_ready = [sem(f"rstd0_ready{i}") for i in range(LANES)]
        x_ready = [sem(f"x_ready{i}") for i in range(LANES)]
        xb_ready = [sem(f"xb_ready{i}") for i in range(LANES)]
        gatemax_ready = [sem(f"gatemax_ready{i}") for i in range(LANES)]
        gateexp_ready = [sem(f"gateexp_ready{i}") for i in range(LANES)]
        gatew_ready = [sem(f"gatew_ready{i}") for i in range(LANES)]
        rowmax_ready = [sem(f"rowmax_ready{i}") for i in range(LANES)]
        probs_ready = [sem(f"probs_ready{i}") for i in range(LANES)]
        act_own = [sem(f"act_own{i}") for i in range(LANES)]
        dve_own = sem("dve_own")
        cleared = range(first.num, dve_own.num + 1)

        def where(lane, block, what):
            return bank[lane][TURNS[block, what][0]]

        def full(lane, block, what):
            return filled[lane][TURNS[block, what][0]]

        def free(lane, block, what):
            return drained[lane][TURNS[block, what][0]]

        def wait_free(pe, lane, block, what):
            if TURNS[block, what][1] > 0:
                pe.wait_ge(free(lane, block, what), TURNS[block, what][1])

        def wait_filled(eng, lane, block, what):
            eng.wait_ge(full(lane, block, what), TURNS[block, what][1] + 1)

        def wait_drained(eng, lane, block, what):
            eng.wait_ge(free(lane, block, what), TURNS[block, what][1] + 1)

        def take_turns(*programs):
            live = list(programs)
            for _ in range(LAG):
                next(live[0])
            while live:
                live = [program for program in live if next(program, live) is None]

        LAG = 12

        with nc.Block() as block:
            @block.sync
            def _(sp):
                sp.dma_start(xT_all[:], ins["xT"]).then_inc(ld_x, 16)
                sp.dma_start(proj_w[:, 0:6, :], ins["proj"][:, 0:6, :]).then_inc(ld_p0, 16)
                sp.dma_start(cols[:], ins["cols"]).then_inc(ld_p0, 16)
                sp.dma_start(rows[:].rearrange("p a b -> p (a b)"),
                             ins["rows"].partition_broadcast(P)).then_inc(ld_p0, 16)
                sp.dma_start(x_all[:], ins["x"]).then_inc(ld_x, 16)
                sp.dma_start(cT_all[:], ins["cT"]).then_inc(ld_x, 16)
                sp.dma_start(proj_w[:, 6:16, :], ins["proj"][:, 6:16, :]).then_inc(ld_p1, 16)
                sp.dma_start(b1[:], ins["b1"]).then_inc(ld_mix0, 16)
                sp.dma_start(b2[:], ins["b2"]).then_inc(ld_mix0, 16)
                sp.dma_start(mix0_w1[:], ins["mix0_w1"]).then_inc(ld_mix0, 16)
                sp.dma_start(mix0_w2[:], ins["mix0_w2"]).then_inc(ld_mix0, 16)
                sp.dma_start(mix1_w1[:], ins["mix1_w1"]).then_inc(ld_mix1, 16)
                sp.dma_start(mix1_w2[:], ins["mix1_w2"]).then_inc(ld_mix1, 16)

            staging = expo[0][:, 0:4, :].rearrange("p a (t c) -> p a t c", t=GROUPS)

            @block.scalar
            def _(act):
                act.dma_start(const[:], ins["const"]).then_inc(ld_const, 16)
                act.dma_start(staging, ins["spread"]).then_inc(ld_spread, 16)
                act.dma_start(gate_w[:], ins["gates"]).then_inc(ld_gate, 16)
                act.wait_ge(ld_spread, 16)
                nc.scalar.preload_act_table_set("natural_log_exp_and_others")
                nc.scalar.activation(spread[:], staging, ACT.Copy).then_inc(setup_done, 1)

            @block.gpsimd
            def _(pool):
                for lane in range(LANES):
                    nc.gpsimd.memset(negmax[lane][:], 0.0)

            @block.vector
            def _(dve):
                for lane in range(LANES):
                    last = nc.vector.memset(v_aug[lane][:].bitcast(u32), 0)
                last.then_inc(v_zeroed, 1)
                dve.wait_ge(v_zeroed, 1)
                for lane in range(LANES):
                    nc.vector.memset(v_aug[lane][:, :, :, HD:HD + 1], 1.0)

        with nc.Fori(0, BATCH // LANES) as pair:
            with nc.Block() as block:
                @block.gpsimd
                def _(pool):
                    def program(lane):
                        if lane == 0:
                            pool.wait_ge(ld_x, 48)
                            pool.wait_ge(ld_p0, 48)
                        nc.gpsimd.tensor_copy(x[lane][:].rearrange("p a d -> p (a d)"),
                                              x_all[:, bass.ds(pair * LANES + lane, 1), :]
                                              .rearrange("p a d -> p (a d)"))
                        nc.gpsimd.tensor_copy(cT[lane][:], cT_all[:, bass.ds(pair * LANES + lane, 1), :]
                                              .rearrange("p a d -> p (a d)")).then_inc(x_copied[lane], 1)
                        pool.wait_ge(x_copied[lane], 1)
                        for block_, bias in ((SELF0, "bo0"), (CROSS0, "box0"), (CROSS1, "box1")):
                            if block_ > SELF0:
                                pool.wait_ge(x_ready[lane], block_)
                            nc.gpsimd.tensor_tensor(
                                xb[lane][:], x[lane][:],
                                row(bias).unsqueeze(1).broadcast_to([P, QT, P]), ALU.add
                            ).then_inc(xb_ready[lane], 1)
                            yield

                    steps = [program(lane) for lane in range(LANES)]
                    for _ in range(3):
                        for s in steps:
                            next(s)

                @block.tensor
                def _(pe):
                    mm = nc.tensor.matmul

                    def attention(lane, b, wq, wk, wv, wo, rope):
                        source = xT[lane] if b == SELF0 else cT[lane]
                        if b == SELF0:
                            pe.wait_ge(ld_p0, 48)
                            pe.wait_ge(xT_copied[lane], 1)
                        else:
                            pe.wait_ge(ld_p1, 16)
                            pe.wait_ge(x_copied[lane], 1)
                            wait_drained(pe, lane, b - 1, "xT")
                        for what, w, src in (("q", wq, xT[lane]), ("k", wk, source)):
                            wait_free(pe, lane, b, what)
                            ps = where(lane, b, what)
                            last = mm(ps[:, 0:SEQ], weight(w), src[:], start=True, stop=True)
                            if rope:
                                last = mm(ps[:, SEQ:2 * SEQ], weight(w + "s"), src[:],
                                          start=True, stop=True)
                            last.then_inc(full(lane, b, what), 1)
                        wait_free(pe, lane, b, "v")
                        ps = where(lane, b, "v")
                        for k in range(QT):
                            last = mm(ps[:, k * P:(k + 1) * P], source[:, k * P:(k + 1) * P],
                                      weight(wv), start=True, stop=True)
                        last.then_inc(full(lane, b, "v"), 1)
                        yield
                        yield
                        pe.wait_ge(split_ready[lane], MHA[b] + 1)
                        if b == SELF0:
                            pe.wait_ge(setup_done, 1)
                        for what, i, hi, lo in (("sq", 0, QHI, QLO), ("sk", 1, KHI, KLO)):
                            for half in range(2):
                                wait_free(pe, lane, b, f"{what}{half}")
                                ps = where(lane, b, f"{what}{half}")
                                for t in (2 * half, 2 * half + 1):
                                    dst = ps[:, (t % 2) * SEQ:(t % 2 + 1) * SEQ]
                                    mm(dst, spread[:, hi, t, :], qk_hi[lane][:, i, :],
                                       start=True, stop=False)
                                    last = mm(dst, spread[:, lo, t, :], qk_lo[lane][:, i, :],
                                              start=False, stop=True)
                                last.then_inc(full(lane, b, f"{what}{half}"), 1)
                        yield
                        for k in range(HEADS + 7):
                            if k < HEADS:
                                t, g = k // 4, k % 4
                                if k == 0:
                                    wait_drained(pe, lane, b, "sq0")
                                    wait_drained(pe, lane, b, "sk0")
                                if k == 8:
                                    wait_drained(pe, lane, b, "sk1")
                                wait_free(pe, lane, b, ("max", k))
                                for qt in range(QT):
                                    last = mm(where(lane, b, ("max", k))[:, qt * SEQ:(qt + 1) * SEQ],
                                              q_sp[lane][32 * g:32 * g + 32, t, qt * P:(qt + 1) * P],
                                              k_sp[lane][32 * g:32 * g + 32, t, :],
                                              start=True, stop=True)
                                last.then_inc(full(lane, b, ("max", k)), 1)
                            if k % 4 == 1 and 4 < k < 21:
                                t = k // 4 - 1
                                wait_drained(pe, lane, b, ("max", 4 * t + 3))
                                wait_free(pe, lane, b, ("shift", t))
                                for qt in range(QT):
                                    last = nc.tensor.transpose(
                                        where(lane, b, ("shift", t))[:, qt * P:(qt + 1) * P],
                                        negmax[lane][:, t, qt, :], ident)
                                last.then_inc(full(lane, b, ("shift", t)), 1)
                            if k >= 6 and k - 6 < HEADS:
                                h = k - 6
                                t, g = h // 4, h % 4
                                if g == 0:
                                    wait_drained(pe, lane, b, ("shift", t))
                                wait_free(pe, lane, b, ("exp", h))
                                for kt in range(QT):
                                    last = mm(where(lane, b, ("exp", h))[:, kt * SEQ:(kt + 1) * SEQ],
                                              k_sp[lane][32 * g:32 * g + 32, t, kt * P:(kt + 1) * P],
                                              q_sh[lane][32 * g:32 * g + 32, t, :],
                                              start=True, stop=True)
                                last.then_inc(full(lane, b, ("exp", h)), 1)
                            if k >= 10 and (k - 10) % 4 == 0:
                                t = (k - 10) // 4
                                wait_drained(pe, lane, b, ("exp", 4 * t + 3))
                                wait_free(pe, lane, b, ("pv", t))
                                if t == 0:
                                    wait_drained(pe, lane, b, "v")
                                for kt in range(QT):
                                    for g in range(4):
                                        h = 4 * t + g
                                        last = mm(where(lane, b, ("pv", t))[32 * g:32 * g + 32, 0:SEQ],
                                                  v_aug[lane][:, kt, h, :],
                                                  expo[lane][:, h % ESLOTS, kt * SEQ:(kt + 1) * SEQ],
                                                  start=(kt == 0), stop=(kt == QT - 1))
                                last.then_inc(full(lane, b, ("pv", t)), 1)
                            yield
                        wait_drained(pe, lane, b, ("pv", GROUPS - 1))
                        for qt in range(QT):
                            wait_free(pe, lane, b, f"back{qt}")
                            for t in range(GROUPS):
                                last = nc.tensor.transpose(
                                    where(lane, b, f"back{qt}")[:, t * P:(t + 1) * P],
                                    ctx_sb[lane][:, t, qt * P:(qt + 1) * P], ident)
                            last.then_inc(full(lane, b, f"back{qt}"), 1)
                        yield
                        wait_free(pe, lane, b, "ctx")
                        for qt in range(QT):
                            wait_drained(pe, lane, b, f"back{qt}")
                            last = nc.tensor.transpose(where(lane, b, "ctx")[:, qt * P:(qt + 1) * P],
                                                       ctx_n[lane][:, qt, :], ident)
                        last.then_inc(full(lane, b, "ctx"), 1)
                        yield
                        wait_drained(pe, lane, b, "ctx")
                        yield from output(lane, b, "out", weight(wo))

                    def output(lane, b, what, w):
                        wait_free(pe, lane, b, what)
                        for qt in range(QT):
                            last = mm(where(lane, b, what)[:, qt * P:(qt + 1) * P],
                                      aT[lane][:, qt * P:(qt + 1) * P], w, start=True, stop=True)
                        last.then_inc(full(lane, b, what), 1)
                        yield

                    def transpose_x(lane, b):
                        yield
                        pe.wait_ge(x_ready[lane], b + 1)
                        wait_free(pe, lane, b, "xT")
                        for qt in range(QT):
                            last = nc.tensor.transpose(where(lane, b, "xT")[:, qt * P:(qt + 1) * P],
                                                       x[lane][:, qt, :], ident)
                        last.then_inc(full(lane, b, "xT"), 1)
                        yield

                    def mixture(lane):
                        b = MIX0
                        pe.wait_ge(ld_gate, 16)
                        wait_drained(pe, lane, b - 1, "xT")
                        wait_free(pe, lane, b, "gate")
                        for qt in range(QT):
                            last = mm(where(lane, b, "gate")[:, qt * EXPERTS:(qt + 1) * EXPERTS],
                                      xT[lane][:, qt * P:(qt + 1) * P], gate_w[:, 0, :],
                                      start=True, stop=True)
                        last.then_inc(full(lane, b, "gate"), 1)
                        yield
                        yield
                        pe.wait_ge(gatew_ready[lane], 1)
                        wait_free(pe, lane, b, "wT")
                        for qt in range(QT):
                            last = nc.tensor.transpose(
                                where(lane, b, "wT")[0:EXPERTS, qt * P:(qt + 1) * P],
                                g_w[lane][:, qt, :], ident)
                        last.then_inc(full(lane, b, "wT"), 1)
                        yield
                        pe.wait_ge(ld_mix0, 64)
                        wait_drained(pe, lane, b, "wT")
                        wait_free(pe, lane, b, "b2")
                        for qt in range(QT):
                            last = mm(where(lane, b, "b2")[:, qt * P:(qt + 1) * P],
                                      g_wT[lane][:, qt * P:(qt + 1) * P], b2[:],
                                      start=True, stop=True)
                        last.then_inc(full(lane, b, "b2"), 1)
                        yield
                        hidden = expo[lane][:, 0:4, :].rearrange("p a (h n) -> p (a h) n", n=SEQ)
                        for n in range(2 * EXPERTS + 2):
                            if n < 2 * EXPERTS:
                                e = n // 2
                                wait_free(pe, lane, b, ("up", n))
                                for i in range(2):
                                    f = 2 * (n % 2) + i
                                    last = mm(where(lane, b, ("up", n))[:, i * SEQ:(i + 1) * SEQ],
                                              mix0_w1[:, e, f * P:(f + 1) * P], xT[lane][:],
                                              start=True, stop=True)
                                last.then_inc(full(lane, b, ("up", n)), 1)
                            if n % 2 == 1 and n > 2:
                                e = (n - 3) // 2
                                for m in (2 * e, 2 * e + 1):
                                    wait_drained(pe, lane, b, ("up", m))
                                wait_free(pe, lane, b, ("down", e))
                                for qt in range(QT):
                                    for f in range(FC):
                                        last = mm(where(lane, b, ("down", e))[:, qt * P:(qt + 1) * P],
                                                  hidden[:, (e % 2) * FC + f, qt * P:(qt + 1) * P],
                                                  mix0_w2[:, e, f, :],
                                                  start=(f == 0), stop=(f == FC - 1))
                                last.then_inc(full(lane, b, ("down", e)), 1)
                            yield

                    def causal(lane):
                        b = CAUSAL1
                        pe.wait_ge(ld_p1, 16)
                        wait_drained(pe, lane, b - 1, "xT")
                        wait_free(pe, lane, b, "g")
                        mm(where(lane, b, "g")[:, 0:SEQ], weight("qk"), xT[lane][:],
                           start=True, stop=True).then_inc(full(lane, b, "g"), 1)
                        yield
                        wait_drained(pe, lane, b, "g")
                        wait_free(pe, lane, b, "score")
                        ps = where(lane, b, "score")
                        mm(ps[:, 0:P], aT[lane][:, 0:P], xT[lane][:, 0:P], start=True, stop=True)
                        mm(ps[:, P:3 * P], aT[lane][:, P:SEQ], xT[lane][:],
                           start=True, stop=True).then_inc(full(lane, b, "score"), 1)
                        yield
                        yield
                        pe.wait_ge(probs_ready[lane], 1)
                        wait_free(pe, lane, b, "pT")
                        for i in range(3):
                            last = nc.tensor.transpose(where(lane, b, "pT")[:, i * P:(i + 1) * P],
                                                       masked[lane][:, i * P:(i + 1) * P], ident)
                        last.then_inc(full(lane, b, "pT"), 1)
                        yield
                        wait_drained(pe, lane, b, "pT")
                        wait_free(pe, lane, b, "ax")
                        pT = expo[lane][:, 0, 0:3 * P]
                        mm(where(lane, b, "ax")[:, 0:SEQ], x[lane][:, 0, :], pT[:, 0:SEQ],
                           start=True, stop=False)
                        mm(where(lane, b, "ax")[:, P:SEQ], x[lane][:, 1, :], pT[:, SEQ:3 * P],
                           start=False, stop=True).then_inc(full(lane, b, "ax"), 1)
                        yield
                        wait_drained(pe, lane, b, "ax")
                        yield from output(lane, b, "out", weight("ov"))

                    def program(lane):
                        yield from attention(lane, SELF0, "q0", "k0", "v0", "o0", True)
                        yield from transpose_x(lane, SELF0)
                        yield from attention(lane, CROSS0, "qx0", "kx0", "vx0", "ox0", False)
                        yield from transpose_x(lane, CROSS0)
                        yield from mixture(lane)
                        yield from transpose_x(lane, MIX0)
                        yield from causal(lane)
                        yield from transpose_x(lane, CAUSAL1)
                        yield from attention(lane, CROSS1, "qx1", "kx1", "vx1", "ox1", False)
                        yield from transpose_x(lane, CROSS1)
                        wait_drained(pe, lane, CROSS1, "xT")
                        wait_free(pe, lane, CROSS1, "route")
                        for qt in range(QT):
                            last = mm(where(lane, CROSS1, "route")[:, qt * EXPERTS:(qt + 1) * EXPERTS],
                                      xT[lane][:, qt * P:(qt + 1) * P], gate_w[:, 1, :],
                                      start=True, stop=True)
                        last.then_inc(full(lane, CROSS1, "route"), 1)
                        yield

                    pe.wait_ge(ld_const, 16)
                    take_turns(*[program(lane) for lane in range(LANES)])

                @block.scalar
                def _(act):
                    activate = nc.scalar.activation

                    def attention(lane, b, bq, bk, scale):
                        if b != SELF0:
                            for i, (what, bias) in enumerate((("q", bq), ("k", bk))):
                                wait_filled(act, lane, b, what)
                                activate(qk[lane][:, i, :], where(lane, b, what)[:, 0:SEQ],
                                         ACT.Identity, bias=bias).then_inc(free(lane, b, what), 1)
                        yield
                        yield
                        for half in range(2):
                            wait_filled(act, lane, b, f"sk{half}")
                            activate(k_sp[lane][:, 2 * half:2 * half + 2, :],
                                     where(lane, b, f"sk{half}")[:].rearrange("p (t n) -> p t n", t=2),
                                     ACT.Identity, bias=const[:, C_KONE:C_KONE + 1]
                                     ).then_inc(free(lane, b, f"sk{half}"), 1)
                        yield
                        for k in range(HEADS + 7):
                            if k >= 6 and k - 6 < HEADS:
                                h = k - 6
                                wait_filled(act, lane, b, ("exp", h))
                                if h >= ESLOTS:
                                    wait_filled(act, lane, b, ("pv", (h - ESLOTS) // 4))
                                activate(expo[lane][:, h % ESLOTS, :], where(lane, b, ("exp", h))[:],
                                         ACT.Exp, scale=scale).then_inc(free(lane, b, ("exp", h)), 1)
                            if k >= 10 and (k - 10) % 4 == 0:
                                t = (k - 10) // 4
                                wait_filled(act, lane, b, ("pv", t))
                                activate(ctx_sb[lane][:, t, :], where(lane, b, ("pv", t))[:, 0:SEQ],
                                         ACT.Copy).then_inc(free(lane, b, ("pv", t)), 1)
                            yield
                        yield
                        wait_filled(act, lane, b, "ctx")
                        activate(aT[lane][:], where(lane, b, "ctx")[:, 0:SEQ],
                                 ACT.Copy).then_inc(free(lane, b, "ctx"), 1)
                        yield
                        yield

                    def normalise(lane, b):
                        act.wait_ge(var_ready[lane], b + 1)
                        activate(r0[lane][:], mv[lane][:, :, 1], ACT.Ln,
                                 bias=const[:, C_EPS:C_EPS + 1]).then_inc(act_own[lane], 1)
                        act.wait_ge(act_own[lane], b + 1)
                        activate(r0[lane][:], r0[lane][:], ACT.Exp,
                                 scale=-0.5).then_inc(rstd0_ready[lane], 1)
                        yield
                        wait_filled(act, lane, b, "xT")
                        activate(xT[lane][:], where(lane, b, "xT")[:, 0:SEQ],
                                 ACT.Copy).then_inc(free(lane, b, "xT"), 1)
                        yield

                    def mixture(lane):
                        b = MIX0
                        yield
                        act.wait_ge(gatemax_ready[lane], 1)
                        for qt in range(QT):
                            last = activate(g_exp[lane][:, qt, :], gate[lane][:, qt, :], ACT.Exp,
                                            bias=small[lane][:, 0, qt:qt + 1])
                        last.then_inc(gateexp_ready[lane], 1)
                        yield
                        wait_filled(act, lane, b, "wT")
                        activate(g_wT[lane][:], where(lane, b, "wT")[0:EXPERTS, 0:SEQ],
                                 ACT.Copy).then_inc(free(lane, b, "wT"), 1)
                        yield
                        yield
                        hidden = expo[lane][:, 0:4, :].rearrange("p a (h n) -> p (a h) n", n=SEQ)
                        act.wait_ge(ld_mix0, 64)
                        for n in range(2 * EXPERTS + 2):
                            if n < 2 * EXPERTS and n % 2 == 0:
                                e = n // 2
                                wait_filled(act, lane, b, ("up", n))
                                if e >= 2:
                                    wait_filled(act, lane, b, ("down", e - 2))
                                for i in range(2):
                                    f = 2 * (n % 2) + i
                                    last = activate(hidden[:, (e % 2) * FC + f, :],
                                                    where(lane, b, ("up", n))[:, i * SEQ:(i + 1) * SEQ],
                                                    ACT.Relu, bias=b1[:, e * FC + f:e * FC + f + 1])
                                last.then_inc(free(lane, b, ("up", n)), 1)
                            yield

                    def causal(lane):
                        b = CAUSAL1
                        wait_filled(act, lane, b, "g")
                        activate(aT[lane][:], where(lane, b, "g")[:, 0:SEQ],
                                 ACT.Copy).then_inc(free(lane, b, "g"), 1)
                        yield
                        yield
                        act.wait_ge(rowmax_ready[lane], 1)
                        for qt, (lo, hi) in enumerate(((0, P), (P, 3 * P))):
                            last = activate(masked[lane][:, lo:hi], masked[lane][:, lo:hi], ACT.Exp,
                                            scale=float(P) ** -0.5, bias=small[lane][:, 1, qt:qt + 1],
                                            accum_out=small[lane][:, 2, qt:qt + 1])
                        last.then_inc(probs_ready[lane], 1)
                        yield
                        wait_filled(act, lane, b, "pT")
                        activate(expo[lane][:, 0, 0:3 * P], where(lane, b, "pT")[:, 0:3 * P],
                                 ACT.Copy).then_inc(free(lane, b, "pT"), 1)
                        yield
                        wait_filled(act, lane, b, "ax")
                        activate(aT[lane][:], where(lane, b, "ax")[:, 0:SEQ],
                                 ACT.Copy).then_inc(free(lane, b, "ax"), 1)
                        yield
                        yield

                    def program(lane):
                        scale = float(HD) ** -0.5
                        yield from attention(lane, SELF0, None, None, scale)
                        yield from normalise(lane, SELF0)
                        yield from attention(lane, CROSS0, col("bqx0"), col("bkx0"), scale)
                        yield from normalise(lane, CROSS0)
                        yield from mixture(lane)
                        yield from normalise(lane, MIX0)
                        yield from causal(lane)
                        yield from normalise(lane, CAUSAL1)
                        yield from attention(lane, CROSS1, 0.0, 0.0, scale)
                        yield from normalise(lane, CROSS1)
                        yield

                    act.wait_ge(ld_x, 48)
                    act.wait_ge(ld_const, 16)
                    act.wait_ge(ld_p0, 48)
                    for lane in range(LANES):
                        activate(xT[lane][:], xT_all[:, bass.ds(pair * LANES + lane, 1), :]
                                 .rearrange("p a d -> p (a d)"), ACT.Copy).then_inc(xT_copied[lane], 1)
                    take_turns(*[program(lane) for lane in range(LANES)])

                @block.vector
                def _(dve):
                    own = [0]

                    def link(instruction):
                        own[0] += 1
                        instruction.then_inc(dve_own, 1)
                        dve.wait_ge(dve_own, own[0])

                    V = nc.vector

                    def attention(lane, b, bv):
                        if b == SELF0:
                            t0 = ctx_sb[lane][:, 0:2, :]
                            t1 = ctx_sb[lane][:, 2:4, :]
                            for i, (what, c0, c1) in enumerate((("q", "bq0", "bq0s"),
                                                                ("k", "bk0", "bk0s"))):
                                wait_filled(dve, lane, b, what)
                                ps = where(lane, b, what)
                                V.scalar_tensor_tensor(t0[:, i, :], ps[:, 0:SEQ], col(c0),
                                                       const[:, C_COS:C_COS + SEQ], ALU.add, ALU.mult)
                                V.scalar_tensor_tensor(t1[:, i, :], ps[:, SEQ:2 * SEQ], col(c1),
                                                       const[:, C_SIN:C_SIN + SEQ], ALU.add, ALU.mult
                                                       ).then_inc(free(lane, b, what), 1)
                            wait_drained(dve, lane, b, "q")
                            wait_drained(dve, lane, b, "k")
                            link(V.tensor_tensor(qk[lane][:], t0, t1, ALU.add))
                        wait_filled(dve, lane, b, "v")
                        ps = where(lane, b, "v")
                        for k in range(QT):
                            src = ps[:, k * P:(k + 1) * P].rearrange("p (h d) -> p h d", d=HD)
                            dst = v_aug[lane][:, k, :, 0:HD]
                            if bv is None:
                                last = V.tensor_copy(dst, src)
                            else:
                                last = V.tensor_tensor(dst, src, row(bv).rearrange(
                                    "p (h d) -> p h d", d=HD), ALU.add)
                        last.then_inc(free(lane, b, "v"), 1)
                        yield
                        if b != SELF0:
                            wait_drained(dve, lane, b, "q")
                            wait_drained(dve, lane, b, "k")
                        link(V.tensor_copy(qk_hi[lane][:], qk[lane][:]))
                        V.tensor_tensor(qk_lo[lane][:], qk[lane][:], qk_hi[lane][:].bitcast(f32),
                                        ALU.subtract).then_inc(split_ready[lane], 1)
                        yield
                        for half in range(2):
                            wait_filled(dve, lane, b, f"sq{half}")
                            V.tensor_copy(q_sp[lane][:, 2 * half:2 * half + 2, :],
                                          where(lane, b, f"sq{half}")[:].rearrange(
                                              "p (t n) -> p t n", t=2)
                                          ).then_inc(free(lane, b, f"sq{half}"), 1)
                        yield
                        for k in range(HEADS + 7):
                            if k < HEADS:
                                wait_filled(dve, lane, b, ("max", k))
                                V.tensor_reduce(negmax[lane][:, k // 4, :, 32 * (k % 4)],
                                                where(lane, b, ("max", k))[:].rearrange(
                                                    "p (q n) -> p q n", q=QT),
                                                AX.X, ALU.max, negate=True
                                                ).then_inc(free(lane, b, ("max", k)), 1)
                            if k % 4 == 1 and 4 < k < 21:
                                t = k // 4 - 1
                                wait_filled(dve, lane, b, ("shift", t))
                                V.tensor_tensor(q_sh[lane][:, t, :], q_sp[lane][:, t, :].bitcast(f32),
                                                where(lane, b, ("shift", t))[:, 0:SEQ], ALU.add
                                                ).then_inc(free(lane, b, ("shift", t)), 1)
                            yield
                        for qt in range(QT):
                            wait_filled(dve, lane, b, f"back{qt}")
                            heads = where(lane, b, f"back{qt}")[:].rearrange("p (h r) -> p h r", r=32)
                            link(V.reciprocal(recip[lane][:, qt, :], heads[:, :, HD]))
                            V.tensor_tensor(ctx_n[lane][:, qt, :].rearrange("p (h d) -> p h d", d=HD),
                                            heads[:, :, 0:HD],
                                            recip[lane][:, qt, :].unsqueeze(2).broadcast_to([P, HEADS, HD]),
                                            ALU.mult).then_inc(free(lane, b, f"back{qt}"), 1)
                        yield
                        yield
                        wait_filled(dve, lane, b, "out")
                        dve.wait_ge(xb_ready[lane], MHA[b] + 1)
                        V.tensor_tensor(y[lane][:].rearrange("p a d -> p (a d)"),
                                        where(lane, b, "out")[:, 0:SEQ],
                                        xb[lane][:].rearrange("p a d -> p (a d)"), ALU.add
                                        ).then_inc(free(lane, b, "out"), 1)
                        wait_drained(dve, lane, b, "out")
                        moments(lane)
                        yield

                    def moments(lane):
                        for qt in range(QT):
                            last = V.bn_stats(stats[lane][:, qt, :], y[lane][:, qt, :])
                        link(last)
                        for qt in range(QT):
                            last = V.bn_aggr(mv[lane][:, qt, :], stats[lane][:, qt, :])
                        last.then_inc(var_ready[lane], 1)

                    def normalise(lane, b):
                        dve.wait_ge(rstd0_ready[lane], b + 1)
                        r, (n0, n1, n2) = r0[lane][:], (newton[lane][:, i, :] for i in range(3))
                        link(V.tensor_tensor(n0, r, r, ALU.mult))
                        link(V.scalar_tensor_tensor(n1, mv[lane][:, :, 1], const[:, C_EPS:C_EPS + 1],
                                                    n0, ALU.add, ALU.mult))
                        link(V.tensor_scalar(n0, n1, -0.5, 1.5, ALU.mult, ALU.add))
                        link(V.tensor_tensor(n2, n0, r, ALU.mult))
                        for qt in range(QT):
                            last = V.tensor_scalar(x[lane][:, qt, :], y[lane][:, qt, :],
                                                   mv[lane][:, qt, 0:1], newton[lane][:, 2, qt:qt + 1],
                                                   ALU.subtract, ALU.mult)
                        last.then_inc(x_ready[lane], 1)
                        yield
                        yield

                    def mixture(lane):
                        b = MIX0
                        wait_filled(dve, lane, b, "gate")
                        V.tensor_copy(gate[lane][:].rearrange("p a e -> p (a e)"),
                                      where(lane, b, "gate")[:, 0:QT * EXPERTS]
                                      ).then_inc(free(lane, b, "gate"), 1)
                        wait_drained(dve, lane, b, "gate")
                        for qt in range(QT):
                            last = V.max(top[lane][:, qt, :], gate[lane][:, qt, :])
                        link(last)
                        V.tensor_scalar(small[lane][:, 0, :], top[lane][:, :, 0], -1.0, None,
                                        ALU.mult).then_inc(gatemax_ready[lane], 1)
                        yield
                        dve.wait_ge(gateexp_ready[lane], 1)
                        for qt in range(QT):
                            last = V.scalar_tensor_tensor(g_sel[lane][:, qt, :], gate[lane][:, qt, :],
                                                          top[lane][:, qt, 1:2], g_exp[lane][:, qt, :],
                                                          ALU.is_ge, ALU.mult)
                        link(last)
                        link(V.tensor_reduce(small[lane][:, 4, :], g_sel[lane][:], AX.X, ALU.add))
                        link(V.reciprocal(small[lane][:, 5, :], small[lane][:, 4, :]))
                        for qt in range(QT):
                            last = V.tensor_scalar(g_w[lane][:, qt, :], g_sel[lane][:, qt, :],
                                                   small[lane][:, 5, qt:qt + 1], 1.0 / EXPERTS,
                                                   ALU.mult, ALU.mult)
                        last.then_inc(gatew_ready[lane], 1)
                        yield
                        yield
                        wait_filled(dve, lane, b, "b2")
                        V.tensor_tensor(y[lane][:].rearrange("p a d -> p (a d)"),
                                        where(lane, b, "b2")[:, 0:SEQ],
                                        x[lane][:].rearrange("p a d -> p (a d)"), ALU.add
                                        ).then_inc(free(lane, b, "b2"), 1)
                        yield
                        hidden = expo[lane][:, 0:4, :].rearrange("p a (h n) -> p (a h) n", n=SEQ)
                        dve.wait_ge(gatew_ready[lane], 1)
                        wait_drained(dve, lane, b, "b2")
                        for n in range(2 * EXPERTS + 2):
                            if n < 2 * EXPERTS and n % 2 == 1:
                                e = n // 2
                                wait_filled(dve, lane, b, ("up", n))
                                if e >= 2:
                                    wait_filled(dve, lane, b, ("down", e - 2))
                                for i in range(2):
                                    f = 2 * (n % 2) + i
                                    last = V.tensor_scalar(hidden[:, (e % 2) * FC + f, :],
                                                           where(lane, b, ("up", n))[:, i * SEQ:(i + 1) * SEQ],
                                                           b1[:, e * FC + f:e * FC + f + 1], 0.0,
                                                           ALU.add, ALU.max)
                                last.then_inc(free(lane, b, ("up", n)), 1)
                            if n % 2 == 1 and n > 2:
                                e = (n - 3) // 2
                                wait_filled(dve, lane, b, ("down", e))
                                if e > 0:
                                    wait_drained(dve, lane, b, ("down", e - 1))
                                for qt in range(QT):
                                    last = V.scalar_tensor_tensor(
                                        y[lane][:, qt, :], where(lane, b, ("down", e))[:, qt * P:(qt + 1) * P],
                                        g_w[lane][:, qt, e:e + 1], y[lane][:, qt, :], ALU.mult, ALU.add)
                                last.then_inc(free(lane, b, ("down", e)), 1)
                            if n == 2 * EXPERTS + 1:
                                wait_drained(dve, lane, b, ("down", EXPERTS - 1))
                                moments(lane)
                            yield

                    def causal(lane):
                        b = CAUSAL1
                        yield
                        wait_filled(dve, lane, b, "score")
                        V.tensor_tensor(masked[lane][:], where(lane, b, "score")[:, 0:3 * P],
                                        const[:, C_MASK:C_MASK + 3 * P], ALU.add
                                        ).then_inc(free(lane, b, "score"), 1)
                        wait_drained(dve, lane, b, "score")
                        V.tensor_reduce(small[lane][:, 3, 0:1], masked[lane][:, 0:P], AX.X, ALU.max,
                                        negate=True)
                        link(V.tensor_reduce(small[lane][:, 3, 1:2], masked[lane][:, P:3 * P], AX.X,
                                             ALU.max, negate=True))
                        V.tensor_scalar(small[lane][:, 1, :], small[lane][:, 3, :], float(P) ** -0.5,
                                        None, ALU.mult).then_inc(rowmax_ready[lane], 1)
                        yield
                        dve.wait_ge(probs_ready[lane], 1)
                        link(V.reciprocal(small[lane][:, 4, :], small[lane][:, 2, :]))
                        yield
                        yield
                        yield
                        wait_filled(dve, lane, b, "out")
                        for qt in range(QT):
                            last = V.scalar_tensor_tensor(
                                y[lane][:, qt, :], where(lane, b, "out")[:, qt * P:(qt + 1) * P],
                                small[lane][:, 4, qt:qt + 1], x[lane][:, qt, :], ALU.mult, ALU.add)
                        last.then_inc(free(lane, b, "out"), 1)
                        wait_drained(dve, lane, b, "out")
                        moments(lane)
                        yield

                    def program(lane):
                        yield from attention(lane, SELF0, "bv0")
                        yield from normalise(lane, SELF0)
                        yield from attention(lane, CROSS0, "bvx0")
                        yield from normalise(lane, CROSS0)
                        yield from mixture(lane)
                        yield from normalise(lane, MIX0)
                        yield from causal(lane)
                        yield from normalise(lane, CAUSAL1)
                        yield from attention(lane, CROSS1, None)
                        yield from normalise(lane, CROSS1)
                        dve.wait_ge(x_ready[lane], CROSS1 + 1)
                        V.tensor_copy(x_all[:, bass.ds(pair * LANES + lane, 1), :]
                                      .rearrange("p a d -> p (a d)"),
                                      x[lane][:].rearrange("p a d -> p (a d)"))
                        wait_filled(dve, lane, CROSS1, "route")
                        V.tensor_copy(logit_all[:, bass.ds(pair * LANES + lane, 1), :]
                                      .rearrange("p a d -> p (a d)"),
                                      where(lane, CROSS1, "route")[:, 0:QT * EXPERTS]
                                      ).then_inc(free(lane, CROSS1, "route"), 1)
                        yield

                    dve.wait_ge(ld_p0, 48)
                    dve.wait_ge(ld_const, 16)
                    for lane in range(LANES):
                        dve.wait_ge(x_copied[lane], 1)
                    take_turns(*[program(lane) for lane in range(LANES)])

            with nc.Block() as block:
                @block.sync
                def _(sp):
                    sp.sem_clear(cleared)

        last_mixture(nc, stack, ins, out, dict(
            const=const, x_all=x_all, logit_all=logit_all, w1=mix1_w1, w2=mix1_w2, banks=bank,
            expo=expo, ctx_sb=ctx_sb, ident=ident, ld_mix1=ld_mix1, zero=negmax))


def last_mixture(nc, stack, ins, out, t):
    f32, i32 = mybir.dt.float32, mybir.dt.int32
    u32 = mybir.dt.uint32
    ALU, ACT, AX = mybir.AluOpType, mybir.ActivationFunctionType, mybir.AxisListType
    TE = TILES * EXPERTS

    def sb(name, shape, dt=f32):
        return stack.enter_context(nc.sbuf_tensor(name, shape, dt))

    def sem(name):
        return stack.enter_context(nc.semaphore(name))

    const, x_all, logit_all, ident = t["const"], t["x_all"], t["logit_all"], t["ident"]
    w1, w2 = t["w1"], t["w2"]
    x8 = x_all[:].rearrange("p b (a d) -> p (b a) d", d=P)
    lg = logit_all[:].rearrange("p b (a e) -> p (b a) e", e=EXPERTS)
    r = sb("r_work", [P, 6, TILES, EXPERTS])
    c8 = sb("c_work", [P, 10, TILES])
    slot = sb("slot", [P, TILES], i32)
    xe = t["expo"][0][:].rearrange("p a b -> p (a b)")[:, 0:EXPERTS * P].rearrange("p (e d) -> p e d", d=P)
    xeT = t["expo"][0][:].rearrange("p a b -> p (a b)")[:, 1024:2048].rearrange("p (e d) -> p e d", d=P)
    ye = t["expo"][0][:].rearrange("p a b -> p (a b)")[:, 2048:3072].rearrange("p (e d) -> p e d", d=P)
    hid = t["expo"][1][:].rearrange("p a b -> p (a b)")[:, 0:1024].rearrange("p (s f n) -> p s f n", s=2, f=FC)
    yg = t["expo"][1][:].rearrange("p a b -> p (a b)")[:, 1024:2048].rearrange("p (a d) -> p a d", d=P)
    yo = t["expo"][1][:].rearrange("p a b -> p (a b)")[:, 2048:3072].rearrange("p (a d) -> p a d", d=P)
    stats = sb("stats_all", [P, TILES, 6])
    mv = sb("mv_all", [P, TILES, 2])
    rs = sb("rs_all", [P, 4, TILES])
    xe_dram = nc.dram_tensor("xe_scratch", (EXPERTS * CAP, P), f32, kind="Internal").ap()
    ye_dram = nc.dram_tensor("ye_scratch", (EXPERTS * CAP, P), f32, kind="Internal").ap()
    ps = [t["banks"][lane][b] for lane in range(LANES) for b in "SECM"]

    xe_zeroed, zero_ready, shifted, exp_ready, onehot_ready, rank_filled, slot_ready = (
        sem("xe_zeroed"), sem("zero_ready"), sem("shifted"), sem("exp_ready"), sem("onehot_ready"),
        sem("rank_filled"), sem("slot_ready"))
    scattered, xe_loaded, xeT_filled, xeT_ready = (
        sem("scattered"), sem("xe_loaded"), sem("xeT_filled"), sem("xeT_ready"))
    up_filled, hid_act, down_filled, ye_ready, ye_stored = (
        sem("up_filled"), sem("hid_ready"), sem("down_filled"), sem("ye_ready"), sem("ye_stored"))
    gathered, var_ready, rstd0_ready, y_ready, stored, yg_zeroed, prefix_ready, ln_own = (
        sem("gathered"), sem("var_all_ready"), sem("rstd0_all_ready"), sem("y_ready"), sem("stored"),
        sem("yg_zeroed"), sem("prefix_ready"), sem("ln_own"))
    own_sem = sem("dve_last_own")
    base = const[:, C_BASE:C_BASE + TE].rearrange("p (a e) -> p a e", e=EXPERTS)
    order = const[:, C_FIRST:C_FIRST + TE].rearrange("p (a e) -> p a e", e=EXPERTS)

    with nc.Block() as block:
        @block.vector
        def _(dve):
            V = nc.vector
            own = [0]

            def link(instruction):
                own[0] += 1
                instruction.then_inc(own_sem, 1)
                dve.wait_ge(own_sem, own[0])

            def wide(ap):
                return ap.unsqueeze(2).broadcast_to([P, TILES, EXPERTS])

            V.memset(xe.bitcast(u32), 0).then_inc(zero_ready, 1)
            mx, total, p_tok, rank, keep, dest, weight = (c8[:, i, :] for i in range(7))
            link(V.tensor_reduce(mx, lg, AX.X, ALU.max))
            V.tensor_tensor(r[:, 0], lg, wide(mx), ALU.subtract).then_inc(shifted, 1)
            link(V.tensor_tensor(r[:, 1], lg, wide(mx), ALU.is_ge))
            link(V.tensor_tensor(r[:, 2], r[:, 1], order, ALU.mult))
            link(V.tensor_reduce(c8[:, 7, :], r[:, 2], AX.X, ALU.max))
            link(V.tensor_tensor(r[:, 1], r[:, 2], wide(c8[:, 7, :]), ALU.is_equal))
            link(V.memset(r[:, 3, 0, :], 0.0))
            for i in range(1, TILES):
                link(V.tensor_tensor(r[:, 3, i, :], r[:, 3, i - 1, :], r[:, 1, i - 1, :], ALU.add))
            V.memset(yg.bitcast(u32), 0).then_inc(yg_zeroed, 1)
            dve.wait_ge(exp_ready, 1)
            link(V.tensor_reduce(total, r[:, 4], AX.X, ALU.add))
            link(V.reciprocal(p_tok, total))
            dve.wait_ge(rank_filled, 1)
            ranks = ps[0][:, 0:TE].rearrange("p (a e) -> p a e", e=EXPERTS)
            link(V.tensor_tensor(r[:, 0], ranks, r[:, 1], ALU.mult))
            link(V.tensor_tensor(r[:, 2], base, r[:, 1], ALU.mult))
            link(V.tensor_reduce(rank, r[:, 0], AX.X, ALU.add))
            link(V.tensor_reduce(dest, r[:, 2], AX.X, ALU.add))
            link(V.tensor_scalar(keep, rank, float(CAP), None, ALU.is_lt))
            link(V.tensor_tensor(c8[:, 8, :], rank, dest, ALU.add))
            link(V.tensor_scalar(c8[:, 9, :], keep, -float(4 * TOKENS), float(4 * TOKENS),
                                 ALU.mult, ALU.add))
            V.tensor_tensor(slot[:], c8[:, 8, :], c8[:, 9, :], ALU.add).then_inc(slot_ready, 1)
            link(V.tensor_tensor(weight, p_tok, keep, ALU.mult))
            for half in range(2):
                dve.wait_ge(xeT_filled, half + 1)
                V.tensor_copy(xeT[:, 4 * half:4 * half + 4, :].rearrange("p a b -> p (a b)"),
                              ps[1 + half][:]).then_inc(xeT_ready, 1)
            for e in range(EXPERTS):
                dve.wait_ge(down_filled, e + 1)
                V.tensor_copy(ye[:, e, :], ps[5 + e % 2][:, 0:P]).then_inc(ye_ready, 1)
            dve.wait_ge(gathered, 16 * TILES)
            for i in range(TILES):
                last = V.scalar_tensor_tensor(yo[:, i, :], yg[:, i, :], weight[:, i:i + 1],
                                              x8[:, i, :], ALU.mult, ALU.add)
            link(last)
            for i in range(TILES):
                last = V.bn_stats(stats[:, i, :], yo[:, i, :])
            link(last)
            for i in range(TILES):
                last = V.bn_aggr(mv[:, i, :], stats[:, i, :])
            last.then_inc(var_ready, 1)
            dve.wait_ge(rstd0_ready, 1)
            link(V.tensor_tensor(rs[:, 1], rs[:, 0], rs[:, 0], ALU.mult))
            link(V.scalar_tensor_tensor(rs[:, 2], mv[:, :, 1], const[:, C_EPS:C_EPS + 1], rs[:, 1],
                                        ALU.add, ALU.mult))
            link(V.tensor_scalar(rs[:, 1], rs[:, 2], -0.5, 1.5, ALU.mult, ALU.add))
            link(V.tensor_tensor(rs[:, 3], rs[:, 1], rs[:, 0], ALU.mult))
            for i in range(TILES):
                V.tensor_scalar(yg[:, i, :], yo[:, i, :], mv[:, i, 0:1], rs[:, 3, i:i + 1],
                                ALU.subtract, ALU.mult).then_inc(y_ready, 1)

        @block.scalar
        def _(act):
            act.wait_ge(shifted, 1)
            nc.scalar.activation(r[:, 4], r[:, 0], ACT.Exp).then_inc(exp_ready, 1)
            for e in range(EXPERTS):
                act.wait_ge(up_filled, e + 1)
                if e >= 2:
                    act.wait_ge(down_filled, e - 1)
                nc.scalar.activation(hid[:, e % 2].rearrange("p f n -> p (f n)"), ps[3 + e % 2][:],
                                     ACT.Relu).then_inc(hid_act, 1)
            act.wait_ge(var_ready, 1)
            nc.scalar.activation(rs[:, 0], mv[:, :, 1], ACT.Ln,
                                 bias=const[:, C_EPS:C_EPS + 1]).then_inc(ln_own, 1)
            act.wait_ge(ln_own, 1)
            nc.scalar.activation(rs[:, 0], rs[:, 0], ACT.Exp, scale=-0.5).then_inc(rstd0_ready, 1)

        @block.tensor
        def _(pe):
            mm = nc.tensor.matmul
            pe.wait_ge(own_sem, 6 + TILES - 1)
            flat = lambda i: r[:, i].rearrange("p a e -> p (a e)")
            mm(ps[0][:, 0:TE], const[:, C_TRI:C_TRI + P], flat(1), start=True, stop=False)
            mm(ps[0][:, 0:TE], const[:, C_ONES:C_ONES + P], flat(3), start=False,
               stop=True).then_inc(rank_filled, 1)
            pe.wait_ge(xe_loaded, 16)
            for half in range(2):
                for e in range(4 * half, 4 * half + 4):
                    last = nc.tensor.transpose(ps[1 + half][:, (e % 4) * P:(e % 4 + 1) * P],
                                               xe[:, e, :], ident)
                last.then_inc(xeT_filled, 1)
            pe.wait_ge(t["ld_mix1"], 32)
            for e in range(EXPERTS + 1):
                if e < EXPERTS:
                    pe.wait_ge(xeT_ready, e // 4 + 1)
                    if e >= 2:
                        pe.wait_ge(hid_act, e - 1)
                    for f in range(FC):
                        last = mm(ps[3 + e % 2][:, f * P:(f + 1) * P], w1[:, e, f * P:(f + 1) * P],
                                  xeT[:, e, :], start=True, stop=True)
                    last.then_inc(up_filled, 1)
                if e > 0:
                    d = e - 1
                    pe.wait_ge(hid_act, d + 1)
                    if d >= 2:
                        pe.wait_ge(ye_ready, d - 1)
                    for f in range(FC):
                        last = mm(ps[5 + d % 2][:, 0:P], hid[:, d % 2, f, :], w2[:, d, f, :],
                                  start=(f == 0), stop=(f == FC - 1))
                    last.then_inc(down_filled, 1)

        @block.gpsimd
        def _(pool):
            pool.wait_ge(slot_ready, 1)
            pool.wait_ge(xe_zeroed, 16)
            for i in range(TILES):
                nc.gpsimd.indirect_dma_start(
                    xe_dram, bass.IndirectOffsetOnAxis(slot[:, i:i + 1].bitcast(u32), 0),
                    x8[:, i, :], None, bounds_check=TOKENS - 1, oob_is_err=False
                ).then_inc(scattered, 16)
            pool.wait_ge(ye_stored, 16 * EXPERTS)
            pool.wait_ge(yg_zeroed, 1)
            for i in range(TILES):
                nc.gpsimd.indirect_dma_start(
                    yg[:, i, :], None, ye_dram,
                    bass.IndirectOffsetOnAxis(slot[:, i:i + 1].bitcast(u32), 0),
                    bounds_check=TOKENS - 1, oob_is_err=False).then_inc(gathered, 16)

        @block.sync
        def _(sp):
            sp.wait_ge(zero_ready, 1)
            sp.dma_start(xe_dram.rearrange("(e p) d -> p e d", p=P), xe).then_inc(xe_zeroed, 16)
            sp.wait_ge(xe_zeroed, 16)
            sp.wait_ge(scattered, 16 * TILES)
            sp.dma_start(xe, xe_dram.rearrange("(e p) d -> p e d", p=P)).then_inc(xe_loaded, 16)
            for e in range(EXPERTS):
                sp.wait_ge(ye_ready, e + 1)
                sp.dma_start(ye_dram[e * CAP:(e + 1) * CAP, :], ye[:, e, :]).then_inc(ye_stored, 16)
            for half in range(2):
                n = TILES // 2
                sp.wait_ge(y_ready, n * (half + 1))
                sp.dma_start(out.rearrange("b (a p) d -> p (b a) d", p=P)[:, n * half:n * (half + 1), :],
                             yg[:, n * half:n * (half + 1), :]).then_inc(stored, 16)
            sp.wait_ge(stored, 32)


def kernel(**inputs):
    import concourse.bacc as _bacc
    from concourse.bass_utils import run_bass_kernel_spmd as _run

    a = {k: np.asarray(v) for k, v in inputs.items()}
    swap = np.arange(P) ^ 1

    def by_token(v):
        return v.reshape(TILES, P, P).transpose(1, 0, 2).reshape(P, BATCH, SEQ)

    def by_width(v):
        return v.reshape(BATCH, SEQ, P).transpose(2, 0, 1)

    wq, wk = a["L0_attn_wq"].T, a["L0_attn_wk"].T
    mats = [wq, wq[:, swap], wk, wk[:, swap], a["L0_attn_wv"].T, a["L0_attn_wo"].T,
            a["L0_xattn_Wq"].T, a["L0_xattn_Wk"].T, a["L0_xattn_Wv"].T, a["L0_xattn_Wo"].T,
            a["L1_attn_qk"], a["L1_attn_ov"],
            a["L1_xattn_Wq"].T, a["L1_xattn_Wk"].T, a["L1_xattn_Wv"].T, a["L1_xattn_Wo"].T]
    bq, bk = a["L0_attn_bq"], a["L0_attn_bk"]
    const, spread = constants()
    arrays = {
        "x": by_token(a["x"]), "xT": by_width(a["x"]), "cT": by_width(a["ctx_1024"]),
        "proj": np.stack(mats, 1),
        "cols": np.stack([bq, bq[swap], bk, bk[swap], a["L0_xattn_bq"], a["L0_xattn_bk"]], 1),
        "rows": np.concatenate([a["L0_attn_bv"], a["L0_attn_bo"], a["L0_xattn_bv"],
                                a["L0_xattn_bo"], a["L1_xattn_bo"]]),
        "gates": np.stack([a["L0_ffn_W_gate"], a["L1_ffn_Wr"]], 1),
        "b1": a["L0_ffn_b1"].reshape(EXPERTS * FC, P).T, "b2": a["L0_ffn_b2"],
        "mix0_w1": a["L0_ffn_W1"].transpose(1, 0, 2),
        "mix0_w2": a["L0_ffn_W2"].reshape(EXPERTS, FC, P, P).transpose(2, 0, 1, 3),
        "mix1_w1": a["L1_ffn_W1"].transpose(1, 0, 2),
        "mix1_w2": a["L1_ffn_W2"].reshape(EXPERTS, FC, P, P).transpose(2, 0, 1, 3),
        "const": const, "spread": spread,
    }
    arrays = {k: np.ascontiguousarray(v) for k, v in arrays.items()}
    nc = _bacc.Bacc("TRN2", target_bir_lowering=False, num_devices=1)
    ins = {k: nc.dram_tensor(f"in_{k}", v.shape, mybir.dt.from_np(v.dtype), kind="ExternalInput").ap()
           for k, v in arrays.items()}
    ins["spread"] = ins["spread"].rearrange("p (k t c) -> p k t c", k=4, t=GROUPS)
    out = nc.dram_tensor("out", (BATCH, SEQ, P), mybir.dt.float32, kind="ExternalOutput").ap()
    decoder(nc, ins, out)
    r = _run(nc, [{f"in_{k}": v for k, v in arrays.items()}], core_ids=[0])
    return r.results[0]["out"]
```

```python
import numpy as np
import concourse.bass as bass
from concourse import mybir
from contextlib import ExitStack

P = 128
BATCH, SEQ = 4, 256
TOKENS = BATCH * SEQ
TILES = TOKENS // P
QT = SEQ // P
HEADS, HD = 16, 8
GROUPS = HEADS // 4
EXPERTS, HID = 8, 512
FC = HID // P
CAP = TOKENS // EXPERTS
LANES = 2
EPS = 1e-5
ESLOTS = 6
MASKED = -3.0e38

C_ID, C_TRI, C_ONES, C_MASK, C_COS, C_SIN = 0, 128, 256, 384, 768, 1024
C_KONE, C_EPS, C_FIRST, C_BASE, C_END = 1280, 1281, 1282, 1346, 1410
QHI, QLO, KHI, KLO = range(4)
W_NAMES = ["q0", "q0s", "k0", "k0s", "v0", "o0", "qx0", "kx0", "vx0", "ox0",
           "qk", "ov", "qx1", "kx1", "vx1", "ox1"]
COL_NAMES = ["bq0", "bq0s", "bk0", "bk0s", "bqx0", "bkx0"]
ROW_NAMES = ["bv0", "bo0", "bvx0", "box0", "box1"]

SELF0, CROSS0, MIX0, CAUSAL1, CROSS1 = range(5)
MHA = {SELF0: 0, CROSS0: 1, CROSS1: 2}


LAG = 16
SHIFT_AT = 5
EXP_AT = 6
VALUES_AT = 11
HEAD_STEPS = VALUES_AT + 4 * (GROUPS - 1) + 1
MIX_STEPS = 2 * EXPERTS + 2
MOMENTS_LEAD = 0
ROOT_LEAD = 0
OUTPUT_LEAD = 1
GATE_LEAD = 1
PROBS_LEAD = 1
SPLIT_LEAD = 0


def take_turns(*programs):
    live = list(programs)
    for _ in range(LAG):
        next(live[0])
    while live:
        live = [program for program in live if next(program, live) is None]


def group_at(step, start):
    t, rest = divmod(step - start, 4)
    return t if rest == 0 and 0 <= t < GROUPS else None


def empty(steps):
    for _ in range(steps):
        yield


def bank_turns():
    turns, count = {}, {pool: 0 for pool in POOLS}

    def lane_steps(lane):
        def turn(block, what, pool):
            turns[lane, block, what] = (pool, count[pool] % POOLS[pool], count[pool] // POOLS[pool])
            count[pool] += 1

        def keys_values(b):
            turn(b, "k", "M")
            turn(b, "v", "C")
            yield
            for half in range(2):
                turn(b, f"sk{half}", "M")
            yield

        def queries(b):
            turn(b, "q", "M")
            yield from empty(1 + SPLIT_LEAD)
            for half in range(2):
                turn(b, f"sq{half}", "M")
            yield

        def heads(b):
            for k in range(HEAD_STEPS):
                if group_at(k, SHIFT_AT) is not None:
                    turn(b, ("shift", group_at(k, SHIFT_AT)), "M")
                if k < HEADS:
                    turn(b, ("max", k), "S")
                if 0 <= k - EXP_AT < HEADS:
                    turn(b, ("exp", k - EXP_AT), "E")
                if group_at(k, VALUES_AT) is not None:
                    turn(b, ("pv", group_at(k, VALUES_AT)), "C")
                yield

        def attention_end(b, side):
            turn(b, "back0", "M")
            turn(b, "back1", "M")
            next(side, None)
            yield
            turn(b, "ctx", "M")
            next(side, None)
            yield
            turn(b, "out", "M")
            yield

        def end(b):
            yield from empty(MOMENTS_LEAD + ROOT_LEAD + 1 + OUTPUT_LEAD)
            turn(b, "xT", "M")
            yield

        turn(SELF0, "k", "E")
        yield
        turn(SELF0, "q", "S")
        yield
        turn(SELF0, "v", "C")
        yield
        for what in ("sk0", "sk1", "sq0", "sq1"):
            turn(SELF0, what, "M")
            if what[-1] == "1":
                yield
        yield
        yield from heads(SELF0)
        yield from attention_end(SELF0, keys_values(CROSS0))
        yield from end(SELF0)
        yield from queries(CROSS0)
        yield from heads(CROSS0)
        yield from attention_end(CROSS0, iter(()))
        yield from end(CROSS0)
        turn(MIX0, "gate", "M")
        yield from empty(2 + GATE_LEAD)
        turn(MIX0, "wT", "M")
        yield
        turn(MIX0, "b2", "M")
        yield
        side = keys_values(CROSS1)
        for n in range(MIX_STEPS):
            if n < 2 * EXPERTS:
                turn(MIX0, ("up", n), "SE"[n % 2])
            if n % 2 == 1 and n > 2:
                turn(MIX0, ("down", (n - 3) // 2), "C")
            if n in SIDE_STEPS:
                next(side, None)
            yield
        yield from end(MIX0)
        turn(CAUSAL1, "g", "M")
        yield
        turn(CAUSAL1, "score", "M")
        yield from empty(2 + PROBS_LEAD)
        turn(CAUSAL1, "pT", "M")
        yield
        turn(CAUSAL1, "ax", "M")
        yield
        turn(CAUSAL1, "out", "M")
        yield
        yield from end(CAUSAL1)
        yield from queries(CROSS1)
        yield from heads(CROSS1)
        yield from attention_end(CROSS1, iter(()))
        yield from end(CROSS1)
        turn(CROSS1, "route", "M")
        yield

    take_turns(*[lane_steps(lane) for lane in range(LANES)])
    return turns


POOLS = {"S": 2, "E": 2, "C": 2, "M": 2}
SIDE_STEPS = (12, 16)
TURNS = bank_turns()


def constants():
    c = np.zeros((P, C_END), np.float32)
    c[:, C_ID:C_ID + P] = np.eye(P)
    c[:, C_TRI:C_TRI + P] = np.triu(np.ones((P, P)), 1)
    c[:, C_ONES:C_ONES + P] = 1.0
    diag = np.where(np.arange(P)[None, :] > np.arange(P)[:, None], MASKED, 0.0)
    c[:, C_MASK:C_MASK + P] = diag
    c[:, C_MASK + 2 * P:C_MASK + 3 * P] = diag
    freqs = np.float32(10000.0) ** (np.arange(0, HD, 2, dtype=np.float32) / np.float32(HD))
    angles = np.arange(SEQ, dtype=np.float32)[:, None] / freqs[None, :]
    cos = np.tile(np.repeat(np.cos(angles), 2, axis=1).T, (HEADS, 1))
    sin = np.tile(np.repeat(np.sin(angles), 2, axis=1).T, (HEADS, 1))
    sin[0::2] *= -1.0
    c[:, C_COS:C_COS + SEQ] = cos
    c[:, C_SIN:C_SIN + SEQ] = sin
    c[0::32, C_KONE] = 1.0
    c[:, C_EPS] = EPS
    c[:, C_FIRST:C_FIRST + 64] = np.tile(EXPERTS - np.arange(EXPERTS), TILES)
    c[:, C_BASE:C_BASE + 64] = np.tile(CAP * np.arange(EXPERTS), TILES)
    spread = np.zeros((P, 4, GROUPS, P), np.float32)
    for t in range(GROUPS):
        for g in range(4):
            for j in range(HD):
                d, r = (4 * t + g) * HD + j, 32 * g + j
                spread[d, QHI, t, [r + 8, r + 16]] = 1.0
                spread[d, QLO, t, r + 24] = 1.0
                spread[d, KHI, t, [r + 8, r + 24]] = 1.0
                spread[d, KLO, t, r + 16] = 1.0
    return c, spread.reshape(P, 4 * GROUPS * P)


def decoder(nc, ins, out):
    f32, f32r, u32 = mybir.dt.float32, mybir.dt.float32r, mybir.dt.uint32
    ALU, ACT, AX = mybir.AluOpType, mybir.ActivationFunctionType, mybir.AxisListType
    stack = ExitStack()
    with stack:
        def sb(name, shape, dt=f32):
            return stack.enter_context(nc.sbuf_tensor(name, shape, dt))

        def sem(name):
            return stack.enter_context(nc.semaphore(name))

        const = sb("const", [P, C_END])
        spread = sb("spread", [P, 4, GROUPS, P], f32r)
        proj_w = sb("proj_w", [P, len(W_NAMES), P])
        cols = sb("cols", [P, len(COL_NAMES)])
        rows = sb("rows", [P, len(ROW_NAMES), P])
        gate_w = sb("gate_w", [P, 2, EXPERTS])
        b1 = sb("b1", [P, EXPERTS * FC])
        b2 = sb("b2", [EXPERTS, P])
        mix0_w1 = sb("mix0_w1", [P, EXPERTS, HID])
        mix0_w2 = sb("mix0_w2", [P, EXPERTS, FC, P])
        x_all = sb("x_all", [P, BATCH, SEQ])
        xT_all = sb("xT_all", [P, BATCH, SEQ])
        cT_all = sb("cT_all", [P, BATCH, SEQ])
        logit_all = sb("logit_all", [P, BATCH, QT * EXPERTS])

        ident = const[:, C_ID:C_ID + P]

        def weight(name):
            return proj_w[:, W_NAMES.index(name), :]

        def col(name):
            i = COL_NAMES.index(name)
            return cols[:, i:i + 1]

        def row(name):
            return rows[:, ROW_NAMES.index(name), :]

        def lanes(name, shape, dt=f32):
            return [sb(f"{name}{lane}", shape, dt) for lane in range(LANES)]

        x = lanes("x", [P, QT, P])
        xT = lanes("xT", [P, SEQ])
        cT = lanes("cT", [P, SEQ])
        xb = lanes("xb", [P, QT, P])
        qk = lanes("qk", [P, 2, SEQ])
        qk_hi = lanes("qk_hi", [P, 2, SEQ], f32r)
        qk_lo = lanes("qk_lo", [P, 2, SEQ], f32r)
        q_sp = lanes("q_sp", [P, GROUPS, SEQ], f32r)
        k_sp = lanes("k_sp", [P, GROUPS, SEQ], f32r)
        k_head = lanes("k_head", [P, GROUPS, 4, SEQ], f32r)
        q_sh = lanes("q_sh", [P, GROUPS, SEQ], f32r)
        v_aug = lanes("v_aug", [P, QT, HEADS, 32])
        negmax = lanes("negmax", [P, GROUPS, QT, P])
        expo = lanes("expo", [P, ESLOTS, QT * SEQ])
        ctx_sb = lanes("ctx_sb", [P, GROUPS, SEQ])
        recip = lanes("recip", [P, QT, HEADS])
        ctx_n = lanes("ctx_n", [P, QT, P])
        aT = lanes("aT", [P, SEQ])
        y = lanes("y", [P, QT, P])
        stats = lanes("stats", [P, QT, 6])
        mv = lanes("mv", [P, QT, 2])
        r0 = lanes("r0", [P, QT])
        newton = lanes("newton", [P, 3, QT])
        gate = lanes("gate", [P, QT, EXPERTS])
        top = lanes("top", [P, QT, 8])
        small = lanes("small", [P, 6, QT])
        g_exp = lanes("g_exp", [P, QT, EXPERTS])
        g_sel = lanes("g_sel", [P, QT, EXPERTS])
        g_w = lanes("g_w", [P, QT, EXPERTS])
        g_wT = lanes("g_wT", [EXPERTS, SEQ])
        masked = lanes("masked", [P, 3 * P])

        bank = {pool: [stack.enter_context(nc.psum_tensor(f"bank_{pool}{i}", [P, 512], f32))
                       for i in range(n)] for pool, n in POOLS.items()}

        ld_x, ld_const, ld_spread, ld_gate = sem("ld_x"), sem("ld_const"), sem("ld_spread"), sem("ld_gate")
        ld_p0, ld_p1 = sem("ld_p0"), sem("ld_p1")
        ld_mix0 = sem("ld_mix0")
        setup_done, v_zeroed = sem("setup_done"), sem("v_zeroed")

        first = sem("x_copied0")
        x_copied = [first, sem("x_copied1")]
        xT_copied = [sem(f"xT_copied{i}") for i in range(LANES)]
        filled = {pool: [sem(f"filled_{pool}{i}") for i in range(n)] for pool, n in POOLS.items()}
        drained = {pool: [sem(f"drained_{pool}{i}") for i in range(n)] for pool, n in POOLS.items()}
        k_head_ready = [[sem(f"k_head_ready{i}_{half}") for half in range(2)] for i in range(LANES)]
        split_q_ready = [sem(f"split_q_ready{i}") for i in range(LANES)]
        split_k_ready = [sem(f"split_k_ready{i}") for i in range(LANES)]
        var_ready = [sem(f"var_ready{i}") for i in range(LANES)]
        rstd0_ready = [sem(f"rstd0_ready{i}") for i in range(LANES)]
        x_ready = [sem(f"x_ready{i}") for i in range(LANES)]
        xb_ready = [sem(f"xb_ready{i}") for i in range(LANES)]
        gatemax_ready = [sem(f"gatemax_ready{i}") for i in range(LANES)]
        gateexp_ready = [sem(f"gateexp_ready{i}") for i in range(LANES)]
        gatew_ready = [sem(f"gatew_ready{i}") for i in range(LANES)]
        rowmax_ready = [sem(f"rowmax_ready{i}") for i in range(LANES)]
        probs_ready = [sem(f"probs_ready{i}") for i in range(LANES)]
        act_own = [sem(f"act_own{i}") for i in range(LANES)]
        dve_own = sem("dve_own")
        cleared = range(first.num, dve_own.num + 1)

        def where(lane, block, what):
            pool, i, _ = TURNS[lane, block, what]
            return bank[pool][i]

        def full(lane, block, what):
            pool, i, _ = TURNS[lane, block, what]
            return filled[pool][i]

        def free(lane, block, what):
            pool, i, _ = TURNS[lane, block, what]
            return drained[pool][i]

        def wait_free(pe, lane, block, what):
            if TURNS[lane, block, what][2] > 0:
                pe.wait_ge(free(lane, block, what), TURNS[lane, block, what][2])

        def wait_filled(eng, lane, block, what):
            eng.wait_ge(full(lane, block, what), TURNS[lane, block, what][2] + 1)

        def wait_drained(eng, lane, block, what):
            eng.wait_ge(free(lane, block, what), TURNS[lane, block, what][2] + 1)

        with nc.Block() as block:
            @block.sync
            def _(sp):
                sp.dma_start(xT_all[:], ins["xT"]).then_inc(ld_x, 16)
                sp.dma_start(proj_w[:, 0:6, :], ins["proj"][:, 0:6, :]).then_inc(ld_p0, 16)
                sp.dma_start(cols[:], ins["cols"]).then_inc(ld_p0, 16)
                sp.dma_start(rows[:].rearrange("p a b -> p (a b)"),
                             ins["rows"].partition_broadcast(P)).then_inc(ld_p0, 16)
                sp.dma_start(x_all[:], ins["x"]).then_inc(ld_x, 16)
                sp.dma_start(cT_all[:], ins["cT"]).then_inc(ld_x, 16)
                sp.dma_start(proj_w[:, 6:16, :], ins["proj"][:, 6:16, :]).then_inc(ld_p1, 16)
                sp.dma_start(b1[:], ins["b1"]).then_inc(ld_mix0, 16)
                sp.dma_start(b2[:], ins["b2"]).then_inc(ld_mix0, 16)
                sp.dma_start(mix0_w1[:], ins["mix0_w1"]).then_inc(ld_mix0, 16)
                sp.dma_start(mix0_w2[:], ins["mix0_w2"]).then_inc(ld_mix0, 16)

            staging = expo[0][:, 0:4, :].rearrange("p a (t c) -> p a t c", t=GROUPS)

            @block.scalar
            def _(act):
                act.dma_start(const[:], ins["const"]).then_inc(ld_const, 16)
                act.dma_start(staging, ins["spread"]).then_inc(ld_spread, 16)
                act.dma_start(gate_w[:], ins["gates"]).then_inc(ld_gate, 16)
                act.wait_ge(ld_spread, 16)
                nc.scalar.preload_act_table_set("natural_log_exp_and_others")
                nc.scalar.activation(spread[:], staging, ACT.Copy).then_inc(setup_done, 1)

            @block.gpsimd
            def _(pool):
                nc.gpsimd.memset(k_head[1][:].bitcast(u32), 0)
                for lane in range(LANES):
                    nc.gpsimd.memset(negmax[lane][:], 0.0)

            @block.vector
            def _(dve):
                for lane in range(LANES):
                    last = nc.vector.memset(v_aug[lane][:].bitcast(u32), 0)
                nc.vector.memset(k_head[0][:].bitcast(u32), 0)
                last.then_inc(v_zeroed, 1)
                dve.wait_ge(v_zeroed, 1)
                for lane in range(LANES):
                    nc.vector.memset(v_aug[lane][:, :, :, HD:HD + 1], 1.0)

        with nc.Fori(0, BATCH // LANES) as pair:
            with nc.Block() as block:
                @block.gpsimd
                def _(pool):
                    def program(lane):
                        if lane == 0:
                            pool.wait_ge(ld_x, 48)
                            pool.wait_ge(ld_p0, 48)
                        nc.gpsimd.tensor_copy(x[lane][:].rearrange("p a d -> p (a d)"),
                                              x_all[:, bass.ds(pair * LANES + lane, 1), :]
                                              .rearrange("p a d -> p (a d)"))
                        nc.gpsimd.tensor_copy(cT[lane][:], cT_all[:, bass.ds(pair * LANES + lane, 1), :]
                                              .rearrange("p a d -> p (a d)")).then_inc(x_copied[lane], 1)
                        pool.wait_ge(x_copied[lane], 1)
                        for block_, bias in ((SELF0, "bo0"), (CROSS0, "box0"), (CROSS1, "box1")):
                            if block_ > SELF0:
                                pool.wait_ge(x_ready[lane], block_)
                            nc.gpsimd.tensor_tensor(
                                xb[lane][:], x[lane][:],
                                row(bias).unsqueeze(1).broadcast_to([P, QT, P]), ALU.add
                            ).then_inc(xb_ready[lane], 1)
                            yield

                    steps = [program(lane) for lane in range(LANES)]
                    for _ in range(3):
                        for s in steps:
                            next(s)

                @block.sync
                def _(sp):
                    for block_ in MHA:
                        for lane in range(LANES):
                            for half in range(2):
                                wait_drained(sp, lane, block_, f"sk{half}")
                                t = slice(2 * half, 2 * half + 2)
                                for g in range(4):
                                    r = slice(32 * g, 32 * g + 32)
                                    sp.dma_start(k_head[lane][r, t, g, :].bitcast(f32), k_sp[lane][r, t, :].bitcast(f32)
                                                 ).then_inc(k_head_ready[lane][half], 16)

                @block.tensor
                def _(pe):
                    mm = nc.tensor.matmul

                    def project(lane, b, what, w, source, rope=False):
                        wait_free(pe, lane, b, what)
                        ps = where(lane, b, what)
                        last = mm(ps[:, 0:SEQ], weight(w), source[:], start=True, stop=True)
                        if rope:
                            last = mm(ps[:, SEQ:2 * SEQ], weight(w + "s"), source[:],
                                      start=True, stop=True)
                        last.then_inc(full(lane, b, what), 1)

                    def project_values(lane, b, w, source):
                        wait_free(pe, lane, b, "v")
                        for k in range(QT):
                            last = mm(where(lane, b, "v")[:, k * P:(k + 1) * P],
                                      source[:, k * P:(k + 1) * P], weight(w), start=True, stop=True)
                        last.then_inc(full(lane, b, "v"), 1)

                    def spread_rows(lane, b, what, i, hi, lo):
                        for half in range(2):
                            wait_free(pe, lane, b, f"{what}{half}")
                            for t in (2 * half, 2 * half + 1):
                                dst = where(lane, b, f"{what}{half}")[:, (t % 2) * SEQ:(t % 2 + 1) * SEQ]
                                mm(dst, spread[:, hi, t, :], qk_hi[lane][:, i, :],
                                   start=True, stop=False)
                                last = mm(dst, spread[:, lo, t, :], qk_lo[lane][:, i, :],
                                          start=False, stop=True)
                            last.then_inc(full(lane, b, f"{what}{half}"), 1)

                    def keys_values(lane, b, wk, wv):
                        pe.wait_ge(ld_p1, 16)
                        pe.wait_ge(x_copied[lane], 1)
                        project(lane, b, "k", wk, cT[lane])
                        project_values(lane, b, wv, cT[lane])
                        yield
                        pe.wait_ge(split_k_ready[lane], MHA[b] + 1)
                        spread_rows(lane, b, "sk", 1, KHI, KLO)
                        yield

                    def queries(lane, b, wq):
                        wait_drained(pe, lane, b - 1, "xT")
                        project(lane, b, "q", wq, xT[lane])
                        yield from empty(1 + SPLIT_LEAD)
                        pe.wait_ge(split_q_ready[lane], MHA[b] + 1)
                        spread_rows(lane, b, "sq", 0, QHI, QLO)
                        yield

                    def self_projections(lane):
                        b = SELF0
                        pe.wait_ge(ld_p0, 48)
                        pe.wait_ge(xT_copied[lane], 1)
                        project(lane, b, "k", "k0", xT[lane], rope=True)
                        yield
                        project(lane, b, "q", "q0", xT[lane], rope=True)
                        yield
                        project_values(lane, b, "v0", xT[lane])
                        yield
                        pe.wait_ge(setup_done, 1)
                        pe.wait_ge(split_k_ready[lane], 1)
                        spread_rows(lane, b, "sk", 1, KHI, KLO)
                        yield
                        pe.wait_ge(split_q_ready[lane], 1)
                        spread_rows(lane, b, "sq", 0, QHI, QLO)
                        yield
                        yield

                    def heads(lane, b):
                        for k in range(HEAD_STEPS):
                            if group_at(k, SHIFT_AT) is not None:
                                t = group_at(k, SHIFT_AT)
                                wait_drained(pe, lane, b, ("max", 4 * t + 3))
                                wait_free(pe, lane, b, ("shift", t))
                                for qt in range(QT):
                                    last = nc.tensor.transpose(
                                        where(lane, b, ("shift", t))[:, qt * P:(qt + 1) * P],
                                        negmax[lane][:, t, qt, :], ident)
                                last.then_inc(full(lane, b, ("shift", t)), 1)
                            if k < HEADS:
                                t, g = k // 4, k % 4
                                if k == 0:
                                    wait_drained(pe, lane, b, "sq0")
                                    pe.wait_ge(k_head_ready[lane][0], 64 * (MHA[b] + 1))
                                if k == 8:
                                    wait_drained(pe, lane, b, "sq1")
                                    pe.wait_ge(k_head_ready[lane][1], 64 * (MHA[b] + 1))
                                wait_free(pe, lane, b, ("max", k))
                                for qt in range(QT):
                                    last = mm(where(lane, b, ("max", k))[:, qt * SEQ:(qt + 1) * SEQ],
                                              q_sp[lane][:, t, qt * P:(qt + 1) * P],
                                              k_head[lane][:, t, g, :],
                                              start=True, stop=True)
                                last.then_inc(full(lane, b, ("max", k)), 1)
                            if 0 <= k - EXP_AT < HEADS:
                                h = k - EXP_AT
                                t, g = h // 4, h % 4
                                if g == 0:
                                    wait_drained(pe, lane, b, ("shift", t))
                                wait_free(pe, lane, b, ("exp", h))
                                for kt in range(QT):
                                    last = mm(where(lane, b, ("exp", h))[:, kt * SEQ:(kt + 1) * SEQ],
                                              k_head[lane][:, t, g, kt * P:(kt + 1) * P],
                                              q_sh[lane][:, t, :],
                                              start=True, stop=True)
                                last.then_inc(full(lane, b, ("exp", h)), 1)
                            if group_at(k, VALUES_AT) is not None:
                                t = group_at(k, VALUES_AT)
                                wait_drained(pe, lane, b, ("exp", 4 * t + 3))
                                wait_free(pe, lane, b, ("pv", t))
                                if t == 0:
                                    wait_drained(pe, lane, b, "v")
                                for kt in range(QT):
                                    for g in range(4):
                                        h = 4 * t + g
                                        last = mm(where(lane, b, ("pv", t))[32 * g:32 * g + 32, 0:SEQ],
                                                  v_aug[lane][:, kt, h, :],
                                                  expo[lane][:, h % ESLOTS, kt * SEQ:(kt + 1) * SEQ],
                                                  start=(kt == 0), stop=(kt == QT - 1))
                                last.then_inc(full(lane, b, ("pv", t)), 1)
                            yield

                    def attention_end(lane, b, wo, side):
                        wait_drained(pe, lane, b, ("pv", GROUPS - 1))
                        for qt in range(QT):
                            wait_free(pe, lane, b, f"back{qt}")
                            for t in range(GROUPS):
                                last = nc.tensor.transpose(
                                    where(lane, b, f"back{qt}")[:, t * P:(t + 1) * P],
                                    ctx_sb[lane][:, t, qt * P:(qt + 1) * P], ident)
                            last.then_inc(full(lane, b, f"back{qt}"), 1)
                        next(side, None)
                        yield
                        wait_free(pe, lane, b, "ctx")
                        for qt in range(QT):
                            wait_drained(pe, lane, b, f"back{qt}")
                            last = nc.tensor.transpose(where(lane, b, "ctx")[:, qt * P:(qt + 1) * P],
                                                       ctx_n[lane][:, qt, :], ident)
                        last.then_inc(full(lane, b, "ctx"), 1)
                        next(side, None)
                        yield
                        wait_drained(pe, lane, b, "ctx")
                        yield from output(lane, b, "out", weight(wo))

                    def output(lane, b, what, w):
                        wait_free(pe, lane, b, what)
                        for qt in range(QT):
                            last = mm(where(lane, b, what)[:, qt * P:(qt + 1) * P],
                                      aT[lane][:, qt * P:(qt + 1) * P], w, start=True, stop=True)
                        last.then_inc(full(lane, b, what), 1)
                        yield

                    def transpose_x(lane, b):
                        yield from empty(MOMENTS_LEAD + ROOT_LEAD + 1 + OUTPUT_LEAD)
                        pe.wait_ge(x_ready[lane], b + 1)
                        wait_free(pe, lane, b, "xT")
                        for qt in range(QT):
                            last = nc.tensor.transpose(where(lane, b, "xT")[:, qt * P:(qt + 1) * P],
                                                       x[lane][:, qt, :], ident)
                        last.then_inc(full(lane, b, "xT"), 1)
                        yield

                    def mixture(lane):
                        b = MIX0
                        pe.wait_ge(ld_gate, 16)
                        wait_drained(pe, lane, b - 1, "xT")
                        wait_free(pe, lane, b, "gate")
                        for qt in range(QT):
                            last = mm(where(lane, b, "gate")[:, qt * EXPERTS:(qt + 1) * EXPERTS],
                                      xT[lane][:, qt * P:(qt + 1) * P], gate_w[:, 0, :],
                                      start=True, stop=True)
                        last.then_inc(full(lane, b, "gate"), 1)
                        yield from empty(2 + GATE_LEAD)
                        pe.wait_ge(gatew_ready[lane], 1)
                        wait_free(pe, lane, b, "wT")
                        for qt in range(QT):
                            last = nc.tensor.transpose(
                                where(lane, b, "wT")[0:EXPERTS, qt * P:(qt + 1) * P],
                                g_w[lane][:, qt, :], ident)
                        last.then_inc(full(lane, b, "wT"), 1)
                        yield
                        pe.wait_ge(ld_mix0, 64)
                        wait_drained(pe, lane, b, "wT")
                        wait_free(pe, lane, b, "b2")
                        for qt in range(QT):
                            last = mm(where(lane, b, "b2")[:, qt * P:(qt + 1) * P],
                                      g_wT[lane][:, qt * P:(qt + 1) * P], b2[:],
                                      start=True, stop=True)
                        last.then_inc(full(lane, b, "b2"), 1)
                        yield
                        hidden = expo[lane][:, 0:4, :].rearrange("p a (h n) -> p (a h) n", n=SEQ)
                        side = keys_values(lane, CROSS1, "kx1", "vx1")
                        for n in range(MIX_STEPS):
                            if n < 2 * EXPERTS:
                                e = n // 2
                                wait_free(pe, lane, b, ("up", n))
                                for i in range(2):
                                    f = 2 * (n % 2) + i
                                    last = mm(where(lane, b, ("up", n))[:, i * SEQ:(i + 1) * SEQ],
                                              mix0_w1[:, e, f * P:(f + 1) * P], xT[lane][:],
                                              start=True, stop=True)
                                last.then_inc(full(lane, b, ("up", n)), 1)
                            if n % 2 == 1 and n > 2:
                                e = (n - 3) // 2
                                for m in (2 * e, 2 * e + 1):
                                    wait_drained(pe, lane, b, ("up", m))
                                wait_free(pe, lane, b, ("down", e))
                                for qt in range(QT):
                                    for f in range(FC):
                                        last = mm(where(lane, b, ("down", e))[:, qt * P:(qt + 1) * P],
                                                  hidden[:, (e % 2) * FC + f, qt * P:(qt + 1) * P],
                                                  mix0_w2[:, e, f, :],
                                                  start=(f == 0), stop=(f == FC - 1))
                                last.then_inc(full(lane, b, ("down", e)), 1)
                            if n in SIDE_STEPS:
                                next(side, None)
                            yield

                    def causal(lane):
                        b = CAUSAL1
                        pe.wait_ge(ld_p1, 16)
                        wait_drained(pe, lane, b - 1, "xT")
                        wait_free(pe, lane, b, "g")
                        mm(where(lane, b, "g")[:, 0:SEQ], weight("qk"), xT[lane][:],
                           start=True, stop=True).then_inc(full(lane, b, "g"), 1)
                        yield
                        wait_drained(pe, lane, b, "g")
                        wait_free(pe, lane, b, "score")
                        ps = where(lane, b, "score")
                        mm(ps[:, 0:P], aT[lane][:, 0:P], xT[lane][:, 0:P], start=True, stop=True)
                        mm(ps[:, P:3 * P], aT[lane][:, P:SEQ], xT[lane][:],
                           start=True, stop=True).then_inc(full(lane, b, "score"), 1)
                        yield from empty(2 + PROBS_LEAD)
                        pe.wait_ge(probs_ready[lane], 1)
                        wait_free(pe, lane, b, "pT")
                        for i in range(3):
                            last = nc.tensor.transpose(where(lane, b, "pT")[:, i * P:(i + 1) * P],
                                                       masked[lane][:, i * P:(i + 1) * P], ident)
                        last.then_inc(full(lane, b, "pT"), 1)
                        yield
                        wait_drained(pe, lane, b, "pT")
                        wait_free(pe, lane, b, "ax")
                        pT = expo[lane][:, 0, 0:3 * P]
                        mm(where(lane, b, "ax")[:, 0:SEQ], x[lane][:, 0, :], pT[:, 0:SEQ],
                           start=True, stop=False)
                        mm(where(lane, b, "ax")[:, P:SEQ], x[lane][:, 1, :], pT[:, SEQ:3 * P],
                           start=False, stop=True).then_inc(full(lane, b, "ax"), 1)
                        yield
                        wait_drained(pe, lane, b, "ax")
                        yield from output(lane, b, "out", weight("ov"))

                    def program(lane):
                        yield from self_projections(lane)
                        yield from heads(lane, SELF0)
                        yield from attention_end(lane, SELF0, "o0",
                                                 keys_values(lane, CROSS0, "kx0", "vx0"))
                        yield from transpose_x(lane, SELF0)
                        yield from queries(lane, CROSS0, "qx0")
                        yield from heads(lane, CROSS0)
                        yield from attention_end(lane, CROSS0, "ox0", iter(()))
                        yield from transpose_x(lane, CROSS0)
                        yield from mixture(lane)
                        yield from transpose_x(lane, MIX0)
                        yield from causal(lane)
                        yield from transpose_x(lane, CAUSAL1)
                        yield from queries(lane, CROSS1, "qx1")
                        yield from heads(lane, CROSS1)
                        yield from attention_end(lane, CROSS1, "ox1", iter(()))
                        yield from transpose_x(lane, CROSS1)
                        wait_drained(pe, lane, CROSS1, "xT")
                        wait_free(pe, lane, CROSS1, "route")
                        for qt in range(QT):
                            last = mm(where(lane, CROSS1, "route")[:, qt * EXPERTS:(qt + 1) * EXPERTS],
                                      xT[lane][:, qt * P:(qt + 1) * P], gate_w[:, 1, :],
                                      start=True, stop=True)
                        last.then_inc(full(lane, CROSS1, "route"), 1)
                        yield

                    pe.wait_ge(ld_const, 16)
                    take_turns(*[program(lane) for lane in range(LANES)])

                @block.scalar
                def _(act):
                    activate = nc.scalar.activation

                    def evacuate(lane, b, what, i, bias):
                        wait_filled(act, lane, b, what)
                        activate(qk_hi[lane][:, i, :], where(lane, b, what)[:, 0:SEQ],
                                 ACT.Identity, bias=bias)
                        activate(qk[lane][:, i, :], where(lane, b, what)[:, 0:SEQ],
                                 ACT.Identity, bias=bias).then_inc(free(lane, b, what), 1)

                    def spread_keys(lane, b):
                        for half in range(2):
                            wait_filled(act, lane, b, f"sk{half}")
                            activate(k_sp[lane][:, 2 * half:2 * half + 2, :],
                                     where(lane, b, f"sk{half}")[:].rearrange("p (t n) -> p t n", t=2),
                                     ACT.Identity, bias=const[:, C_KONE:C_KONE + 1]
                                     ).then_inc(free(lane, b, f"sk{half}"), 1)

                    def spread_queries(lane, b):
                        wait_filled(act, lane, b, "sq0")
                        activate(q_sp[lane][:, 0:2, :],
                                 where(lane, b, "sq0")[:].rearrange("p (t n) -> p t n", t=2),
                                 ACT.Copy).then_inc(free(lane, b, "sq0"), 1)

                    def keys_values(lane, b, bk):
                        evacuate(lane, b, "k", 1, bk)
                        yield
                        spread_keys(lane, b)
                        yield

                    def queries(lane, b, bq):
                        evacuate(lane, b, "q", 0, bq)
                        yield from empty(1 + SPLIT_LEAD)
                        spread_queries(lane, b)
                        yield

                    def self_projections(lane):
                        for _ in range(3):
                            yield
                        spread_keys(lane, SELF0)
                        yield
                        spread_queries(lane, SELF0)
                        yield
                        yield

                    def heads(lane, b):
                        scale = float(HD) ** -0.5
                        for k in range(HEAD_STEPS):
                            if 0 <= k - EXP_AT < HEADS:
                                h = k - EXP_AT
                                wait_filled(act, lane, b, ("exp", h))
                                if h >= ESLOTS:
                                    wait_filled(act, lane, b, ("pv", (h - ESLOTS) // 4))
                                activate(expo[lane][:, h % ESLOTS, :], where(lane, b, ("exp", h))[:],
                                         ACT.Exp, scale=scale).then_inc(free(lane, b, ("exp", h)), 1)
                            if group_at(k, VALUES_AT) is not None:
                                t = group_at(k, VALUES_AT)
                                wait_filled(act, lane, b, ("pv", t))
                                activate(ctx_sb[lane][:, t, :], where(lane, b, ("pv", t))[:, 0:SEQ],
                                         ACT.Copy).then_inc(free(lane, b, ("pv", t)), 1)
                            yield

                    def attention_end(lane, b, side):
                        next(side, None)
                        yield
                        wait_filled(act, lane, b, "ctx")
                        activate(aT[lane][:], where(lane, b, "ctx")[:, 0:SEQ],
                                 ACT.Copy).then_inc(free(lane, b, "ctx"), 1)
                        next(side, None)
                        yield
                        yield

                    def normalise(lane, b):
                        yield from empty(MOMENTS_LEAD)
                        act.wait_ge(var_ready[lane], b + 1)
                        activate(r0[lane][:], mv[lane][:, :, 1], ACT.Ln,
                                 bias=const[:, C_EPS:C_EPS + 1]).then_inc(act_own[lane], 1)
                        act.wait_ge(act_own[lane], b + 1)
                        activate(r0[lane][:], r0[lane][:], ACT.Exp,
                                 scale=-0.5).then_inc(rstd0_ready[lane], 1)
                        yield from empty(ROOT_LEAD + 1 + OUTPUT_LEAD)
                        wait_filled(act, lane, b, "xT")
                        activate(xT[lane][:], where(lane, b, "xT")[:, 0:SEQ],
                                 ACT.Copy).then_inc(free(lane, b, "xT"), 1)
                        yield

                    def mixture(lane):
                        b = MIX0
                        yield
                        act.wait_ge(gatemax_ready[lane], 1)
                        for qt in range(QT):
                            last = activate(g_exp[lane][:, qt, :], gate[lane][:, qt, :], ACT.Exp,
                                            bias=small[lane][:, 0, qt:qt + 1])
                        last.then_inc(gateexp_ready[lane], 1)
                        yield from empty(1 + GATE_LEAD)
                        wait_filled(act, lane, b, "wT")
                        activate(g_wT[lane][:], where(lane, b, "wT")[0:EXPERTS, 0:SEQ],
                                 ACT.Copy).then_inc(free(lane, b, "wT"), 1)
                        yield
                        yield
                        hidden = expo[lane][:, 0:4, :].rearrange("p a (h n) -> p (a h) n", n=SEQ)
                        act.wait_ge(ld_mix0, 64)
                        side = keys_values(lane, CROSS1, 0.0)
                        for n in range(MIX_STEPS):
                            if n < 2 * EXPERTS and n % 2 == 0:
                                e = n // 2
                                wait_filled(act, lane, b, ("up", n))
                                if e >= 2:
                                    wait_filled(act, lane, b, ("down", e - 2))
                                for i in range(2):
                                    f = 2 * (n % 2) + i
                                    last = activate(hidden[:, (e % 2) * FC + f, :],
                                                    where(lane, b, ("up", n))[:, i * SEQ:(i + 1) * SEQ],
                                                    ACT.Relu, bias=b1[:, e * FC + f:e * FC + f + 1])
                                last.then_inc(free(lane, b, ("up", n)), 1)
                            if n in SIDE_STEPS:
                                next(side, None)
                            yield

                    def causal(lane):
                        b = CAUSAL1
                        wait_filled(act, lane, b, "g")
                        activate(aT[lane][:], where(lane, b, "g")[:, 0:SEQ],
                                 ACT.Copy).then_inc(free(lane, b, "g"), 1)
                        yield
                        yield
                        act.wait_ge(rowmax_ready[lane], 1)
                        for qt, (lo, hi) in enumerate(((0, P), (P, 3 * P))):
                            last = activate(masked[lane][:, lo:hi], masked[lane][:, lo:hi], ACT.Exp,
                                            scale=float(P) ** -0.5, bias=small[lane][:, 1, qt:qt + 1],
                                            accum_out=small[lane][:, 2, qt:qt + 1])
                        last.then_inc(probs_ready[lane], 1)
                        yield from empty(1 + PROBS_LEAD)
                        wait_filled(act, lane, b, "pT")
                        activate(expo[lane][:, 0, 0:3 * P], where(lane, b, "pT")[:, 0:3 * P],
                                 ACT.Copy).then_inc(free(lane, b, "pT"), 1)
                        yield
                        wait_filled(act, lane, b, "ax")
                        activate(aT[lane][:], where(lane, b, "ax")[:, 0:SEQ],
                                 ACT.Copy).then_inc(free(lane, b, "ax"), 1)
                        yield
                        yield

                    def program(lane):
                        yield from self_projections(lane)
                        yield from heads(lane, SELF0)
                        yield from attention_end(lane, SELF0, keys_values(lane, CROSS0, col("bkx0")))
                        yield from normalise(lane, SELF0)
                        yield from queries(lane, CROSS0, col("bqx0"))
                        yield from heads(lane, CROSS0)
                        yield from attention_end(lane, CROSS0, iter(()))
                        yield from normalise(lane, CROSS0)
                        yield from mixture(lane)
                        yield from normalise(lane, MIX0)
                        yield from causal(lane)
                        yield from normalise(lane, CAUSAL1)
                        yield from queries(lane, CROSS1, 0.0)
                        yield from heads(lane, CROSS1)
                        yield from attention_end(lane, CROSS1, iter(()))
                        yield from normalise(lane, CROSS1)
                        yield

                    act.wait_ge(ld_x, 48)
                    act.wait_ge(ld_const, 16)
                    act.wait_ge(ld_p0, 48)
                    for lane in range(LANES):
                        activate(xT[lane][:], xT_all[:, bass.ds(pair * LANES + lane, 1), :]
                                 .rearrange("p a d -> p (a d)"), ACT.Copy).then_inc(xT_copied[lane], 1)
                    take_turns(*[program(lane) for lane in range(LANES)])

                @block.vector
                def _(dve):
                    own = [0]

                    def link(instruction):
                        own[0] += 1
                        instruction.then_inc(dve_own, 1)
                        dve.wait_ge(dve_own, own[0])

                    V = nc.vector

                    def values(lane, b, bv):
                        wait_filled(dve, lane, b, "v")
                        for k in range(QT):
                            src = where(lane, b, "v")[:, k * P:(k + 1) * P].rearrange(
                                "p (h d) -> p h d", d=HD)
                            dst = v_aug[lane][:, k, :, 0:HD]
                            if bv is None:
                                last = V.tensor_copy(dst, src)
                            else:
                                last = V.tensor_tensor(dst, src, row(bv).rearrange(
                                    "p (h d) -> p h d", d=HD), ALU.add)
                        last.then_inc(free(lane, b, "v"), 1)

                    def low_part(lane, i, ready):
                        V.tensor_tensor(qk_lo[lane][:, i, :], qk[lane][:, i, :],
                                        qk_hi[lane][:, i, :].bitcast(f32), ALU.subtract
                                        ).then_inc(ready[lane], 1)

                    def spread_queries(lane, b):
                        wait_filled(dve, lane, b, "sq1")
                        V.tensor_copy(q_sp[lane][:, 2:4, :],
                                      where(lane, b, "sq1")[:].rearrange("p (t n) -> p t n", t=2)
                                      ).then_inc(free(lane, b, "sq1"), 1)

                    def keys_values(lane, b, bv):
                        wait_drained(dve, lane, b, "k")
                        low_part(lane, 1, split_k_ready)
                        values(lane, b, bv)
                        yield
                        yield

                    def queries(lane, b):
                        wait_drained(dve, lane, b, "q")
                        low_part(lane, 0, split_q_ready)
                        yield from empty(1 + SPLIT_LEAD)
                        spread_queries(lane, b)
                        yield

                    def self_projections(lane):
                        b = SELF0
                        t0 = ctx_sb[lane][:, 0:2, :]
                        t1 = ctx_sb[lane][:, 2:4, :]

                        def rotate(i, what, c0, c1):
                            wait_filled(dve, lane, b, what)
                            ps = where(lane, b, what)
                            V.scalar_tensor_tensor(t0[:, i, :], ps[:, 0:SEQ], col(c0),
                                                   const[:, C_COS:C_COS + SEQ], ALU.add, ALU.mult)
                            V.scalar_tensor_tensor(t1[:, i, :], ps[:, SEQ:2 * SEQ], col(c1),
                                                   const[:, C_SIN:C_SIN + SEQ], ALU.add, ALU.mult
                                                   ).then_inc(free(lane, b, what), 1)

                        def split(i, what, ready):
                            wait_drained(dve, lane, b, what)
                            link(V.tensor_tensor(qk[lane][:, i, :], t0[:, i, :], t1[:, i, :], ALU.add))
                            link(V.tensor_copy(qk_hi[lane][:, i, :], qk[lane][:, i, :]))
                            low_part(lane, i, ready)

                        rotate(1, "k", "bk0", "bk0s")
                        yield
                        split(1, "k", split_k_ready)
                        rotate(0, "q", "bq0", "bq0s")
                        yield
                        split(0, "q", split_q_ready)
                        values(lane, b, "bv0")
                        yield
                        yield
                        spread_queries(lane, b)
                        yield
                        yield

                    def heads(lane, b):
                        for k in range(HEAD_STEPS):
                            if group_at(k, SHIFT_AT) is not None:
                                t = group_at(k, SHIFT_AT)
                                if t == 0:
                                    wait_drained(dve, lane, b, "sq0")
                                wait_filled(dve, lane, b, ("shift", t))
                                V.tensor_tensor(q_sh[lane][:, t, :], q_sp[lane][:, t, :].bitcast(f32),
                                                where(lane, b, ("shift", t))[:, 0:SEQ], ALU.add
                                                ).then_inc(free(lane, b, ("shift", t)), 1)
                            if k < HEADS:
                                wait_filled(dve, lane, b, ("max", k))
                                V.tensor_reduce(negmax[lane][:, k // 4, :, 32 * (k % 4)],
                                                where(lane, b, ("max", k))[:].rearrange(
                                                    "p (q n) -> p q n", q=QT),
                                                AX.X, ALU.max, negate=True
                                                ).then_inc(free(lane, b, ("max", k)), 1)
                            yield

                    def attention_end(lane, b, side):
                        for qt in range(QT):
                            wait_filled(dve, lane, b, f"back{qt}")
                            rows_of = where(lane, b, f"back{qt}")[:].rearrange("p (h r) -> p h r", r=32)
                            link(V.reciprocal(recip[lane][:, qt, :], rows_of[:, :, HD]))
                            V.tensor_tensor(ctx_n[lane][:, qt, :].rearrange("p (h d) -> p h d", d=HD),
                                            rows_of[:, :, 0:HD],
                                            recip[lane][:, qt, :].unsqueeze(2).broadcast_to([P, HEADS, HD]),
                                            ALU.mult).then_inc(free(lane, b, f"back{qt}"), 1)
                        next(side, None)
                        yield
                        next(side, None)
                        yield
                        wait_filled(dve, lane, b, "out")
                        dve.wait_ge(xb_ready[lane], MHA[b] + 1)
                        V.tensor_tensor(y[lane][:].rearrange("p a d -> p (a d)"),
                                        where(lane, b, "out")[:, 0:SEQ],
                                        xb[lane][:].rearrange("p a d -> p (a d)"), ALU.add
                                        ).then_inc(free(lane, b, "out"), 1)
                        wait_drained(dve, lane, b, "out")
                        moments(lane)
                        yield

                    def moments(lane):
                        for qt in range(QT):
                            last = V.bn_stats(stats[lane][:, qt, :], y[lane][:, qt, :])
                        link(last)
                        for qt in range(QT):
                            last = V.bn_aggr(mv[lane][:, qt, :], stats[lane][:, qt, :])
                        last.then_inc(var_ready[lane], 1)

                    def normalise(lane, b):
                        yield from empty(MOMENTS_LEAD + ROOT_LEAD)
                        dve.wait_ge(rstd0_ready[lane], b + 1)
                        r, (n0, n1, n2) = r0[lane][:], (newton[lane][:, i, :] for i in range(3))
                        link(V.tensor_tensor(n0, r, r, ALU.mult))
                        link(V.scalar_tensor_tensor(n1, mv[lane][:, :, 1], const[:, C_EPS:C_EPS + 1],
                                                    n0, ALU.add, ALU.mult))
                        link(V.tensor_scalar(n0, n1, -0.5, 1.5, ALU.mult, ALU.add))
                        link(V.tensor_tensor(n2, n0, r, ALU.mult))
                        for qt in range(QT):
                            last = V.tensor_scalar(x[lane][:, qt, :], y[lane][:, qt, :],
                                                   mv[lane][:, qt, 0:1], newton[lane][:, 2, qt:qt + 1],
                                                   ALU.subtract, ALU.mult)
                        last.then_inc(x_ready[lane], 1)
                        yield from empty(1 + OUTPUT_LEAD + 1)

                    def mixture(lane):
                        b = MIX0
                        wait_filled(dve, lane, b, "gate")
                        V.tensor_copy(gate[lane][:].rearrange("p a e -> p (a e)"),
                                      where(lane, b, "gate")[:, 0:QT * EXPERTS]
                                      ).then_inc(free(lane, b, "gate"), 1)
                        wait_drained(dve, lane, b, "gate")
                        for qt in range(QT):
                            last = V.max(top[lane][:, qt, :], gate[lane][:, qt, :])
                        link(last)
                        V.tensor_scalar(small[lane][:, 0, :], top[lane][:, :, 0], -1.0, None,
                                        ALU.mult).then_inc(gatemax_ready[lane], 1)
                        yield
                        dve.wait_ge(gateexp_ready[lane], 1)
                        for qt in range(QT):
                            last = V.scalar_tensor_tensor(g_sel[lane][:, qt, :], gate[lane][:, qt, :],
                                                          top[lane][:, qt, 1:2], g_exp[lane][:, qt, :],
                                                          ALU.is_ge, ALU.mult)
                        link(last)
                        link(V.tensor_reduce(small[lane][:, 4, :], g_sel[lane][:], AX.X, ALU.add))
                        link(V.reciprocal(small[lane][:, 5, :], small[lane][:, 4, :]))
                        for qt in range(QT):
                            last = V.tensor_scalar(g_w[lane][:, qt, :], g_sel[lane][:, qt, :],
                                                   small[lane][:, 5, qt:qt + 1], 1.0 / EXPERTS,
                                                   ALU.mult, ALU.mult)
                        last.then_inc(gatew_ready[lane], 1)
                        yield from empty(GATE_LEAD)
                        yield
                        yield
                        wait_filled(dve, lane, b, "b2")
                        V.tensor_tensor(y[lane][:].rearrange("p a d -> p (a d)"),
                                        where(lane, b, "b2")[:, 0:SEQ],
                                        x[lane][:].rearrange("p a d -> p (a d)"), ALU.add
                                        ).then_inc(free(lane, b, "b2"), 1)
                        yield
                        hidden = expo[lane][:, 0:4, :].rearrange("p a (h n) -> p (a h) n", n=SEQ)
                        dve.wait_ge(gatew_ready[lane], 1)
                        wait_drained(dve, lane, b, "b2")
                        side = keys_values(lane, CROSS1, None)
                        for n in range(MIX_STEPS):
                            if n < 2 * EXPERTS and n % 2 == 1:
                                e = n // 2
                                wait_filled(dve, lane, b, ("up", n))
                                if e >= 2:
                                    wait_filled(dve, lane, b, ("down", e - 2))
                                for i in range(2):
                                    f = 2 * (n % 2) + i
                                    last = V.tensor_scalar(hidden[:, (e % 2) * FC + f, :],
                                                           where(lane, b, ("up", n))[:, i * SEQ:(i + 1) * SEQ],
                                                           b1[:, e * FC + f:e * FC + f + 1], 0.0,
                                                           ALU.add, ALU.max)
                                last.then_inc(free(lane, b, ("up", n)), 1)
                            if n % 2 == 1 and n > 2:
                                e = (n - 3) // 2
                                wait_filled(dve, lane, b, ("down", e))
                                if e > 0:
                                    wait_drained(dve, lane, b, ("down", e - 1))
                                for qt in range(QT):
                                    last = V.scalar_tensor_tensor(
                                        y[lane][:, qt, :], where(lane, b, ("down", e))[:, qt * P:(qt + 1) * P],
                                        g_w[lane][:, qt, e:e + 1], y[lane][:, qt, :], ALU.mult, ALU.add)
                                last.then_inc(free(lane, b, ("down", e)), 1)
                            if n == 2 * EXPERTS + 1:
                                wait_drained(dve, lane, b, ("down", EXPERTS - 1))
                                moments(lane)
                            if n in SIDE_STEPS:
                                next(side, None)
                            yield

                    def causal(lane):
                        b = CAUSAL1
                        yield
                        wait_filled(dve, lane, b, "score")
                        V.tensor_tensor(masked[lane][:], where(lane, b, "score")[:, 0:3 * P],
                                        const[:, C_MASK:C_MASK + 3 * P], ALU.add
                                        ).then_inc(free(lane, b, "score"), 1)
                        wait_drained(dve, lane, b, "score")
                        V.tensor_reduce(small[lane][:, 3, 0:1], masked[lane][:, 0:P], AX.X, ALU.max,
                                        negate=True)
                        link(V.tensor_reduce(small[lane][:, 3, 1:2], masked[lane][:, P:3 * P], AX.X,
                                             ALU.max, negate=True))
                        V.tensor_scalar(small[lane][:, 1, :], small[lane][:, 3, :], float(P) ** -0.5,
                                        None, ALU.mult).then_inc(rowmax_ready[lane], 1)
                        yield
                        dve.wait_ge(probs_ready[lane], 1)
                        link(V.reciprocal(small[lane][:, 4, :], small[lane][:, 2, :]))
                        yield from empty(PROBS_LEAD)
                        yield
                        yield
                        yield
                        wait_filled(dve, lane, b, "out")
                        for qt in range(QT):
                            last = V.scalar_tensor_tensor(
                                y[lane][:, qt, :], where(lane, b, "out")[:, qt * P:(qt + 1) * P],
                                small[lane][:, 4, qt:qt + 1], x[lane][:, qt, :], ALU.mult, ALU.add)
                        last.then_inc(free(lane, b, "out"), 1)
                        wait_drained(dve, lane, b, "out")
                        moments(lane)
                        yield

                    def program(lane):
                        yield from self_projections(lane)
                        yield from heads(lane, SELF0)
                        yield from attention_end(lane, SELF0, keys_values(lane, CROSS0, "bvx0"))
                        yield from normalise(lane, SELF0)
                        yield from queries(lane, CROSS0)
                        yield from heads(lane, CROSS0)
                        yield from attention_end(lane, CROSS0, iter(()))
                        yield from normalise(lane, CROSS0)
                        yield from mixture(lane)
                        yield from normalise(lane, MIX0)
                        yield from causal(lane)
                        yield from normalise(lane, CAUSAL1)
                        yield from queries(lane, CROSS1)
                        yield from heads(lane, CROSS1)
                        yield from attention_end(lane, CROSS1, iter(()))
                        yield from normalise(lane, CROSS1)
                        dve.wait_ge(x_ready[lane], CROSS1 + 1)
                        V.tensor_copy(x_all[:, bass.ds(pair * LANES + lane, 1), :]
                                      .rearrange("p a d -> p (a d)"),
                                      x[lane][:].rearrange("p a d -> p (a d)"))
                        wait_filled(dve, lane, CROSS1, "route")
                        V.tensor_copy(logit_all[:, bass.ds(pair * LANES + lane, 1), :]
                                      .rearrange("p a d -> p (a d)"),
                                      where(lane, CROSS1, "route")[:, 0:QT * EXPERTS]
                                      ).then_inc(free(lane, CROSS1, "route"), 1)
                        yield

                    dve.wait_ge(ld_p0, 48)
                    dve.wait_ge(ld_const, 16)
                    for lane in range(LANES):
                        dve.wait_ge(x_copied[lane], 1)
                    take_turns(*[program(lane) for lane in range(LANES)])

            with nc.Block() as block:
                @block.sync
                def _(sp):
                    sp.sem_clear(cleared)

        last_mixture(nc, stack, ins, out, dict(
            const=const, x_all=x_all, logit_all=logit_all, w1=mix0_w1, w2=mix0_w2, banks=bank,
            expo=expo, ctx_sb=ctx_sb, ident=ident))


def last_mixture(nc, stack, ins, out, t):
    f32, i32 = mybir.dt.float32, mybir.dt.int32
    u32 = mybir.dt.uint32
    ALU, ACT, AX = mybir.AluOpType, mybir.ActivationFunctionType, mybir.AxisListType
    TE = TILES * EXPERTS

    def sb(name, shape, dt=f32):
        return stack.enter_context(nc.sbuf_tensor(name, shape, dt))

    def sem(name):
        return stack.enter_context(nc.semaphore(name))

    const, x_all, logit_all, ident = t["const"], t["x_all"], t["logit_all"], t["ident"]
    w1, w2 = t["w1"], t["w2"]
    x8 = x_all[:].rearrange("p b (a d) -> p (b a) d", d=P)
    lg = logit_all[:].rearrange("p b (a e) -> p (b a) e", e=EXPERTS)
    r = sb("r_work", [P, 6, TILES, EXPERTS])
    c8 = sb("c_work", [P, 10, TILES])
    slot = sb("slot", [P, TILES], i32)
    xe = t["expo"][0][:].rearrange("p a b -> p (a b)")[:, 0:EXPERTS * P].rearrange("p (e d) -> p e d", d=P)
    xeT = t["expo"][0][:].rearrange("p a b -> p (a b)")[:, 1024:2048].rearrange("p (e d) -> p e d", d=P)
    ye = t["expo"][0][:].rearrange("p a b -> p (a b)")[:, 2048:3072].rearrange("p (e d) -> p e d", d=P)
    hid = t["expo"][1][:].rearrange("p a b -> p (a b)")[:, 0:1024].rearrange("p (s f n) -> p s f n", s=2, f=FC)
    yg = t["expo"][1][:].rearrange("p a b -> p (a b)")[:, 1024:2048].rearrange("p (a d) -> p a d", d=P)
    yo = t["expo"][1][:].rearrange("p a b -> p (a b)")[:, 2048:3072].rearrange("p (a d) -> p a d", d=P)
    stats = sb("stats_all", [P, TILES, 6])
    mv = sb("mv_all", [P, TILES, 2])
    rs = sb("rs_all", [P, 4, TILES])
    xe_dram = nc.dram_tensor("xe_scratch", (EXPERTS * CAP, P), f32, kind="Internal").ap()
    ye_dram = nc.dram_tensor("ye_scratch", (EXPERTS * CAP, P), f32, kind="Internal").ap()
    ps = [b for pool in POOLS for b in t["banks"][pool]]

    xe_zeroed, zero_ready, shifted, exp_ready, onehot_ready, rank_filled, slot_ready = (
        sem("xe_zeroed"), sem("zero_ready"), sem("shifted"), sem("exp_ready"), sem("onehot_ready"),
        sem("rank_filled"), sem("slot_ready"))
    scattered, xe_loaded, xeT_filled, xeT_ready = (
        sem("scattered"), sem("xe_loaded"), sem("xeT_filled"), sem("xeT_ready"))
    up_filled, hid_act, down_filled, ye_ready, ye_stored = (
        sem("up_filled"), sem("hid_ready"), sem("down_filled"), sem("ye_ready"), sem("ye_stored"))
    gathered, var_ready, rstd0_ready, y_ready, stored, yg_zeroed, prefix_ready, ln_own = (
        sem("gathered"), sem("var_all_ready"), sem("rstd0_all_ready"), sem("y_ready"), sem("stored"),
        sem("yg_zeroed"), sem("prefix_ready"), sem("ln_own"))
    own_sem = sem("dve_last_own")
    weights_loaded = [sem(f"weights_loaded{i}") for i in range(EXPERTS // 2)]
    base = const[:, C_BASE:C_BASE + TE].rearrange("p (a e) -> p a e", e=EXPERTS)
    order = const[:, C_FIRST:C_FIRST + TE].rearrange("p (a e) -> p a e", e=EXPERTS)

    with nc.Block() as block:
        @block.vector
        def _(dve):
            V = nc.vector
            own = [0]

            def link(instruction):
                own[0] += 1
                instruction.then_inc(own_sem, 1)
                dve.wait_ge(own_sem, own[0])

            def wide(ap):
                return ap.unsqueeze(2).broadcast_to([P, TILES, EXPERTS])

            V.memset(xe.bitcast(u32), 0).then_inc(zero_ready, 1)
            mx, total, p_tok, rank, keep, dest, weight = (c8[:, i, :] for i in range(7))
            link(V.tensor_reduce(mx, lg, AX.X, ALU.max))
            V.tensor_tensor(r[:, 0], lg, wide(mx), ALU.subtract).then_inc(shifted, 1)
            link(V.tensor_tensor(r[:, 1], lg, wide(mx), ALU.is_ge))
            link(V.tensor_tensor(r[:, 2], r[:, 1], order, ALU.mult))
            link(V.tensor_reduce(c8[:, 7, :], r[:, 2], AX.X, ALU.max))
            link(V.tensor_tensor(r[:, 1], r[:, 2], wide(c8[:, 7, :]), ALU.is_equal))
            link(V.memset(r[:, 3, 0, :], 0.0))
            for i in range(1, TILES):
                link(V.tensor_tensor(r[:, 3, i, :], r[:, 3, i - 1, :], r[:, 1, i - 1, :], ALU.add))
            V.memset(yg.bitcast(u32), 0).then_inc(yg_zeroed, 1)
            dve.wait_ge(exp_ready, 1)
            link(V.tensor_reduce(total, r[:, 4], AX.X, ALU.add))
            link(V.reciprocal(p_tok, total))
            dve.wait_ge(rank_filled, 1)
            ranks = ps[0][:, 0:TE].rearrange("p (a e) -> p a e", e=EXPERTS)
            link(V.tensor_tensor(r[:, 0], ranks, r[:, 1], ALU.mult))
            link(V.tensor_tensor(r[:, 2], base, r[:, 1], ALU.mult))
            link(V.tensor_reduce(rank, r[:, 0], AX.X, ALU.add))
            link(V.tensor_reduce(dest, r[:, 2], AX.X, ALU.add))
            link(V.tensor_scalar(keep, rank, float(CAP), None, ALU.is_lt))
            link(V.tensor_tensor(c8[:, 8, :], rank, dest, ALU.add))
            link(V.tensor_scalar(c8[:, 9, :], keep, -float(4 * TOKENS), float(4 * TOKENS),
                                 ALU.mult, ALU.add))
            V.tensor_tensor(slot[:], c8[:, 8, :], c8[:, 9, :], ALU.add).then_inc(slot_ready, 1)
            link(V.tensor_tensor(weight, p_tok, keep, ALU.mult))
            for half in range(2):
                dve.wait_ge(xeT_filled, half + 1)
                V.tensor_copy(xeT[:, 4 * half:4 * half + 4, :].rearrange("p a b -> p (a b)"),
                              ps[1 + half][:]).then_inc(xeT_ready, 1)
            for e in range(EXPERTS):
                dve.wait_ge(down_filled, e + 1)
                V.tensor_copy(ye[:, e, :], ps[5 + e % 2][:, 0:P]).then_inc(ye_ready, 1)
            dve.wait_ge(gathered, 16 * TILES)
            for i in range(TILES):
                last = V.scalar_tensor_tensor(yo[:, i, :], yg[:, i, :], weight[:, i:i + 1],
                                              x8[:, i, :], ALU.mult, ALU.add)
            link(last)
            for i in range(TILES):
                last = V.bn_stats(stats[:, i, :], yo[:, i, :])
            link(last)
            for i in range(TILES):
                last = V.bn_aggr(mv[:, i, :], stats[:, i, :])
            last.then_inc(var_ready, 1)
            dve.wait_ge(rstd0_ready, 1)
            link(V.tensor_tensor(rs[:, 1], rs[:, 0], rs[:, 0], ALU.mult))
            link(V.scalar_tensor_tensor(rs[:, 2], mv[:, :, 1], const[:, C_EPS:C_EPS + 1], rs[:, 1],
                                        ALU.add, ALU.mult))
            link(V.tensor_scalar(rs[:, 1], rs[:, 2], -0.5, 1.5, ALU.mult, ALU.add))
            link(V.tensor_tensor(rs[:, 3], rs[:, 1], rs[:, 0], ALU.mult))
            for i in range(TILES):
                V.tensor_scalar(yg[:, i, :], yo[:, i, :], mv[:, i, 0:1], rs[:, 3, i:i + 1],
                                ALU.subtract, ALU.mult).then_inc(y_ready, 1)

        @block.scalar
        def _(act):
            act.wait_ge(shifted, 1)
            nc.scalar.activation(r[:, 4], r[:, 0], ACT.Exp).then_inc(exp_ready, 1)
            for e in range(EXPERTS):
                act.wait_ge(up_filled, e + 1)
                if e >= 2:
                    act.wait_ge(down_filled, e - 1)
                nc.scalar.activation(hid[:, e % 2].rearrange("p f n -> p (f n)"), ps[3 + e % 2][:],
                                     ACT.Relu).then_inc(hid_act, 1)
            act.wait_ge(var_ready, 1)
            nc.scalar.activation(rs[:, 0], mv[:, :, 1], ACT.Ln,
                                 bias=const[:, C_EPS:C_EPS + 1]).then_inc(ln_own, 1)
            act.wait_ge(ln_own, 1)
            nc.scalar.activation(rs[:, 0], rs[:, 0], ACT.Exp, scale=-0.5).then_inc(rstd0_ready, 1)

        @block.tensor
        def _(pe):
            mm = nc.tensor.matmul
            pe.wait_ge(own_sem, 6 + TILES - 1)
            flat = lambda i: r[:, i].rearrange("p a e -> p (a e)")
            mm(ps[0][:, 0:TE], const[:, C_TRI:C_TRI + P], flat(1), start=True, stop=False)
            mm(ps[0][:, 0:TE], const[:, C_ONES:C_ONES + P], flat(3), start=False,
               stop=True).then_inc(rank_filled, 1)
            pe.wait_ge(xe_loaded, 16)
            for half in range(2):
                for e in range(4 * half, 4 * half + 4):
                    last = nc.tensor.transpose(ps[1 + half][:, (e % 4) * P:(e % 4 + 1) * P],
                                               xe[:, e, :], ident)
                last.then_inc(xeT_filled, 1)
            for e in range(EXPERTS + 1):
                if e < EXPERTS:
                    pe.wait_ge(weights_loaded[e // 2], 64)
                    pe.wait_ge(xeT_ready, e // 4 + 1)
                    if e >= 2:
                        pe.wait_ge(hid_act, e - 1)
                    for f in range(FC):
                        last = mm(ps[3 + e % 2][:, f * P:(f + 1) * P], w1[:, e, f * P:(f + 1) * P],
                                  xeT[:, e, :], start=True, stop=True)
                    last.then_inc(up_filled, 1)
                if e > 0:
                    d = e - 1
                    pe.wait_ge(hid_act, d + 1)
                    if d >= 2:
                        pe.wait_ge(ye_ready, d - 1)
                    for f in range(FC):
                        last = mm(ps[5 + d % 2][:, 0:P], hid[:, d % 2, f, :], w2[:, d, f, :],
                                  start=(f == 0), stop=(f == FC - 1))
                    last.then_inc(down_filled, 1)

        @block.gpsimd
        def _(pool):
            pool.wait_ge(slot_ready, 1)
            pool.wait_ge(xe_zeroed, 16)
            for i in range(TILES):
                nc.gpsimd.indirect_dma_start(
                    xe_dram, bass.IndirectOffsetOnAxis(slot[:, i:i + 1].bitcast(u32), 0),
                    x8[:, i, :], None, bounds_check=TOKENS - 1, oob_is_err=False
                ).then_inc(scattered, 16)
            pool.wait_ge(ye_stored, 16 * EXPERTS)
            pool.wait_ge(yg_zeroed, 1)
            for i in range(TILES):
                nc.gpsimd.indirect_dma_start(
                    yg[:, i, :], None, ye_dram,
                    bass.IndirectOffsetOnAxis(slot[:, i:i + 1].bitcast(u32), 0),
                    bounds_check=TOKENS - 1, oob_is_err=False).then_inc(gathered, 16)

        @block.sync
        def _(sp):
            def zero_rows():
                sp.wait_ge(zero_ready, 1)
                sp.dma_start(xe_dram.rearrange("(e p) d -> p e d", p=P), xe).then_inc(xe_zeroed, 16)

            def load_rows():
                sp.wait_ge(xe_zeroed, 16)
                sp.wait_ge(scattered, 16 * TILES)
                sp.dma_start(xe, xe_dram.rearrange("(e p) d -> p e d", p=P)).then_inc(xe_loaded, 16)

            def store_rows():
                for e in range(EXPERTS):
                    sp.wait_ge(ye_ready, e + 1)
                    sp.dma_start(ye_dram[e * CAP:(e + 1) * CAP, :], ye[:, e, :]).then_inc(ye_stored, 16)

            for e in range(0, EXPERTS, 2):
                for i in (e, e + 1):
                    sp.dma_start(w1[:, i, :], ins["mix1_w1"][:, i, :]).then_inc(weights_loaded[e // 2], 16)
                    sp.dma_start(w2[:, i, :, :], ins["mix1_w2"][:, i, :, :]).then_inc(weights_loaded[e // 2], 16)
                if e > 0:
                    continue
                zero_rows()
            load_rows()
            store_rows()
            for half in range(2):
                n = TILES // 2
                sp.wait_ge(y_ready, n * (half + 1))
                sp.dma_start(out.rearrange("b (a p) d -> p (b a) d", p=P)[:, n * half:n * (half + 1), :],
                             yg[:, n * half:n * (half + 1), :]).then_inc(stored, 16)
            sp.wait_ge(stored, 32)


def kernel(**inputs):
    import concourse.bacc as _bacc
    from concourse.bass_utils import run_bass_kernel_spmd as _run

    a = {k: np.asarray(v) for k, v in inputs.items()}
    swap = np.arange(P) ^ 1

    def by_token(v):
        return v.reshape(TILES, P, P).transpose(1, 0, 2).reshape(P, BATCH, SEQ)

    def by_width(v):
        return v.reshape(BATCH, SEQ, P).transpose(2, 0, 1)

    wq, wk = a["L0_attn_wq"].T, a["L0_attn_wk"].T
    mats = [wq, wq[:, swap], wk, wk[:, swap], a["L0_attn_wv"].T, a["L0_attn_wo"].T,
            a["L0_xattn_Wq"].T, a["L0_xattn_Wk"].T, a["L0_xattn_Wv"].T, a["L0_xattn_Wo"].T,
            a["L1_attn_qk"], a["L1_attn_ov"],
            a["L1_xattn_Wq"].T, a["L1_xattn_Wk"].T, a["L1_xattn_Wv"].T, a["L1_xattn_Wo"].T]
    bq, bk = a["L0_attn_bq"], a["L0_attn_bk"]
    const, spread = constants()
    arrays = {
        "x": by_token(a["x"]), "xT": by_width(a["x"]), "cT": by_width(a["ctx_1024"]),
        "proj": np.stack(mats, 1),
        "cols": np.stack([bq, bq[swap], bk, bk[swap], a["L0_xattn_bq"], a["L0_xattn_bk"]], 1),
        "rows": np.concatenate([a["L0_attn_bv"], a["L0_attn_bo"], a["L0_xattn_bv"],
                                a["L0_xattn_bo"], a["L1_xattn_bo"]]),
        "gates": np.stack([a["L0_ffn_W_gate"], a["L1_ffn_Wr"]], 1),
        "b1": a["L0_ffn_b1"].reshape(EXPERTS * FC, P).T, "b2": a["L0_ffn_b2"],
        "mix0_w1": a["L0_ffn_W1"].transpose(1, 0, 2),
        "mix0_w2": a["L0_ffn_W2"].reshape(EXPERTS, FC, P, P).transpose(2, 0, 1, 3),
        "mix1_w1": a["L1_ffn_W1"].transpose(1, 0, 2),
        "mix1_w2": a["L1_ffn_W2"].reshape(EXPERTS, FC, P, P).transpose(2, 0, 1, 3),
        "const": const, "spread": spread,
    }
    arrays = {k: np.ascontiguousarray(v) for k, v in arrays.items()}
    nc = _bacc.Bacc("TRN2", target_bir_lowering=False, num_devices=1)
    ins = {k: nc.dram_tensor(f"in_{k}", v.shape, mybir.dt.from_np(v.dtype), kind="ExternalInput").ap()
           for k, v in arrays.items()}
    ins["spread"] = ins["spread"].rearrange("p (k t c) -> p k t c", k=4, t=GROUPS)
    out = nc.dram_tensor("out", (BATCH, SEQ, P), mybir.dt.float32, kind="ExternalOutput").ap()
    decoder(nc, ins, out)
    r = _run(nc, [{f"in_{k}": v for k, v in arrays.items()}], core_ids=[0])
    return r.results[0]["out"]
```

```python
import numpy as np
import concourse.bass as bass
from concourse import mybir
from contextlib import ExitStack
from itertools import chain

P = 128
BATCH, SEQ = 4, 256
TOKENS = BATCH * SEQ
TILES = TOKENS // P
QT = SEQ // P
HEADS, HD = 16, 8
GROUPS = HEADS // 4
EXPERTS, HID = 8, 512
FC = HID // P
CAP = TOKENS // EXPERTS
LANES = 2
EPS = 1e-5
ESLOTS = 6
MASKED = -3.0e38

C_ID, C_TRI, C_ONES, C_MASK, C_COS, C_SIN = 0, 128, 256, 384, 768, 1024
C_KONE, C_EPS, C_ORDER, C_BASE, C_TOKEN, C_END = 1280, 1281, 1282, 1298, 1314, 1322
ROW = P + 2
NOWHERE = 4 * TOKENS
QHI, QLO, KHI, KLO = range(4)
W_NAMES = ["q0", "q0s", "k0", "k0s", "v0", "o0", "qx0", "kx0", "vx0", "ox0",
           "qk", "ov", "qx1", "kx1", "vx1", "ox1"]
COL_NAMES = ["bq0", "bq0s", "bk0", "bk0s", "bqx0", "bkx0"]
ROW_NAMES = ["bv0", "bo0", "bvx0", "box0", "box1"]

SELF0, CROSS0, MIX0, CAUSAL1, CROSS1, ROUTE = range(6)
MHA = {SELF0: 0, CROSS0: 1, CROSS1: 2}

LAG = 16
SHIFT_AT = 5
EXP_AT = 7
VALUES_AT = 12
HEAD_STEPS = VALUES_AT + 4 * (GROUPS - 1) + 1
MIX_STEPS = 2 * EXPERTS + 2
MOMENTS_LEAD = 0
ROOT_LEAD = 0
OUTPUT_LEAD = 1
RANK_LEAD = 0
GATE_LEAD = 1
PROBS_LEAD = 0
SPLIT_LEAD = 0


def take_turns(*programs):
    live = list(programs)
    for _ in range(LAG):
        next(live[0])
    while live:
        live = [program for program in live if next(program, live) is None]


def group_at(step, start):
    t, rest = divmod(step - start, 4)
    return t if rest == 0 and 0 <= t < GROUPS else None


def lane_program(program, lane):
    return chain.from_iterable(program(seq) for seq in range(lane, BATCH, LANES))


def relu_on_scalar(n):
    return n % 2 == 0


def empty(steps):
    for _ in range(steps):
        yield


def bank_turns():
    turns, count = {}, {pool: 0 for pool in POOLS}

    def steps(seq):
        def turn(block, what, pool):
            turns[seq, block, what] = (pool, count[pool] % POOLS[pool], count[pool] // POOLS[pool])
            count[pool] += 1

        def keys_values(b):
            turn(b, "k", "M")
            turn(b, "v", "C")
            yield
            for half in range(2):
                turn(b, f"sk{half}", "M")
            yield

        def queries(b):
            turn(b, "q", "M")
            yield from empty(1 + SPLIT_LEAD)
            for half in range(2):
                turn(b, f"sq{half}", "M")
            yield

        def heads(b):
            for k in range(HEAD_STEPS):
                if group_at(k, SHIFT_AT) is not None:
                    turn(b, ("shift", group_at(k, SHIFT_AT)), "M")
                if k < HEADS:
                    turn(b, ("max", k), "S")
                if 0 <= k - EXP_AT < HEADS:
                    turn(b, ("exp", k - EXP_AT), "E")
                if group_at(k, VALUES_AT - 1) is not None:
                    turn(b, ("pv", group_at(k, VALUES_AT - 1)), "C")
                yield

        def attention_end(b, side):
            turn(b, "back0", "M")
            turn(b, "back1", "M")
            next(side, None)
            yield
            turn(b, "ctx", "M")
            next(side, None)
            yield
            turn(b, "out", "M")
            yield

        def end(b):
            yield from empty(MOMENTS_LEAD + ROOT_LEAD + 1 + OUTPUT_LEAD)
            turn(b, "xT", "M")
            yield

        turn(SELF0, "k", "E")
        yield
        turn(SELF0, "q", "S")
        yield
        turn(SELF0, "v", "C")
        yield
        for what in ("sk0", "sk1", "sq0", "sq1"):
            turn(SELF0, what, "M")
            if what[-1] == "1":
                yield
        yield
        yield from heads(SELF0)
        yield from attention_end(SELF0, keys_values(CROSS0))
        yield from end(SELF0)
        yield from queries(CROSS0)
        yield from heads(CROSS0)
        yield from attention_end(CROSS0, iter(()))
        yield from end(CROSS0)
        turn(MIX0, "gate", "M")
        yield from empty(2 + GATE_LEAD)
        turn(MIX0, "wT", "M")
        yield
        turn(MIX0, "b2", "M")
        yield
        side = keys_values(CROSS1)
        for n in range(MIX_STEPS):
            if n < 2 * EXPERTS:
                turn(MIX0, ("up", n), "SE"[n % 2])
            if n % 2 == 1 and n > 2:
                turn(MIX0, ("down", (n - 3) // 2), "C")
            if n in SIDE_STEPS:
                next(side, None)
            yield
        yield from end(MIX0)
        turn(CAUSAL1, "g", "M")
        yield
        turn(CAUSAL1, "score", "M")
        yield from empty(2 + PROBS_LEAD)
        turn(CAUSAL1, "pT", "M")
        yield
        turn(CAUSAL1, "ax", "M")
        yield
        turn(CAUSAL1, "out", "M")
        yield
        yield from end(CAUSAL1)
        yield from queries(CROSS1)
        yield from heads(CROSS1)
        yield from attention_end(CROSS1, iter(()))
        yield from end(CROSS1)
        turn(ROUTE, "logits", "M")
        yield from empty(2 + RANK_LEAD)
        turn(ROUTE, "rank", "M")
        yield

    take_turns(*[lane_program(steps, lane) for lane in range(LANES)])
    return turns


POOLS = {"S": 2, "E": 2, "C": 2, "M": 2}
SIDE_STEPS = (12, 16)
TURNS = bank_turns()


def constants():
    c = np.zeros((P, C_END), np.float32)
    c[:, C_ID:C_ID + P] = np.eye(P)
    c[:, C_TRI:C_TRI + P] = np.triu(np.ones((P, P)), 1)
    c[:, C_ONES:C_ONES + P] = 1.0
    diag = np.where(np.arange(P)[None, :] > np.arange(P)[:, None], MASKED, 0.0)
    c[:, C_MASK:C_MASK + P] = diag
    c[:, C_MASK + 2 * P:C_MASK + 3 * P] = diag
    freqs = np.float32(10000.0) ** (np.arange(0, HD, 2, dtype=np.float32) / np.float32(HD))
    angles = np.arange(SEQ, dtype=np.float32)[:, None] / freqs[None, :]
    cos = np.tile(np.repeat(np.cos(angles), 2, axis=1).T, (HEADS, 1))
    sin = np.tile(np.repeat(np.sin(angles), 2, axis=1).T, (HEADS, 1))
    sin[0::2] *= -1.0
    c[:, C_COS:C_COS + SEQ] = cos
    c[:, C_SIN:C_SIN + SEQ] = sin
    c[0::32, C_KONE] = 1.0
    c[:, C_EPS] = EPS
    c[:, C_ORDER:C_ORDER + QT * EXPERTS] = np.tile(EXPERTS - np.arange(EXPERTS), QT)
    c[:, C_BASE:C_BASE + QT * EXPERTS] = np.tile(CAP * np.arange(EXPERTS), QT)
    c[:, C_TOKEN:C_TOKEN + TILES] = P * np.arange(TILES)[None, :] + np.arange(P)[:, None]
    spread = np.zeros((P, 4, GROUPS, P), np.float32)
    for t in range(GROUPS):
        for g in range(4):
            for j in range(HD):
                d, r = (4 * t + g) * HD + j, 32 * g + j
                spread[d, QHI, t, [r + 8, r + 16]] = 1.0
                spread[d, QLO, t, r + 24] = 1.0
                spread[d, KHI, t, [r + 8, r + 24]] = 1.0
                spread[d, KLO, t, r + 16] = 1.0
    return c, spread.reshape(P, 4 * GROUPS * P)


def decoder(nc, ins, out):
    f32, f32r, u32, i32 = mybir.dt.float32, mybir.dt.float32r, mybir.dt.uint32, mybir.dt.int32
    ALU, ACT, AX = mybir.AluOpType, mybir.ActivationFunctionType, mybir.AxisListType
    stack = ExitStack()
    with stack:
        def sb(name, shape, dt=f32):
            return stack.enter_context(nc.sbuf_tensor(name, shape, dt))

        def sem(name):
            return stack.enter_context(nc.semaphore(name))

        const = sb("const", [P, C_END])
        spread = sb("spread", [P, 4, GROUPS, P], f32r)
        proj_w = sb("proj_w", [P, len(W_NAMES), P])
        cols = sb("cols", [P, len(COL_NAMES)])
        rows = sb("rows", [P, len(ROW_NAMES), P])
        gate_w = sb("gate_w", [P, 2, EXPERTS])
        b1 = sb("b1", [P, EXPERTS * FC])
        b2 = sb("b2", [EXPERTS, P])
        w1_hi = sb("w1_hi", [P, EXPERTS, HID], f32r)
        w1_lo = sb("w1_lo", [P, EXPERTS, HID], f32r)
        mix_w2 = sb("mix_w2", [P, EXPERTS, FC, P])
        x_rows = sb("x_rows", [P, TILES, ROW])
        xT_all = sb("xT_all", [P, BATCH, SEQ])
        cT_all = sb("cT_all", [P, BATCH, SEQ])
        empty_row = sb("empty_row", [P, ROW])
        before = sb("before", [P, TILES + 1, EXPERTS])
        onehot = sb("onehot", [P, TILES, EXPERTS])
        slot = sb("slot", [P, TILES], i32)
        xe_dram = nc.dram_tensor("xe_scratch", (EXPERTS * CAP, ROW), f32, kind="Internal").ap()

        ident = const[:, C_ID:C_ID + P]

        def weight(name):
            return proj_w[:, W_NAMES.index(name), :]

        def col(name):
            i = COL_NAMES.index(name)
            return cols[:, i:i + 1]

        def row(name):
            return rows[:, ROW_NAMES.index(name), :]

        x = [x_rows[:, QT * seq:QT * (seq + 1), 0:P] for seq in range(BATCH)]
        xT = [xT_all[:, seq, :] for seq in range(BATCH)]
        cT = [cT_all[:, seq, :] for seq in range(BATCH)]

        def lanes(name, shape, dt=f32):
            buffers = [sb(f"{name}{lane}", shape, dt) for lane in range(LANES)]
            return [buffers[seq % LANES] for seq in range(BATCH)]

        xb = lanes("xb", [P, QT, P])
        qk = lanes("qk", [P, 2, SEQ])
        qk_hi = lanes("qk_hi", [P, 2, SEQ], f32r)
        qk_lo = lanes("qk_lo", [P, 2, SEQ], f32r)
        q_sp = lanes("q_sp", [P, GROUPS, SEQ], f32r)
        k_head = lanes("k_head", [P, GROUPS, 4, SEQ], f32r)
        q_sh = lanes("q_sh", [P, GROUPS, SEQ], f32r)
        v_aug = lanes("v_aug", [P, QT, HEADS, 32])
        negmax = lanes("negmax", [P, GROUPS, QT, P])
        expo = lanes("expo", [P, ESLOTS, QT * SEQ])
        ctx_sb = lanes("ctx_sb", [P, GROUPS, SEQ])
        k_sp = [e[:, ESLOTS - 2:ESLOTS, :].rearrange("p a (t n) -> p (a t) n", n=SEQ).bitcast(f32r)
                for e in expo]
        masked = [c[:].rearrange("p t n -> p (t n)")[:, 0:3 * P] for c in ctx_sb]
        recip = lanes("recip", [P, QT, HEADS])
        ctx_n = lanes("ctx_n", [P, QT, P])
        aT = lanes("aT", [P, SEQ])
        y = lanes("y", [P, QT, P])
        stats = lanes("stats", [P, QT, 6])
        mv = lanes("mv", [P, QT, 2])
        r0 = lanes("r0", [P, QT])
        newton = lanes("newton", [P, 3, QT])
        gate = lanes("gate", [P, QT, EXPERTS])
        top = lanes("top", [P, QT, 8])
        small = lanes("small", [P, 6, QT])
        g_exp = lanes("g_exp", [P, QT, EXPERTS])
        g_sel = lanes("g_sel", [P, QT, EXPERTS])
        g_w = lanes("g_w", [P, QT, EXPERTS])
        g_wT = lanes("g_wT", [EXPERTS, SEQ])
        route = lanes("route", [P, 5, QT, EXPERTS])
        route_col = lanes("route_col", [P, 8, QT])

        bank = {pool: [stack.enter_context(nc.psum_tensor(f"bank_{pool}{i}", [P, 512], f32))
                       for i in range(n)] for pool, n in POOLS.items()}

        ld_x, ld_xT0, ld_xT, ld_ctx, ld_gate = (
            sem("ld_x"), sem("ld_xT0"), sem("ld_xT"), sem("ld_ctx"), sem("ld_gate"))
        ld_rope, ld_const, ld_cols, ld_rows = (
            sem("ld_rope"), sem("ld_const"), sem("ld_cols"), sem("ld_rows"))
        ld_p0, ld_p1 = sem("ld_p0"), sem("ld_p1")
        ld_spread_k, ld_spread_q, ld_mix_biases = (
            sem("ld_spread_k"), sem("ld_spread_q"), sem("ld_mix_biases"))
        spread_k_ready, spread_q_ready = sem("spread_k_ready"), sem("spread_q_ready")
        v_zeroed, lane1_zeroed = sem("v_zeroed"), sem("lane1_zeroed")
        empty_row_ready, slots_emptied = sem("empty_row_ready"), sem("slots_emptied")

        filled = {pool: [sem(f"filled_{pool}{i}") for i in range(n)] for pool, n in POOLS.items()}
        drained = {pool: [sem(f"drained_{pool}{i}") for i in range(n)] for pool, n in POOLS.items()}
        k_head_ready = [[sem(f"k_head_ready{i}_{half}") for half in range(2)] for i in range(BATCH)]
        split_q_ready = [sem(f"split_q_ready{i}") for i in range(BATCH)]
        split_k_ready = [sem(f"split_k_ready{i}") for i in range(BATCH)]
        var_ready = [sem(f"var_ready{i}") for i in range(BATCH)]
        rstd0_ready = [sem(f"rstd0_ready{i}") for i in range(BATCH)]
        x_ready = [sem(f"x_ready{i}") for i in range(BATCH)]
        xb_ready = [sem(f"xb_ready{i}") for i in range(BATCH)]
        gatemax_ready = [sem(f"gatemax_ready{i}") for i in range(BATCH)]
        gateexp_ready = [sem(f"gateexp_ready{i}") for i in range(BATCH)]
        gatew_ready = [sem(f"gatew_ready{i}") for i in range(BATCH)]
        rowmax_ready = [sem(f"rowmax_ready{i}") for i in range(BATCH)]
        probs_ready = [sem(f"probs_ready{i}") for i in range(BATCH)]
        act_own = [sem(f"act_own{i}") for i in range(BATCH)]
        dve_own = sem("dve_own")
        shifted = [sem(f"shifted{i}") for i in range(BATCH)]
        routeexp_ready = [sem(f"routeexp_ready{i}") for i in range(BATCH)]
        onehot_ready = [sem(f"onehot_ready{i}") for i in range(BATCH)]
        slot_ready = [sem(f"slot_ready{i}") for i in range(BATCH)]
        pool_own = sem("pool_own")
        w1_split = sem("w1_split")
        split_x_ready = [sem(f"split_x_ready{i}") for i in range(BATCH)]
        scattered = sem("scattered")
        w1_loaded = [sem(f"w1_loaded{e}") for e in range(EXPERTS)]
        w2_loaded = [sem(f"w2_loaded{e}") for e in range(EXPERTS)]

        def where(seq, block, what):
            pool, i, _ = TURNS[seq, block, what]
            return bank[pool][i]

        def full(seq, block, what):
            pool, i, _ = TURNS[seq, block, what]
            return filled[pool][i]

        def free(seq, block, what):
            pool, i, _ = TURNS[seq, block, what]
            return drained[pool][i]

        def wait_free(pe, seq, block, what):
            if TURNS[seq, block, what][2] > 0:
                pe.wait_ge(free(seq, block, what), TURNS[seq, block, what][2])

        def wait_filled(eng, seq, block, what):
            eng.wait_ge(full(seq, block, what), TURNS[seq, block, what][2] + 1)

        def wait_drained(eng, seq, block, what):
            eng.wait_ge(free(seq, block, what), TURNS[seq, block, what][2] + 1)

        staging = expo[0][:, 0:4, :].rearrange("p a (t c) -> p a t c", t=GROUPS)

        with nc.Block() as block:
            @block.sync
            def _(sp):
                sp.dma_start(xT_all[:, 0, :], ins["xT"][:, 0, :]).then_inc(ld_xT0, 16)
                sp.dma_start(const[:, C_COS:C_END], ins["const"][:, C_COS:C_END]).then_inc(ld_rope, 16)
                sp.dma_start(staging[:, QHI:QLO + 1, :, :], ins["spread"][:, QHI:QLO + 1, :, :]
                             ).then_inc(ld_spread_q, 16)
                sp.dma_start(const[:, 0:C_COS], ins["const"][:, 0:C_COS]).then_inc(ld_const, 16)
                sp.dma_start(x_rows[:, :, 0:P], ins["x"]).then_inc(ld_x, 16)
                sp.dma_start(cT_all[:], ins["cT"]).then_inc(ld_ctx, 16)

            @block.scalar
            def _(act):
                act.dma_start(proj_w[:, 0:6, :], ins["proj"][:, 0:6, :]).then_inc(ld_p0, 16)
                act.dma_start(cols[:], ins["cols"]).then_inc(ld_cols, 16)
                act.dma_start(staging[:, KHI:KLO + 1, :, :], ins["spread"][:, KHI:KLO + 1, :, :]
                              ).then_inc(ld_spread_k, 16)
                act.dma_start(rows[:].rearrange("p a b -> p (a b)"),
                              ins["rows"].partition_broadcast(P)).then_inc(ld_rows, 16)
                act.dma_start(xT_all[:, 1:BATCH, :], ins["xT"][:, 1:BATCH, :]).then_inc(ld_xT, 16)
                act.dma_start(proj_w[:, 6:16, :], ins["proj"][:, 6:16, :]).then_inc(ld_p1, 16)
                act.dma_start(gate_w[:], ins["gates"]).then_inc(ld_gate, 16)
                nc.scalar.preload_act_table_set("natural_log_exp_and_others")

            @block.gpsimd
            def _(pool):
                nc.gpsimd.memset(k_head[0][:].bitcast(u32), 0)

            @block.vector
            def _(dve):
                nc.vector.memset(v_aug[0][:].bitcast(u32), 0).then_inc(v_zeroed, 1)
                nc.vector.memset(negmax[0][:].bitcast(u32), 0)
                dve.wait_ge(v_zeroed, 1)
                nc.vector.memset(v_aug[0][:, :, :, HD:HD + 1], 1.0)
                nc.vector.memset(before[:, 0, :], 0.0)

        last_w1 = [expo[0][:, e, :] for e in range(ESLOTS)] + [
            negmax[0][:].rearrange("p t q n -> p (t q n)")[:, i * HID:(i + 1) * HID]
            for i in range(EXPERTS - ESLOTS)]
        last_mixture = last_mixture_programs(nc, stack, out, dict(
            const=const, x_rows=x_rows, xe_dram=xe_dram, w1=last_w1, w2=mix_w2, banks=bank,
            drained=drained, xe=expo[1], xeT=xT_all, x_norm=cT_all, ye=v_aug[1], ye_norm=v_aug[0],
            hid=ctx_sb[1], ident=ident, scattered=scattered, w1_loaded=w1_loaded, w2_loaded=w2_loaded))

        with nc.Block() as block:
            @block.gpsimd
            def _(pool):
                def residual(seq, b, bias):
                    if b > SELF0:
                        pool.wait_ge(x_ready[seq], b)
                    nc.gpsimd.tensor_tensor(
                        xb[seq][:], x[seq], row(bias).unsqueeze(1).broadcast_to([P, QT, P]), ALU.add
                    ).then_inc(xb_ready[seq], 1)

                def split_weights(e):
                    w = mix_w2[:, e, :, :].rearrange("p f d -> p (f d)")
                    pool.wait_ge(w1_loaded[e], 16)
                    nc.gpsimd.tensor_copy(w1_hi[:, e, :], w).then_inc(pool_own, 1)
                    pool.wait_ge(pool_own, e + 1)
                    nc.gpsimd.tensor_tensor(w1_lo[:, e, :], w, w1_hi[:, e, :].bitcast(f32), ALU.subtract
                                            ).then_inc(w1_split, 1)

                def scatter(seq):
                    pool.wait_ge(slots_emptied, 16)
                    pool.wait_ge(slot_ready[seq], 1)
                    for i in range(QT * seq, QT * (seq + 1)):
                        nc.gpsimd.indirect_dma_start(
                            xe_dram, bass.IndirectOffsetOnAxis(slot[:, i:i + 1].bitcast(u32), 0),
                            x_rows[:, i, :], None, bounds_check=TOKENS - 1, oob_is_err=False
                        ).then_inc(scattered, 16)

                nc.gpsimd.memset(v_aug[1][:].bitcast(u32), 0).then_inc(v_zeroed, 1)
                nc.gpsimd.memset(negmax[1][:].bitcast(u32), 0)
                nc.gpsimd.memset(k_head[1][:].bitcast(u32), 0)
                pool.wait_ge(v_zeroed, 2)
                nc.gpsimd.memset(v_aug[1][:, :, :, HD:HD + 1], 1.0).then_inc(lane1_zeroed, 1)
                nc.gpsimd.memset(empty_row[:, 0:P], 0.0)
                nc.gpsimd.memset(empty_row[:, P:P + 1], float(NOWHERE))
                nc.gpsimd.memset(empty_row[:, P + 1:ROW], 0.0).then_inc(empty_row_ready, 1)
                pool.wait_ge(ld_x, 16)
                pool.wait_ge(ld_rows, 16)
                for seq, b, what in TURNS:
                    if (seq, b) == (0, CROSS0) and what[0] == "max" and what[1] % 2 == 0:
                        split_weights(what[1] // 2)
                    if (b, what) == (SELF0, "k"):
                        residual(seq, b, "bo0")
                    elif (b, what) == (CROSS0, "q"):
                        residual(seq, b, "box0")
                    elif (b, what) == (CROSS1, "q"):
                        residual(seq, b, "box1")
                    elif (b, what) == (ROUTE, "rank"):
                        scatter(seq)
                last_mixture["gpsimd"](pool)

            @block.sync
            def _(sp):
                def by_head(seq, b, what):
                    half = int(what[2])
                    wait_drained(sp, seq, b, what)
                    if seq == 1:
                        sp.wait_ge(lane1_zeroed, 1)
                    t = slice(2 * half, 2 * half + 2)
                    for g in range(4):
                        r = slice(32 * g, 32 * g + 32)
                        sp.dma_start(k_head[seq][r, t, g, :].bitcast(f32),
                                     k_sp[seq][r, t, :].bitcast(f32)
                                     ).then_inc(k_head_ready[seq][half], 16)

                def load(place, name, e, loaded):
                    sp.dma_start(place, ins[name][:, e]).then_inc(loaded[e], 16)

                for seq, b, what in TURNS:
                    if what in ("sk0", "sk1"):
                        by_head(seq, b, what)
                    elif b == SELF0 and seq < LANES and what[0] == "pv":
                        wait_filled(sp, seq, b, what)
                        e = GROUPS * seq + what[1]
                        load(mix_w2[:, e].rearrange("p f d -> p (f d)"), "mix0_w1", e, w1_loaded)
                    elif (seq, b) == (0, CROSS0) and what[0] == "exp" and what[1] % 2 == 1:
                        sp.wait_ge(w1_split, what[1] // 2 + 1)
                        load(mix_w2[:, what[1] // 2], "mix0_w2", what[1] // 2, w2_loaded)
                    elif b == CROSS0 and seq == 0 and what == ("pv", 0):
                        wait_filled(sp, seq, b, what)
                        sp.dma_start(b1[:], ins["b1"]).then_inc(ld_mix_biases, 16)
                        sp.dma_start(b2[:], ins["b2"]).then_inc(ld_mix_biases, 16)
                        sp.wait_ge(empty_row_ready, 1)
                        sp.dma_start(xe_dram.rearrange("(e p) r -> p e r", p=P),
                                     empty_row[:].unsqueeze(1).broadcast_to([P, EXPERTS, ROW])
                                     ).then_inc(slots_emptied, 16)
                    elif (seq, b) == (BATCH - LANES, CROSS1) and what[0] == "max" and what[1] % 2 == 0:
                        if what[1] == 0:
                            for last in range(BATCH - LANES, BATCH):
                                wait_filled(sp, last, MIX0, ("down", EXPERTS - 1))
                        wait_filled(sp, seq, b, what)
                        load(mix_w2[:, what[1] // 2], "mix1_w2", what[1] // 2, w2_loaded)
                    elif (seq, b, what) == (BATCH - LANES, CROSS1, "out"):
                        wait_filled(sp, seq, b, what)
                        for e in range(EXPERTS):
                            load(last_w1[e], "mix1_w1", e, w1_loaded)
                last_mixture["sync"](sp)

            @block.tensor
            def _(pe):
                mm = nc.tensor.matmul

                def project(seq, b, what, w, source, rope=False):
                    wait_free(pe, seq, b, what)
                    ps = where(seq, b, what)
                    last = mm(ps[:, 0:SEQ], weight(w), source[:], start=True, stop=True)
                    if rope:
                        last = mm(ps[:, SEQ:2 * SEQ], weight(w + "s"), source[:],
                                  start=True, stop=True)
                    last.then_inc(full(seq, b, what), 1)

                def project_values(seq, b, w, source):
                    wait_free(pe, seq, b, "v")
                    for k in range(QT):
                        last = mm(where(seq, b, "v")[:, k * P:(k + 1) * P],
                                  source[:, k * P:(k + 1) * P], weight(w), start=True, stop=True)
                    last.then_inc(full(seq, b, "v"), 1)

                def spread_rows(seq, b, what, i, hi, lo):
                    for half in range(2):
                        wait_free(pe, seq, b, f"{what}{half}")
                        for t in (2 * half, 2 * half + 1):
                            dst = where(seq, b, f"{what}{half}")[:, (t % 2) * SEQ:(t % 2 + 1) * SEQ]
                            mm(dst, spread[:, hi, t, :], qk_hi[seq][:, i, :],
                               start=True, stop=False)
                            last = mm(dst, spread[:, lo, t, :], qk_lo[seq][:, i, :],
                                      start=False, stop=True)
                        last.then_inc(full(seq, b, f"{what}{half}"), 1)

                def keys_values(seq, b, wk, wv):
                    pe.wait_ge(ld_p1, 16)
                    pe.wait_ge(ld_ctx, 16)
                    project(seq, b, "k", wk, cT[seq])
                    project_values(seq, b, wv, cT[seq])
                    yield
                    pe.wait_ge(split_k_ready[seq], MHA[b] + 1)
                    spread_rows(seq, b, "sk", 1, KHI, KLO)
                    yield

                def queries(seq, b, wq):
                    wait_drained(pe, seq, b - 1, "xT")
                    project(seq, b, "q", wq, xT[seq])
                    yield from empty(1 + SPLIT_LEAD)
                    pe.wait_ge(split_q_ready[seq], MHA[b] + 1)
                    spread_rows(seq, b, "sq", 0, QHI, QLO)
                    yield

                def self_projections(seq):
                    b = SELF0
                    pe.wait_ge(ld_p0, 16)
                    pe.wait_ge(ld_xT if seq else ld_xT0, 16)
                    project(seq, b, "k", "k0", xT[seq], rope=True)
                    yield
                    project(seq, b, "q", "q0", xT[seq], rope=True)
                    yield
                    project_values(seq, b, "v0", xT[seq])
                    yield
                    pe.wait_ge(spread_k_ready, 1)
                    pe.wait_ge(split_k_ready[seq], 1)
                    spread_rows(seq, b, "sk", 1, KHI, KLO)
                    yield
                    pe.wait_ge(spread_q_ready, 1)
                    pe.wait_ge(split_q_ready[seq], 1)
                    spread_rows(seq, b, "sq", 0, QHI, QLO)
                    yield
                    yield

                def heads(seq, b):
                    for k in range(HEAD_STEPS):
                        if group_at(k, SHIFT_AT) is not None:
                            t = group_at(k, SHIFT_AT)
                            pe.wait_ge(ld_const, 16)
                            wait_drained(pe, seq, b, ("max", 4 * t + 3))
                            wait_free(pe, seq, b, ("shift", t))
                            for qt in range(QT):
                                last = nc.tensor.transpose(
                                    where(seq, b, ("shift", t))[:, qt * P:(qt + 1) * P],
                                    negmax[seq][:, t, qt, :], ident)
                            last.then_inc(full(seq, b, ("shift", t)), 1)
                        if k < HEADS:
                            t, g = k // 4, k % 4
                            if k == 0:
                                wait_drained(pe, seq, b, "sq0")
                                pe.wait_ge(k_head_ready[seq][0], 64 * (MHA[b] + 1))
                            if k == 8:
                                wait_drained(pe, seq, b, "sq1")
                                pe.wait_ge(k_head_ready[seq][1], 64 * (MHA[b] + 1))
                            wait_free(pe, seq, b, ("max", k))
                            for qt in range(QT):
                                last = mm(where(seq, b, ("max", k))[:, qt * SEQ:(qt + 1) * SEQ],
                                          q_sp[seq][:, t, qt * P:(qt + 1) * P],
                                          k_head[seq][:, t, g, :],
                                          start=True, stop=True)
                            last.then_inc(full(seq, b, ("max", k)), 1)
                        if 0 <= k - EXP_AT < HEADS:
                            h = k - EXP_AT
                            t, g = h // 4, h % 4
                            if g == 0:
                                wait_drained(pe, seq, b, ("shift", t))
                            wait_free(pe, seq, b, ("exp", h))
                            for kt in range(QT):
                                last = mm(where(seq, b, ("exp", h))[:, kt * SEQ:(kt + 1) * SEQ],
                                          k_head[seq][:, t, g, kt * P:(kt + 1) * P],
                                          q_sh[seq][:, t, :],
                                          start=True, stop=True)
                            last.then_inc(full(seq, b, ("exp", h)), 1)
                        for kt in range(QT):
                            t = group_at(k, VALUES_AT - 1 + kt)
                            if t is None:
                                continue
                            if kt == 0:
                                wait_drained(pe, seq, b, ("exp", 4 * t + 3))
                                wait_free(pe, seq, b, ("pv", t))
                                if t == 0:
                                    wait_drained(pe, seq, b, "v")
                            for g in range(4):
                                h = 4 * t + g
                                last = mm(where(seq, b, ("pv", t))[32 * g:32 * g + 32, 0:SEQ],
                                          v_aug[seq][:, kt, h, :],
                                          expo[seq][:, h % ESLOTS, kt * SEQ:(kt + 1) * SEQ],
                                          start=(kt == 0), stop=(kt == QT - 1))
                            if kt == QT - 1:
                                last.then_inc(full(seq, b, ("pv", t)), 1)
                        yield

                def attention_end(seq, b, wo, side):
                    wait_drained(pe, seq, b, ("pv", GROUPS - 1))
                    for qt in range(QT):
                        wait_free(pe, seq, b, f"back{qt}")
                        for t in range(GROUPS):
                            last = nc.tensor.transpose(
                                where(seq, b, f"back{qt}")[:, t * P:(t + 1) * P],
                                ctx_sb[seq][:, t, qt * P:(qt + 1) * P], ident)
                        last.then_inc(full(seq, b, f"back{qt}"), 1)
                    next(side, None)
                    yield
                    wait_free(pe, seq, b, "ctx")
                    for qt in range(QT):
                        wait_drained(pe, seq, b, f"back{qt}")
                        last = nc.tensor.transpose(where(seq, b, "ctx")[:, qt * P:(qt + 1) * P],
                                                   ctx_n[seq][:, qt, :], ident)
                    last.then_inc(full(seq, b, "ctx"), 1)
                    next(side, None)
                    yield
                    wait_drained(pe, seq, b, "ctx")
                    yield from output(seq, b, "out", weight(wo))

                def output(seq, b, what, w):
                    wait_free(pe, seq, b, what)
                    for qt in range(QT):
                        last = mm(where(seq, b, what)[:, qt * P:(qt + 1) * P],
                                  aT[seq][:, qt * P:(qt + 1) * P], w, start=True, stop=True)
                    last.then_inc(full(seq, b, what), 1)
                    yield

                def transpose_x(seq, b):
                    yield from empty(MOMENTS_LEAD + ROOT_LEAD + 1 + OUTPUT_LEAD)
                    pe.wait_ge(x_ready[seq], b + 1)
                    wait_free(pe, seq, b, "xT")
                    for qt in range(QT):
                        last = nc.tensor.transpose(where(seq, b, "xT")[:, qt * P:(qt + 1) * P],
                                                   x[seq][:, qt, :], ident)
                    last.then_inc(full(seq, b, "xT"), 1)
                    yield

                def mixture(seq):
                    b = MIX0
                    pe.wait_ge(ld_gate, 16)
                    wait_drained(pe, seq, b - 1, "xT")
                    wait_free(pe, seq, b, "gate")
                    for qt in range(QT):
                        last = mm(where(seq, b, "gate")[:, qt * EXPERTS:(qt + 1) * EXPERTS],
                                  xT[seq][:, qt * P:(qt + 1) * P], gate_w[:, 0, :],
                                  start=True, stop=True)
                    last.then_inc(full(seq, b, "gate"), 1)
                    yield from empty(2 + GATE_LEAD)
                    pe.wait_ge(gatew_ready[seq], 1)
                    wait_free(pe, seq, b, "wT")
                    for qt in range(QT):
                        last = nc.tensor.transpose(
                            where(seq, b, "wT")[0:EXPERTS, qt * P:(qt + 1) * P],
                            g_w[seq][:, qt, :], ident)
                    last.then_inc(full(seq, b, "wT"), 1)
                    yield
                    pe.wait_ge(ld_mix_biases, 32)
                    wait_drained(pe, seq, b, "wT")
                    wait_free(pe, seq, b, "b2")
                    for qt in range(QT):
                        last = mm(where(seq, b, "b2")[:, qt * P:(qt + 1) * P],
                                  g_wT[seq][:, qt * P:(qt + 1) * P], b2[:],
                                  start=True, stop=True)
                    last.then_inc(full(seq, b, "b2"), 1)
                    yield
                    hidden = expo[seq][:, 0:4, :].rearrange("p a (h n) -> p (a h) n", n=SEQ)
                    side = keys_values(seq, CROSS1, "kx1", "vx1")
                    for n in range(MIX_STEPS):
                        if n < 2 * EXPERTS:
                            e = n // 2
                            pe.wait_ge(w1_split, e + 1)
                            if n == 0:
                                pe.wait_ge(split_x_ready[seq], 1)
                            wait_free(pe, seq, b, ("up", n))
                            hi, lo = qk_hi[seq][:, 0, :], qk_lo[seq][:, 0, :]
                            for i in range(2):
                                f = 2 * (n % 2) + i
                                dst = where(seq, b, ("up", n))[:, i * SEQ:(i + 1) * SEQ]
                                w_hi = w1_hi[:, e, f * P:(f + 1) * P]
                                w_lo = w1_lo[:, e, f * P:(f + 1) * P]
                                mm(dst, w_hi, hi, start=True, stop=False)
                                mm(dst, w_hi, lo, start=False, stop=False)
                                last = mm(dst, w_lo, hi, start=False, stop=True)
                            last.then_inc(full(seq, b, ("up", n)), 1)
                        if n % 2 == 1 and n > 2:
                            e = (n - 3) // 2
                            for m in (2 * e, 2 * e + 1):
                                wait_drained(pe, seq, b, ("up", m))
                            wait_free(pe, seq, b, ("down", e))
                            pe.wait_ge(w2_loaded[e], 16)
                            for qt in range(QT):
                                for f in range(FC):
                                    last = mm(where(seq, b, ("down", e))[:, qt * P:(qt + 1) * P],
                                              hidden[:, (e % 2) * FC + f, qt * P:(qt + 1) * P],
                                              mix_w2[:, e, f, :],
                                              start=(f == 0), stop=(f == FC - 1))
                            last.then_inc(full(seq, b, ("down", e)), 1)
                        if n in SIDE_STEPS:
                            next(side, None)
                        yield

                def causal(seq):
                    b = CAUSAL1
                    pe.wait_ge(ld_p1, 16)
                    wait_drained(pe, seq, b - 1, "xT")
                    wait_free(pe, seq, b, "g")
                    mm(where(seq, b, "g")[:, 0:SEQ], weight("qk"), xT[seq],
                       start=True, stop=True).then_inc(full(seq, b, "g"), 1)
                    yield
                    wait_drained(pe, seq, b, "g")
                    wait_free(pe, seq, b, "score")
                    ps = where(seq, b, "score")
                    mm(ps[:, 0:P], aT[seq][:, 0:P], xT[seq][:, 0:P], start=True, stop=True)
                    mm(ps[:, P:3 * P], aT[seq][:, P:SEQ], xT[seq],
                       start=True, stop=True).then_inc(full(seq, b, "score"), 1)
                    yield from empty(2 + PROBS_LEAD)
                    pe.wait_ge(probs_ready[seq], 1)
                    wait_free(pe, seq, b, "pT")
                    for i in range(3):
                        last = nc.tensor.transpose(where(seq, b, "pT")[:, i * P:(i + 1) * P],
                                                   masked[seq][:, i * P:(i + 1) * P], ident)
                    last.then_inc(full(seq, b, "pT"), 1)
                    yield
                    wait_drained(pe, seq, b, "pT")
                    wait_free(pe, seq, b, "ax")
                    pT = expo[seq][:, 0, 0:3 * P]
                    mm(where(seq, b, "ax")[:, 0:SEQ], x[seq][:, 0, :], pT[:, 0:SEQ],
                       start=True, stop=False)
                    mm(where(seq, b, "ax")[:, P:SEQ], x[seq][:, 1, :], pT[:, SEQ:3 * P],
                       start=False, stop=True).then_inc(full(seq, b, "ax"), 1)
                    yield
                    wait_drained(pe, seq, b, "ax")
                    yield from output(seq, b, "out", weight("ov"))

                def routing(seq):
                    wait_drained(pe, seq, CROSS1, "xT")
                    wait_free(pe, seq, ROUTE, "logits")
                    for qt in range(QT):
                        last = mm(where(seq, ROUTE, "logits")[:, qt * EXPERTS:(qt + 1) * EXPERTS],
                                  xT[seq][:, qt * P:(qt + 1) * P], gate_w[:, 1, :],
                                  start=True, stop=True)
                    last.then_inc(full(seq, ROUTE, "logits"), 1)
                    yield from empty(2 + RANK_LEAD)
                    pe.wait_ge(onehot_ready[seq], 1)
                    wait_free(pe, seq, ROUTE, "rank")
                    for qt in range(QT):
                        dst = where(seq, ROUTE, "rank")[:, qt * EXPERTS:(qt + 1) * EXPERTS]
                        mm(dst, const[:, C_TRI:C_TRI + P], onehot[:, QT * seq + qt, :],
                           start=True, stop=False)
                        last = mm(dst, const[:, C_ONES:C_ONES + P], before[:, QT * seq + qt, :],
                                  start=False, stop=True)
                    last.then_inc(full(seq, ROUTE, "rank"), 1)
                    yield

                def program(seq):
                    yield from self_projections(seq)
                    yield from heads(seq, SELF0)
                    yield from attention_end(seq, SELF0, "o0",
                                             keys_values(seq, CROSS0, "kx0", "vx0"))
                    yield from transpose_x(seq, SELF0)
                    yield from queries(seq, CROSS0, "qx0")
                    yield from heads(seq, CROSS0)
                    yield from attention_end(seq, CROSS0, "ox0", iter(()))
                    yield from transpose_x(seq, CROSS0)
                    yield from mixture(seq)
                    yield from transpose_x(seq, MIX0)
                    yield from causal(seq)
                    yield from transpose_x(seq, CAUSAL1)
                    yield from queries(seq, CROSS1, "qx1")
                    yield from heads(seq, CROSS1)
                    yield from attention_end(seq, CROSS1, "ox1", iter(()))
                    yield from transpose_x(seq, CROSS1)
                    yield from routing(seq)

                take_turns(*[lane_program(program, lane) for lane in range(LANES)])
                last_mixture["tensor"](pe)

            @block.scalar
            def _(act):
                activate = nc.scalar.activation

                def evacuate(seq, b, what, i, bias):
                    wait_filled(act, seq, b, what)
                    activate(qk_hi[seq][:, i, :], where(seq, b, what)[:, 0:SEQ],
                             ACT.Identity, bias=bias)
                    activate(qk[seq][:, i, :], where(seq, b, what)[:, 0:SEQ],
                             ACT.Identity, bias=bias).then_inc(free(seq, b, what), 1)

                def spread_keys(seq, b):
                    for half in range(2):
                        wait_filled(act, seq, b, f"sk{half}")
                        activate(k_sp[seq][:, 2 * half:2 * half + 2, :],
                                 where(seq, b, f"sk{half}")[:].rearrange("p (t n) -> p t n", t=2),
                                 ACT.Identity, bias=const[:, C_KONE:C_KONE + 1]
                                 ).then_inc(free(seq, b, f"sk{half}"), 1)

                def spread_queries(seq, b):
                    for half in range(2):
                        wait_filled(act, seq, b, f"sq{half}")
                        activate(q_sp[seq][:, 2 * half:2 * half + 2, :],
                                 where(seq, b, f"sq{half}")[:].rearrange("p (t n) -> p t n", t=2),
                                 ACT.Copy).then_inc(free(seq, b, f"sq{half}"), 1)

                def keys_values(seq, b, bk):
                    evacuate(seq, b, "k", 1, bk)
                    yield
                    spread_keys(seq, b)
                    yield

                def queries(seq, b, bq):
                    evacuate(seq, b, "q", 0, bq)
                    yield from empty(1 + SPLIT_LEAD)
                    spread_queries(seq, b)
                    yield

                def self_projections(seq):
                    for _ in range(3):
                        yield
                    spread_keys(seq, SELF0)
                    yield
                    spread_queries(seq, SELF0)
                    yield
                    yield

                def heads(seq, b):
                    scale = float(HD) ** -0.5
                    for k in range(HEAD_STEPS):
                        if 0 <= k - EXP_AT < HEADS:
                            h = k - EXP_AT
                            wait_filled(act, seq, b, ("exp", h))
                            if h >= ESLOTS:
                                wait_filled(act, seq, b, ("pv", (h - ESLOTS) // 4))
                            activate(expo[seq][:, h % ESLOTS, :], where(seq, b, ("exp", h))[:],
                                     ACT.Exp, scale=scale).then_inc(free(seq, b, ("exp", h)), 1)
                        if group_at(k, VALUES_AT) is not None:
                            t = group_at(k, VALUES_AT)
                            wait_filled(act, seq, b, ("pv", t))
                            activate(ctx_sb[seq][:, t, :], where(seq, b, ("pv", t))[:, 0:SEQ],
                                     ACT.Copy).then_inc(free(seq, b, ("pv", t)), 1)
                        yield

                def attention_end(seq, b, side):
                    next(side, None)
                    yield
                    wait_filled(act, seq, b, "ctx")
                    activate(aT[seq][:], where(seq, b, "ctx")[:, 0:SEQ],
                             ACT.Copy).then_inc(free(seq, b, "ctx"), 1)
                    next(side, None)
                    yield
                    yield

                def normalise(seq, b):
                    yield from empty(MOMENTS_LEAD)
                    act.wait_ge(var_ready[seq], b + 1)
                    activate(r0[seq][:], mv[seq][:, :, 1], ACT.Ln,
                             bias=const[:, C_EPS:C_EPS + 1]).then_inc(act_own[seq], 1)
                    act.wait_ge(act_own[seq], b + 1)
                    activate(r0[seq][:], r0[seq][:], ACT.Exp,
                             scale=-0.5).then_inc(rstd0_ready[seq], 1)
                    yield from empty(ROOT_LEAD + 1 + OUTPUT_LEAD)
                    wait_filled(act, seq, b, "xT")
                    if b == CROSS0:
                        activate(qk_hi[seq][:, 0, :], where(seq, b, "xT")[:, 0:SEQ], ACT.Copy)
                    activate(xT[seq], where(seq, b, "xT")[:, 0:SEQ],
                             ACT.Copy).then_inc(free(seq, b, "xT"), 1)
                    yield

                def mixture(seq):
                    b = MIX0
                    yield
                    act.wait_ge(gatemax_ready[seq], 1)
                    for qt in range(QT):
                        last = activate(g_exp[seq][:, qt, :], gate[seq][:, qt, :], ACT.Exp,
                                        bias=small[seq][:, 0, qt:qt + 1])
                    last.then_inc(gateexp_ready[seq], 1)
                    yield from empty(1 + GATE_LEAD)
                    wait_filled(act, seq, b, "wT")
                    activate(g_wT[seq][:], where(seq, b, "wT")[0:EXPERTS, 0:SEQ],
                             ACT.Copy).then_inc(free(seq, b, "wT"), 1)
                    yield
                    yield
                    hidden = expo[seq][:, 0:4, :].rearrange("p a (h n) -> p (a h) n", n=SEQ)
                    act.wait_ge(ld_mix_biases, 32)
                    side = keys_values(seq, CROSS1, 0.0)
                    for n in range(MIX_STEPS):
                        if n < 2 * EXPERTS and relu_on_scalar(n):
                            e = n // 2
                            wait_filled(act, seq, b, ("up", n))
                            if e >= 2:
                                wait_filled(act, seq, b, ("down", e - 2))
                            for i in range(2):
                                f = 2 * (n % 2) + i
                                last = activate(hidden[:, (e % 2) * FC + f, :],
                                                where(seq, b, ("up", n))[:, i * SEQ:(i + 1) * SEQ],
                                                ACT.Relu, bias=b1[:, e * FC + f:e * FC + f + 1])
                            last.then_inc(free(seq, b, ("up", n)), 1)
                        if n in SIDE_STEPS:
                            next(side, None)
                        yield

                def causal(seq):
                    b = CAUSAL1
                    wait_filled(act, seq, b, "g")
                    activate(aT[seq][:], where(seq, b, "g")[:, 0:SEQ],
                             ACT.Copy).then_inc(free(seq, b, "g"), 1)
                    yield
                    yield
                    act.wait_ge(rowmax_ready[seq], 1)
                    for qt, (lo, hi) in enumerate(((0, P), (P, 3 * P))):
                        last = activate(masked[seq][:, lo:hi], masked[seq][:, lo:hi], ACT.Exp,
                                        scale=float(P) ** -0.5, bias=small[seq][:, 1, qt:qt + 1],
                                        accum_out=small[seq][:, 2, qt:qt + 1])
                    last.then_inc(probs_ready[seq], 1)
                    yield from empty(1 + PROBS_LEAD)
                    wait_filled(act, seq, b, "pT")
                    activate(expo[seq][:, 0, 0:3 * P], where(seq, b, "pT")[:, 0:3 * P],
                             ACT.Copy).then_inc(free(seq, b, "pT"), 1)
                    yield
                    wait_filled(act, seq, b, "ax")
                    activate(aT[seq][:], where(seq, b, "ax")[:, 0:SEQ],
                             ACT.Copy).then_inc(free(seq, b, "ax"), 1)
                    yield
                    yield

                def program(seq):
                    yield from self_projections(seq)
                    yield from heads(seq, SELF0)
                    yield from attention_end(seq, SELF0, keys_values(seq, CROSS0, col("bkx0")))
                    yield from normalise(seq, SELF0)
                    yield from queries(seq, CROSS0, col("bqx0"))
                    yield from heads(seq, CROSS0)
                    yield from attention_end(seq, CROSS0, iter(()))
                    yield from normalise(seq, CROSS0)
                    yield from mixture(seq)
                    yield from normalise(seq, MIX0)
                    yield from causal(seq)
                    yield from normalise(seq, CAUSAL1)
                    yield from queries(seq, CROSS1, 0.0)
                    yield from heads(seq, CROSS1)
                    yield from attention_end(seq, CROSS1, iter(()))
                    yield from normalise(seq, CROSS1)
                    yield
                    act.wait_ge(shifted[seq], 1)
                    activate(route[seq][:, 3], route[seq][:, 1], ACT.Exp).then_inc(routeexp_ready[seq], 1)
                    yield from empty(1 + RANK_LEAD)
                    yield

                for kinds, loaded, rounded in ((slice(KHI, KLO + 1), ld_spread_k, spread_k_ready),
                                               (slice(QHI, QLO + 1), ld_spread_q, spread_q_ready)):
                    act.wait_ge(loaded, 16)
                    activate(spread[:, kinds, :, :], staging[:, kinds, :, :], ACT.Copy
                             ).then_inc(rounded, 1)
                act.wait_ge(ld_rope, 16)
                act.wait_ge(ld_cols, 16)
                take_turns(*[lane_program(program, lane) for lane in range(LANES)])
                last_mixture["scalar"](act)

            @block.vector
            def _(dve):
                own = [0]

                def link(instruction):
                    own[0] += 1
                    instruction.then_inc(dve_own, 1)
                    dve.wait_ge(dve_own, own[0])

                V = nc.vector

                def values(seq, b, bv):
                    dve.wait_ge(ld_rows, 16)
                    if seq == 1:
                        dve.wait_ge(lane1_zeroed, 1)
                    wait_filled(dve, seq, b, "v")
                    for k in range(QT):
                        src = where(seq, b, "v")[:, k * P:(k + 1) * P].rearrange(
                            "p (h d) -> p h d", d=HD)
                        dst = v_aug[seq][:, k, :, 0:HD]
                        if bv is None:
                            last = V.tensor_copy(dst, src)
                        else:
                            last = V.tensor_tensor(dst, src, row(bv).rearrange(
                                "p (h d) -> p h d", d=HD), ALU.add)
                    last.then_inc(free(seq, b, "v"), 1)

                def low_part(seq, i, ready):
                    V.tensor_tensor(qk_lo[seq][:, i, :], qk[seq][:, i, :],
                                    qk_hi[seq][:, i, :].bitcast(f32), ALU.subtract
                                    ).then_inc(ready[seq], 1)

                def keys_values(seq, b, bv):
                    wait_drained(dve, seq, b, "k")
                    low_part(seq, 1, split_k_ready)
                    values(seq, b, bv)
                    yield
                    yield

                def queries(seq, b):
                    wait_drained(dve, seq, b, "q")
                    low_part(seq, 0, split_q_ready)
                    yield from empty(1 + SPLIT_LEAD)
                    yield

                def self_projections(seq):
                    b = SELF0
                    t0 = ctx_sb[seq][:, 0:2, :]
                    t1 = ctx_sb[seq][:, 2:4, :]

                    def rotate(i, what, c0, c1):
                        wait_filled(dve, seq, b, what)
                        ps = where(seq, b, what)
                        V.scalar_tensor_tensor(t0[:, i, :], ps[:, 0:SEQ], col(c0),
                                               const[:, C_COS:C_COS + SEQ], ALU.add, ALU.mult)
                        V.scalar_tensor_tensor(t1[:, i, :], ps[:, SEQ:2 * SEQ], col(c1),
                                               const[:, C_SIN:C_SIN + SEQ], ALU.add, ALU.mult
                                               ).then_inc(free(seq, b, what), 1)

                    def split(i, what, ready):
                        wait_drained(dve, seq, b, what)
                        link(V.tensor_tensor(qk[seq][:, i, :], t0[:, i, :], t1[:, i, :], ALU.add))
                        link(V.tensor_copy(qk_hi[seq][:, i, :], qk[seq][:, i, :]))
                        low_part(seq, i, ready)

                    rotate(1, "k", "bk0", "bk0s")
                    yield
                    split(1, "k", split_k_ready)
                    rotate(0, "q", "bq0", "bq0s")
                    yield
                    split(0, "q", split_q_ready)
                    values(seq, b, "bv0")
                    yield
                    yield
                    yield
                    yield

                def heads(seq, b):
                    for k in range(HEAD_STEPS):
                        if group_at(k, SHIFT_AT) is not None:
                            t = group_at(k, SHIFT_AT)
                            wait_drained(dve, seq, b, f"sq{t // 2}")
                            wait_filled(dve, seq, b, ("shift", t))
                            V.tensor_tensor(q_sh[seq][:, t, :], q_sp[seq][:, t, :].bitcast(f32),
                                            where(seq, b, ("shift", t))[:, 0:SEQ], ALU.add
                                            ).then_inc(free(seq, b, ("shift", t)), 1)
                        if k < HEADS:
                            wait_filled(dve, seq, b, ("max", k))
                            V.tensor_reduce(negmax[seq][:, k // 4, :, 32 * (k % 4)],
                                            where(seq, b, ("max", k))[:].rearrange(
                                                "p (q n) -> p q n", q=QT),
                                            AX.X, ALU.max, negate=True
                                            ).then_inc(free(seq, b, ("max", k)), 1)
                        yield

                def attention_end(seq, b, side):
                    for qt in range(QT):
                        wait_filled(dve, seq, b, f"back{qt}")
                        rows_of = where(seq, b, f"back{qt}")[:].rearrange("p (h r) -> p h r", r=32)
                        link(V.reciprocal(recip[seq][:, qt, :], rows_of[:, :, HD]))
                        V.tensor_tensor(ctx_n[seq][:, qt, :].rearrange("p (h d) -> p h d", d=HD),
                                        rows_of[:, :, 0:HD],
                                        recip[seq][:, qt, :].unsqueeze(2).broadcast_to([P, HEADS, HD]),
                                        ALU.mult).then_inc(free(seq, b, f"back{qt}"), 1)
                    next(side, None)
                    yield
                    next(side, None)
                    yield
                    wait_filled(dve, seq, b, "out")
                    dve.wait_ge(xb_ready[seq], MHA[b] + 1)
                    V.tensor_tensor(y[seq][:].rearrange("p a d -> p (a d)"),
                                    where(seq, b, "out")[:, 0:SEQ],
                                    xb[seq][:].rearrange("p a d -> p (a d)"), ALU.add
                                    ).then_inc(free(seq, b, "out"), 1)
                    wait_drained(dve, seq, b, "out")
                    moments(seq)
                    yield

                def moments(seq):
                    for qt in range(QT):
                        last = V.bn_stats(stats[seq][:, qt, :], y[seq][:, qt, :])
                    link(last)
                    for qt in range(QT):
                        last = V.bn_aggr(mv[seq][:, qt, :], stats[seq][:, qt, :])
                    last.then_inc(var_ready[seq], 1)

                def normalise(seq, b):
                    yield from empty(MOMENTS_LEAD + ROOT_LEAD)
                    dve.wait_ge(rstd0_ready[seq], b + 1)
                    r, (n0, n1, n2) = r0[seq][:], (newton[seq][:, i, :] for i in range(3))
                    link(V.scalar_tensor_tensor(n0, mv[seq][:, :, 1], const[:, C_EPS:C_EPS + 1], r,
                                                ALU.add, ALU.mult))
                    link(V.scalar_tensor_tensor(n1, n0, -0.5, r, ALU.mult, ALU.mult))
                    link(V.scalar_tensor_tensor(n2, n1, 1.5, r, ALU.add, ALU.mult))
                    for qt in range(QT):
                        last = V.tensor_scalar(x[seq][:, qt, :], y[seq][:, qt, :],
                                               mv[seq][:, qt, 0:1], newton[seq][:, 2, qt:qt + 1],
                                               ALU.subtract, ALU.mult)
                    last.then_inc(x_ready[seq], 1)
                    yield from empty(1 + OUTPUT_LEAD + 1)

                def mixture(seq):
                    b = MIX0
                    wait_drained(dve, seq, CROSS0, "xT")
                    V.tensor_tensor(qk_lo[seq][:, 0, :], xT[seq], qk_hi[seq][:, 0, :].bitcast(f32),
                                    ALU.subtract).then_inc(split_x_ready[seq], 1)
                    wait_filled(dve, seq, b, "gate")
                    V.tensor_copy(gate[seq][:].rearrange("p a e -> p (a e)"),
                                  where(seq, b, "gate")[:, 0:QT * EXPERTS]
                                  ).then_inc(free(seq, b, "gate"), 1)
                    wait_drained(dve, seq, b, "gate")
                    for qt in range(QT):
                        last = V.max(top[seq][:, qt, :], gate[seq][:, qt, :])
                    link(last)
                    V.tensor_scalar(small[seq][:, 0, :], top[seq][:, :, 0], -1.0, None,
                                    ALU.mult).then_inc(gatemax_ready[seq], 1)
                    yield
                    dve.wait_ge(gateexp_ready[seq], 1)
                    for qt in range(QT):
                        last = V.scalar_tensor_tensor(g_sel[seq][:, qt, :], gate[seq][:, qt, :],
                                                      top[seq][:, qt, 1:2], g_exp[seq][:, qt, :],
                                                      ALU.is_ge, ALU.mult)
                    link(last)
                    link(V.tensor_reduce(small[seq][:, 4, :], g_sel[seq][:], AX.X, ALU.add))
                    link(V.reciprocal(small[seq][:, 5, :], small[seq][:, 4, :]))
                    for qt in range(QT):
                        last = V.tensor_scalar(g_w[seq][:, qt, :], g_sel[seq][:, qt, :],
                                               small[seq][:, 5, qt:qt + 1], 1.0 / EXPERTS,
                                               ALU.mult, ALU.mult)
                    last.then_inc(gatew_ready[seq], 1)
                    yield from empty(GATE_LEAD)
                    yield
                    yield
                    wait_filled(dve, seq, b, "b2")
                    dve.wait_ge(ld_mix_biases, 32)
                    V.tensor_tensor(y[seq][:], where(seq, b, "b2")[:, 0:SEQ].rearrange(
                        "p (a d) -> p a d", d=P), x[seq], ALU.add
                                    ).then_inc(free(seq, b, "b2"), 1)
                    yield
                    hidden = expo[seq][:, 0:4, :].rearrange("p a (h n) -> p (a h) n", n=SEQ)
                    dve.wait_ge(gatew_ready[seq], 1)
                    wait_drained(dve, seq, b, "b2")
                    side = keys_values(seq, CROSS1, None)
                    for n in range(MIX_STEPS):
                        if n < 2 * EXPERTS and not relu_on_scalar(n):
                            e = n // 2
                            wait_filled(dve, seq, b, ("up", n))
                            if e >= 2:
                                wait_filled(dve, seq, b, ("down", e - 2))
                            for i in range(2):
                                f = 2 * (n % 2) + i
                                last = V.tensor_scalar(hidden[:, (e % 2) * FC + f, :],
                                                       where(seq, b, ("up", n))[:, i * SEQ:(i + 1) * SEQ],
                                                       b1[:, e * FC + f:e * FC + f + 1], 0.0,
                                                       ALU.add, ALU.max)
                            last.then_inc(free(seq, b, ("up", n)), 1)
                        if n % 2 == 1 and n > 2:
                            e = (n - 3) // 2
                            wait_filled(dve, seq, b, ("down", e))
                            if e > 0:
                                wait_drained(dve, seq, b, ("down", e - 1))
                            for qt in range(QT):
                                last = V.scalar_tensor_tensor(
                                    y[seq][:, qt, :], where(seq, b, ("down", e))[:, qt * P:(qt + 1) * P],
                                    g_w[seq][:, qt, e:e + 1], y[seq][:, qt, :], ALU.mult, ALU.add)
                            last.then_inc(free(seq, b, ("down", e)), 1)
                        if n == 2 * EXPERTS + 1:
                            wait_drained(dve, seq, b, ("down", EXPERTS - 1))
                            moments(seq)
                        if n in SIDE_STEPS:
                            next(side, None)
                        yield

                def causal(seq):
                    b = CAUSAL1
                    yield
                    wait_filled(dve, seq, b, "score")
                    dve.wait_ge(ld_const, 16)
                    V.tensor_tensor(masked[seq], where(seq, b, "score")[:, 0:3 * P],
                                    const[:, C_MASK:C_MASK + 3 * P], ALU.add
                                    ).then_inc(free(seq, b, "score"), 1)
                    wait_drained(dve, seq, b, "score")
                    V.tensor_reduce(small[seq][:, 3, 0:1], masked[seq][:, 0:P], AX.X, ALU.max,
                                    negate=True)
                    link(V.tensor_reduce(small[seq][:, 3, 1:2], masked[seq][:, P:3 * P], AX.X,
                                         ALU.max, negate=True))
                    V.tensor_scalar(small[seq][:, 1, :], small[seq][:, 3, :], float(P) ** -0.5,
                                    None, ALU.mult).then_inc(rowmax_ready[seq], 1)
                    yield
                    dve.wait_ge(probs_ready[seq], 1)
                    link(V.reciprocal(small[seq][:, 4, :], small[seq][:, 2, :]))
                    yield from empty(PROBS_LEAD)
                    yield
                    yield
                    yield
                    wait_filled(dve, seq, b, "out")
                    for qt in range(QT):
                        last = V.scalar_tensor_tensor(
                            y[seq][:, qt, :], where(seq, b, "out")[:, qt * P:(qt + 1) * P],
                            small[seq][:, 4, qt:qt + 1], x[seq][:, qt, :], ALU.mult, ALU.add)
                    last.then_inc(free(seq, b, "out"), 1)
                    wait_drained(dve, seq, b, "out")
                    moments(seq)
                    yield

                def routing(seq):
                    logits, diff, score, exps, work = (route[seq][:, i] for i in range(5))
                    (greatest, first, total, weight, rank, base, beyond, number) = (
                        route_col[seq][:, i, :] for i in range(8))
                    tiles = slice(QT * seq, QT * (seq + 1))

                    def flags(tensor):
                        return tensor.rearrange("p (a e) -> p a e", e=EXPERTS)

                    def wide(column):
                        return column.unsqueeze(2).broadcast_to([P, QT, EXPERTS])

                    wait_filled(dve, seq, ROUTE, "logits")
                    V.tensor_copy(logits, flags(where(seq, ROUTE, "logits")[:, 0:QT * EXPERTS])
                                  ).then_inc(free(seq, ROUTE, "logits"), 1)
                    wait_drained(dve, seq, ROUTE, "logits")
                    link(V.tensor_reduce(greatest, logits, AX.X, ALU.max))
                    V.tensor_tensor(diff, logits, wide(greatest), ALU.subtract).then_inc(shifted[seq], 1)
                    link(V.tensor_tensor(work, logits, wide(greatest), ALU.is_ge))
                    link(V.tensor_tensor(score, work, flags(const[:, C_ORDER:C_ORDER + QT * EXPERTS]),
                                         ALU.mult))
                    link(V.tensor_reduce(first, score, AX.X, ALU.max))
                    link(V.tensor_tensor(onehot[:, tiles, :], score, wide(first), ALU.is_equal))
                    for i in range(QT * seq, QT * (seq + 1)):
                        last = V.tensor_tensor(before[:, i + 1, :], before[:, i, :], onehot[:, i, :],
                                               ALU.add)
                        if i == QT * seq:
                            link(last)
                    last.then_inc(onehot_ready[seq], 1)
                    dve.wait_ge(onehot_ready[seq], 1)
                    link(V.tensor_tensor(work, onehot[:, tiles, :],
                                         flags(const[:, C_BASE:C_BASE + QT * EXPERTS]), ALU.mult))
                    V.tensor_reduce(base, work, AX.X, ALU.add)
                    yield
                    dve.wait_ge(routeexp_ready[seq], 1)
                    link(V.tensor_reduce(total, exps, AX.X, ALU.add))
                    V.reciprocal(x_rows[:, tiles, P + 1], total)
                    V.tensor_copy(x_rows[:, tiles, P],
                                  const[:, C_TOKEN + QT * seq:C_TOKEN + QT * (seq + 1)])
                    yield from empty(1 + RANK_LEAD)
                    wait_filled(dve, seq, ROUTE, "rank")
                    V.tensor_tensor(score, flags(where(seq, ROUTE, "rank")[:, 0:QT * EXPERTS]),
                                    onehot[:, tiles, :], ALU.mult).then_inc(free(seq, ROUTE, "rank"), 1)
                    wait_drained(dve, seq, ROUTE, "rank")
                    link(V.tensor_reduce(rank, score, AX.X, ALU.add))
                    V.tensor_scalar(beyond, rank, float(CAP), float(NOWHERE), ALU.is_ge, ALU.mult)
                    link(V.tensor_tensor(number, rank, base, ALU.add))
                    V.tensor_tensor(slot[:, tiles], number, beyond, ALU.add
                                    ).then_inc(slot_ready[seq], 1)
                    yield

                def program(seq):
                    yield from self_projections(seq)
                    yield from heads(seq, SELF0)
                    yield from attention_end(seq, SELF0, keys_values(seq, CROSS0, "bvx0"))
                    yield from normalise(seq, SELF0)
                    yield from queries(seq, CROSS0)
                    yield from heads(seq, CROSS0)
                    yield from attention_end(seq, CROSS0, iter(()))
                    yield from normalise(seq, CROSS0)
                    yield from mixture(seq)
                    yield from normalise(seq, MIX0)
                    yield from causal(seq)
                    yield from normalise(seq, CAUSAL1)
                    yield from queries(seq, CROSS1)
                    yield from heads(seq, CROSS1)
                    yield from attention_end(seq, CROSS1, iter(()))
                    yield from normalise(seq, CROSS1)
                    yield from routing(seq)

                dve.wait_ge(ld_rope, 16)
                dve.wait_ge(ld_cols, 16)
                take_turns(*[lane_program(program, lane) for lane in range(LANES)])
                last_mixture["vector"](dve)


def last_mixture_programs(nc, stack, out, t):
    f32, i32, u32 = mybir.dt.float32, mybir.dt.int32, mybir.dt.uint32
    ALU, ACT = mybir.AluOpType, mybir.ActivationFunctionType
    GROUP = 2

    def sb(name, shape, dt=f32):
        return stack.enter_context(nc.sbuf_tensor(name, shape, dt))

    def sem(name):
        return stack.enter_context(nc.semaphore(name))

    const, x_rows, xe_dram, ident, w1, w2 = (
        t["const"], t["x_rows"], t["xe_dram"], t["ident"], t["w1"], t["w2"])
    w1_loaded, w2_loaded, scattered = t["w1_loaded"], t["w2_loaded"], t["scattered"]
    xe = t["xe"][:].rearrange("p a b -> p (a b)")[:, 0:EXPERTS * ROW].rearrange("p (e r) -> p e r", r=ROW)
    xeT = t["xeT"][:].rearrange("p b n -> p (b n)")
    x_norm = t["x_norm"][:].rearrange("p b (a d) -> p (b a) d", d=P)
    ye, ye_norm = (t[name][:].rearrange("p a h r -> p (a h r)").rearrange("p (e d) -> p e d", d=P)
                   for name in ("ye", "ye_norm"))
    hid = t["hid"][:].rearrange("p (s a) n -> p s (a n)", s=2).rearrange("p s (f n) -> p s f n", f=FC)
    token = sb("token", [P, EXPERTS], i32)
    stats = sb("stats_all", [P, TILES, 6])
    mv = [sb(f"mv_all{i}", [P, TILES, 2]) for i in range(2)]
    rs = [sb(f"rs_all{i}", [P, 4, TILES]) for i in range(2)]
    ps = [b for pool in POOLS for b in t["banks"][pool]]
    out_rows = out.rearrange("b n d -> (b n) d")

    xe_loaded = [sem(f"xe_loaded{half}") for half in range(2)]
    xeT_filled, xeT_ready, up_filled, hid_ready, down_filled, ye_ready = (
        sem("xeT_filled"), sem("xeT_ready"), sem("up_filled"), sem("hid_ready"), sem("down_filled"),
        sem("ye_ready"))
    var_ready, ln_own, rstd0_ready, own_sem = (
        sem("var_all_ready"), sem("ln_own"), sem("rstd0_all_ready"), sem("dve_last_own"))
    x_norm_ready, x_norm_stored, token_ready, ye_norm_ready, stored = (
        sem("x_norm_ready"), sem("x_norm_stored"), sem("token_ready"), sem("ye_norm_ready"),
        sem("stored"))
    norms = [(0, 0, TILES)] + [(1, e, e + GROUP) for e in range(0, EXPERTS, GROUP)]

    def vector(dve):
        V = nc.vector
        own = [0]

        def link(instruction):
            own[0] += 1
            instruction.then_inc(own_sem, 1)
            dve.wait_ge(own_sem, own[0])

        def layernorm(n, rows_in, rows_out, ready):
            which, lo, hi = norms[n]
            for i in range(lo, hi):
                last = V.bn_stats(stats[:, i, :], rows_in[:, i, 0:P])
            link(last)
            for i in range(lo, hi):
                last = V.bn_aggr(mv[which][:, i, :], stats[:, i, :])
            last.then_inc(var_ready, 1)
            dve.wait_ge(rstd0_ready, n + 1)
            r, n0, n1, root = (rs[which][:, i, lo:hi] for i in range(4))
            link(V.scalar_tensor_tensor(n0, mv[which][:, lo:hi, 1], const[:, C_EPS:C_EPS + 1], r,
                                        ALU.add, ALU.mult))
            link(V.scalar_tensor_tensor(n1, n0, -0.5, r, ALU.mult, ALU.mult))
            link(V.scalar_tensor_tensor(root, n1, 1.5, r, ALU.add, ALU.mult))
            for i in range(lo, hi):
                V.tensor_scalar(rows_out[:, i, :], rows_in[:, i, 0:P], mv[which][:, i, 0:1],
                                rs[which][:, 3, i:i + 1], ALU.subtract, ALU.mult
                                ).then_inc(ready, 1)

        layernorm(0, x_rows, x_norm, x_norm_ready)
        for half in range(2):
            dve.wait_ge(xe_loaded[half], 16)
        V.tensor_copy(token[:], xe[:, :, P]).then_inc(token_ready, 1)
        for e in range(EXPERTS):
            dve.wait_ge(down_filled, e + 1)
            last = V.scalar_tensor_tensor(ye[:, e, :], ps[5 + e % 2][:, 0:P], xe[:, e, P + 1:ROW],
                                          xe[:, e, 0:P], ALU.mult, ALU.add)
            last.then_inc(ye_ready, 1)
            if (e + 1) % GROUP == 0:
                dve.wait_ge(ye_ready, e + 1)
                layernorm(1 + e // GROUP, ye, ye_norm, ye_norm_ready)

    def scalar(act):
        def root(n):
            which, lo, hi = norms[n]
            act.wait_ge(var_ready, n + 1)
            nc.scalar.activation(rs[which][:, 0, lo:hi], mv[which][:, lo:hi, 1], ACT.Ln,
                                 bias=const[:, C_EPS:C_EPS + 1]).then_inc(ln_own, 1)
            act.wait_ge(ln_own, n + 1)
            nc.scalar.activation(rs[which][:, 0, lo:hi], rs[which][:, 0, lo:hi], ACT.Exp,
                                 scale=-0.5).then_inc(rstd0_ready, 1)

        root(0)
        for half in range(2):
            act.wait_ge(xeT_filled, half + 1)
            nc.scalar.activation(xeT[:, 4 * P * half:4 * P * (half + 1)], ps[1 + half][:],
                                 ACT.Copy).then_inc(xeT_ready, 1)
        for e in range(EXPERTS):
            act.wait_ge(up_filled, e + 1)
            if e >= 2:
                act.wait_ge(down_filled, e - 1)
            nc.scalar.activation(hid[:, e % 2].rearrange("p f n -> p (f n)"), ps[3 + e % 2][:],
                                 ACT.Relu).then_inc(hid_ready, 1)
            if e > GROUP and (e - 1) % GROUP == 0:
                root((e - 1) // GROUP)
        root(EXPERTS // GROUP)

    def tensor(pe):
        mm = nc.tensor.matmul
        for pool, sems in t["drained"].items():
            for i, read in enumerate(sems):
                pe.wait_ge(read, 1 + max(n for p, j, n in TURNS.values() if (p, j) == (pool, i)))
        for half in range(2):
            pe.wait_ge(xe_loaded[half], 16)
            for e in range(4 * half, 4 * half + 4):
                last = nc.tensor.transpose(ps[1 + half][:, (e % 4) * P:(e % 4 + 1) * P],
                                           xe[:, e, 0:P], ident)
            last.then_inc(xeT_filled, 1)
        for e in range(EXPERTS + 1):
            if e < EXPERTS:
                pe.wait_ge(w1_loaded[e], 32)
                pe.wait_ge(xeT_ready, e // 4 + 1)
                if e >= 2:
                    pe.wait_ge(hid_ready, e - 1)
                for f in range(FC):
                    last = mm(ps[3 + e % 2][:, f * P:(f + 1) * P], w1[e][:, f * P:(f + 1) * P],
                              xeT[:, e * P:(e + 1) * P], start=True, stop=True)
                last.then_inc(up_filled, 1)
            if e > 0:
                d = e - 1
                pe.wait_ge(w2_loaded[d], 32)
                pe.wait_ge(hid_ready, d + 1)
                if d >= 2:
                    pe.wait_ge(ye_ready, d - 1)
                for f in range(FC):
                    last = mm(ps[5 + d % 2][:, 0:P], hid[:, d % 2, f, :], w2[:, d, f, :],
                              start=(f == 0), stop=(f == FC - 1))
                last.then_inc(down_filled, 1)

    def gpsimd(pool):
        pool.wait_ge(token_ready, 1)
        pool.wait_ge(x_norm_stored, 16)
        for e in range(EXPERTS):
            pool.wait_ge(ye_norm_ready, e + 1)
            nc.gpsimd.indirect_dma_start(
                out_rows, bass.IndirectOffsetOnAxis(token[:, e:e + 1].bitcast(u32), 0),
                ye_norm[:, e, :], None, bounds_check=TOKENS - 1, oob_is_err=False
            ).then_inc(stored, 16)

    def sync(sp):
        sp.wait_ge(scattered, 16 * TILES)
        for half in range(2):
            sp.dma_start(xe[:, 4 * half:4 * half + 4, :],
                         xe_dram.rearrange("(e p) r -> p e r", p=P)[:, 4 * half:4 * half + 4, :]
                         ).then_inc(xe_loaded[half], 16)
        sp.wait_ge(x_norm_ready, TILES)
        sp.dma_start(out_rows.rearrange("(a p) d -> p a d", p=P), x_norm).then_inc(x_norm_stored, 16)
        sp.wait_ge(stored, 16 * EXPERTS)

    return dict(tensor=tensor, scalar=scalar, vector=vector, gpsimd=gpsimd, sync=sync)


def kernel(**inputs):
    import concourse.bacc as _bacc
    from concourse.bass_utils import run_bass_kernel_spmd as _run

    a = {k: np.asarray(v) for k, v in inputs.items()}
    swap = np.arange(P) ^ 1

    def by_token(v):
        return v.reshape(TILES, P, P).transpose(1, 0, 2)

    def by_width(v):
        return v.reshape(BATCH, SEQ, P).transpose(2, 0, 1)

    wq, wk = a["L0_attn_wq"].T, a["L0_attn_wk"].T
    mats = [wq, wq[:, swap], wk, wk[:, swap], a["L0_attn_wv"].T, a["L0_attn_wo"].T,
            a["L0_xattn_Wq"].T, a["L0_xattn_Wk"].T, a["L0_xattn_Wv"].T, a["L0_xattn_Wo"].T,
            a["L1_attn_qk"], a["L1_attn_ov"],
            a["L1_xattn_Wq"].T, a["L1_xattn_Wk"].T, a["L1_xattn_Wv"].T, a["L1_xattn_Wo"].T]
    bq, bk = a["L0_attn_bq"], a["L0_attn_bk"]
    const, spread = constants()
    arrays = {
        "x": by_token(a["x"]), "xT": by_width(a["x"]), "cT": by_width(a["ctx_1024"]),
        "proj": np.stack(mats, 1),
        "cols": np.stack([bq, bq[swap], bk, bk[swap], a["L0_xattn_bq"], a["L0_xattn_bk"]], 1),
        "rows": np.concatenate([a["L0_attn_bv"], a["L0_attn_bo"], a["L0_xattn_bv"],
                                a["L0_xattn_bo"], a["L1_xattn_bo"]]),
        "gates": np.stack([a["L0_ffn_W_gate"], a["L1_ffn_Wr"]], 1),
        "b1": a["L0_ffn_b1"].reshape(EXPERTS * FC, P).T, "b2": a["L0_ffn_b2"],
        "mix0_w1": a["L0_ffn_W1"].transpose(1, 0, 2),
        "mix0_w2": a["L0_ffn_W2"].reshape(EXPERTS, FC, P, P).transpose(2, 0, 1, 3),
        "mix1_w1": a["L1_ffn_W1"].transpose(1, 0, 2),
        "mix1_w2": a["L1_ffn_W2"].reshape(EXPERTS, FC, P, P).transpose(2, 0, 1, 3),
        "const": const, "spread": spread,
    }
    arrays = {k: np.ascontiguousarray(v) for k, v in arrays.items()}
    nc = _bacc.Bacc("TRN2", target_bir_lowering=False, num_devices=1)
    ins = {k: nc.dram_tensor(f"in_{k}", v.shape, mybir.dt.from_np(v.dtype), kind="ExternalInput").ap()
           for k, v in arrays.items()}
    ins["spread"] = ins["spread"].rearrange("p (k t c) -> p k t c", k=4, t=GROUPS)
    out = nc.dram_tensor("out", (BATCH, SEQ, P), mybir.dt.float32, kind="ExternalOutput").ap()
    decoder(nc, ins, out)
    r = _run(nc, [{f"in_{k}": v for k, v in arrays.items()}], core_ids=[0])
    return r.results[0]["out"]
```
